# Optimizing a Trainium2 kernel written in Bass

```python
import numpy as np
import jax
import jax.numpy as jnp

def _softmax(x, axis=-1):
    return jax.nn.softmax(x, axis=axis)

def _gelu(x):
    return jax.nn.gelu(x, approximate=True)

def _silu(x):
    return jax.nn.silu(x)

def _sigmoid(x):
    return jax.nn.sigmoid(x)

def _layernorm(x, axis=-1, eps=1e-05):
    m = jnp.mean(x, axis=axis, keepdims=True)
    v = jnp.var(x, axis=axis, keepdims=True)
    return (x - m) / jnp.sqrt(v + eps)

def _scatter_add(tgt, idx, src, axis=0):
    return tgt.at[idx].add(src)

def _segment_sum(src, seg, n):
    return jax.ops.segment_sum(src, seg, n)
kernel_name = 'mk_gnn_ffn_d1_gnn_r64_a4e554'

def setup_inputs(seed: int=0):
    np.random.seed(seed)
    _w = jnp.asarray

    def _rec_inputs():
        import jax
        import jax.numpy as jnp
        _gk = jax.random.key(seed)
        x = -0.000364 + 1 * jax.random.normal(jax.random.fold_in(_gk, 1), (10000, 768), jnp.float32)
        src = jax.random.randint(jax.random.fold_in(_gk, 2), (5000,), 0, 10000, jnp.int32)
        dst = jnp.minimum((10000 * jax.random.uniform(jax.random.fold_in(_gk, 3), (5000,)) ** 2.0).astype(jnp.int32), 9999)
        _o = jnp.argsort(dst, stable=True)
        src = src[_o]
        dst = dst[_o]
        return (x, src, dst)
    x, src, dst = _rec_inputs()

    def _L0_gnn_setup():
        import jax, jax.numpy as jnp
        import numpy as np
        N = 20000
        E_RAND = 5000
        NEG_SLOPE = 0.2

        def gat_layer(x, W, a_src, a_dst, bias, src, dst, heads, out_c, concat):
            n = x.shape[0]
            h = (x @ W).reshape(n, heads, out_c)
            al_s = jnp.einsum('nhc,hc->nh', h, a_src)
            al_d = jnp.einsum('nhc,hc->nh', h, a_dst)
            e = jax.nn.leaky_relu(al_s[src] + al_d[dst], NEG_SLOPE)
            m = jax.ops.segment_max(e, dst, num_segments=n)
            ex = jnp.exp(e - m[dst])
            z = jax.ops.segment_sum(ex, dst, num_segments=n)
            alpha = ex / (z[dst] + 1e-16)
            msg = h[src] * alpha[:, :, None]
            out = jax.ops.segment_sum(msg, dst, num_segments=n)
            out = out.reshape(n, heads * out_c) if concat else out.mean(axis=1)
            return out + bias
        key = jax.random.key(seed)
        ks = jax.random.split(key, 10)
        x = jax.random.normal(ks[0], (N, 768), dtype=jnp.float32)
        src = jax.random.randint(ks[1], (E_RAND,), 0, N)
        dst = jax.random.randint(ks[2], (E_RAND,), 0, N)
        loop = jnp.arange(N)
        edge_index = jnp.stack([jnp.concatenate([src, loop]), jnp.concatenate([dst, loop])])
        s = 1.0 / np.sqrt(768.0)
        W1 = jax.random.normal(ks[3], (768, 768), dtype=jnp.float32) * s
        a_src1 = jax.random.normal(ks[4], (8, 96), dtype=jnp.float32) * 0.1
        a_dst1 = jax.random.normal(ks[5], (8, 96), dtype=jnp.float32) * 0.1
        b1 = jnp.zeros((768,), dtype=jnp.float32)
        W2 = jax.random.normal(ks[6], (768, 768), dtype=jnp.float32) * s
        a_src2 = jax.random.normal(ks[7], (1, 768), dtype=jnp.float32) * 0.1
        a_dst2 = jax.random.normal(ks[8], (1, 768), dtype=jnp.float32) * 0.1
        b2 = jnp.zeros((768,), dtype=jnp.float32)
        return {'x': x, 'edge_index': edge_index, 'W1': W1, 'a_src1': a_src1, 'a_dst1': a_dst1, 'b1': b1, 'W2': W2, 'a_src2': a_src2, 'a_dst2': a_dst2, 'b2': b2}
    _L0_gnn_all = _L0_gnn_setup()
    _L0_gnn_in = {k: v for k, v in _L0_gnn_all.items() if k in ('W1', 'a_src1', 'a_dst1', 'b1', 'W2', 'a_src2', 'a_dst2', 'b2')}
    del _L0_gnn_all

    def _L0_ffn_setup():
        import jax, jax.numpy as jnp
        import numpy as np
        D_MODEL = 768
        D_HID = 48
        NUM_EXPERTS = 8
        TOP_K = 2
        B, T = (1, 32)
        key = jax.random.key(seed)
        k0, k1, k2, k3 = jax.random.split(key, 4)
        x = jax.random.normal(k0, (B, T, D_MODEL), dtype=jnp.float32)
        gate_w = jax.random.normal(k1, (D_MODEL, NUM_EXPERTS), dtype=jnp.float32) * (1.0 / np.sqrt(D_MODEL))
        s1 = float(np.sqrt(2.0 / D_MODEL))
        s2 = float(np.sqrt(2.0 / D_HID))
        w1 = jax.random.normal(k2, (NUM_EXPERTS, D_MODEL, D_HID), dtype=jnp.float32) * s1
        w2 = jax.random.normal(k3, (NUM_EXPERTS, D_HID, D_MODEL), dtype=jnp.float32) * s2
        b1 = jnp.zeros((NUM_EXPERTS, 1, D_HID), dtype=jnp.float32)
        b2 = jnp.zeros((NUM_EXPERTS, 1, D_MODEL), dtype=jnp.float32)
        return {'x': x, 'gate_w': gate_w, 'w1': w1, 'b1': b1, 'w2': w2, 'b2': b2}
    _L0_ffn_all = _L0_ffn_setup()
    _L0_ffn_in = {k: v for k, v in _L0_ffn_all.items() if k in ('gate_w', 'w1', 'b1', 'w2', 'b2')}
    del _L0_ffn_all
    return {'x': x, 'src': src, 'dst': dst, 'L0_gnn_W1': _L0_gnn_in['W1'], 'L0_gnn_a_src1': _L0_gnn_in['a_src1'], 'L0_gnn_a_dst1': _L0_gnn_in['a_dst1'], 'L0_gnn_b1': _L0_gnn_in['b1'], 'L0_gnn_W2': _L0_gnn_in['W2'], 'L0_gnn_a_src2': _L0_gnn_in['a_src2'], 'L0_gnn_a_dst2': _L0_gnn_in['a_dst2'], 'L0_gnn_b2': _L0_gnn_in['b2'], 'L0_ffn_gate_w': _L0_ffn_in['gate_w'], 'L0_ffn_w1': _L0_ffn_in['w1'], 'L0_ffn_b1': _L0_ffn_in['b1'], 'L0_ffn_w2': _L0_ffn_in['w2'], 'L0_ffn_b2': _L0_ffn_in['b2']}

def reference(x, src, dst, L0_gnn_W1, L0_gnn_a_src1, L0_gnn_a_dst1, L0_gnn_b1, L0_gnn_W2, L0_gnn_a_src2, L0_gnn_a_dst2, L0_gnn_b2, L0_ffn_gate_w, L0_ffn_w1, L0_ffn_b1, L0_ffn_w2, L0_ffn_b2):
    import jax
    import jax.numpy as jnp

    def _L0_gnn_ref(x, edge_index, W1, a_src1, a_dst1, b1, W2, a_src2, a_dst2, b2):
        import jax, jax.numpy as jnp
        import numpy as np
        N = 20000
        E_RAND = 5000
        NEG_SLOPE = 0.2

        def gat_layer(x, W, a_src, a_dst, bias, src, dst, heads, out_c, concat):
            n = x.shape[0]
            h = (x @ W).reshape(n, heads, out_c)
            al_s = jnp.einsum('nhc,hc->nh', h, a_src)
            al_d = jnp.einsum('nhc,hc->nh', h, a_dst)
            e = jax.nn.leaky_relu(al_s[src] + al_d[dst], NEG_SLOPE)
            m = jax.ops.segment_max(e, dst, num_segments=n)
            ex = jnp.exp(e - m[dst])
            z = jax.ops.segment_sum(ex, dst, num_segments=n)
            alpha = ex / (z[dst] + 1e-16)
            msg = h[src] * alpha[:, :, None]
            out = jax.ops.segment_sum(msg, dst, num_segments=n)
            out = out.reshape(n, heads * out_c) if concat else out.mean(axis=1)
            return out + bias
        src, dst = (edge_index[0], edge_index[1])
        h = gat_layer(x, W1, a_src1, a_dst1, b1, src, dst, heads=8, out_c=96, concat=True)
        h = jax.nn.elu(h)
        out = gat_layer(h, W2, a_src2, a_dst2, b2, src, dst, heads=1, out_c=768, concat=False)
        return out

    def _L0_ffn_ref(x, gate_w, w1, b1, w2, b2):
        import jax, jax.numpy as jnp
        import numpy as np
        D_MODEL = 768
        D_HID = 48
        NUM_EXPERTS = 8
        TOP_K = 2
        B, T = (1, 32)
        "MoE FFN: top-k router, per-expert GELU FFN, weighted combine.\n\n            Math identical to the torch sort/pad/bmm/scatter-add path: each token's\n            output is sum over its top-k experts of (normalized weight) * FFN_e(x).\n            Expressed here as a dense dispatch (combine matrix [N, E]) which is\n            jit-friendly (static shapes) and exactly equivalent since padded slots /\n            unrouted (token, expert) pairs carry zero combine weight.\n            "
        Bx, Tx, D = x.shape
        E = w1.shape[0]
        xf = x.reshape(-1, D)
        router_logits = xf @ gate_w
        scores = jax.nn.softmax(router_logits, axis=-1)
        topk_w, topk_idx = jax.lax.top_k(scores, TOP_K)
        topk_w = topk_w / jnp.sum(topk_w, axis=-1, keepdims=True)
        combine = jnp.einsum('nk,nke->ne', topk_w, jax.nn.one_hot(topk_idx, E, dtype=xf.dtype))
        h = jnp.einsum('nd,edh->enh', xf, w1) + b1
        h = jax.nn.gelu(h, approximate=False)
        y = jnp.einsum('enh,ehd->end', h, w2) + b2
        out = jnp.einsum('ne,end->nd', combine, y)
        return out.reshape(Bx, Tx, D)
    edge_index = jnp.stack([src, dst])
    x = x + _L0_gnn_ref(_layernorm(x, axis=-1), edge_index, L0_gnn_W1, L0_gnn_a_src1, L0_gnn_a_dst1, L0_gnn_b1, L0_gnn_W2, L0_gnn_a_src2, L0_gnn_a_dst2, L0_gnn_b2)
    x = x + _L0_ffn_ref(_layernorm(x, axis=-1)[None], L0_ffn_gate_w, L0_ffn_w1, L0_ffn_b1, L0_ffn_w2, L0_ffn_b2)[0]
    return x

_drawn_inputs = setup_inputs


def setup_inputs(seed=0):
    import zlib

    import numpy as np

    out = dict(_drawn_inputs(seed))
    spreads = {'L0_gnn_b1': (0.0, 0.1),
     'L0_gnn_b2': (0.0, 0.1),
     'L0_ffn_b1': (0.0, 0.1),
     'L0_ffn_b2': (0.0, 0.1)}
    factors = {}
    for name, (base, spread) in spreads.items():
        noise = np.random.default_rng([zlib.crc32(name.encode()), seed]).standard_normal(out[name].shape)
        drawn = base * np.exp(spread * noise) if base else spread * noise
        out[name] = jnp.asarray(drawn.astype(out[name].dtype))
    for name, factor in factors.items():
        out[name] = (out[name] * factor).astype(out[name].dtype)
    return out
```

```python
from contextlib import ExitStack

import concourse.bass as bass
from concourse import mybir

ALU = mybir.AluOpType
ACT = mybir.ActivationFunctionType
AX = mybir.AxisListType
F32 = mybir.dt.float32
F32R = mybir.dt.float32r
BF16 = mybir.dt.bfloat16
I32 = mybir.dt.int32

P = 128
N, D = 10000, 768
E = 5000
KC = D // P
HEADS, HC = 8, 96
HR = P // HEADS
GE = 512
TG = GE // P
ET = -(-E // P)
EP = ET * P
EG = EP // GE
NG = -(-N // GE)
EXPERTS, HID = 8, 48
FH = EXPERTS * HID
FC = FH // P
HALF = D // 2
RW = D + 1
SLOPE = 0.2
EPS = 1e-5
BIG = 3e38
assert EP % GE == 0 and FH % P == 0 and EXPERTS == HEADS and KC * HR == HC and FC * HR == HID


def wait(eng, sem, value):
    if isinstance(value, int) and value <= 0:
        return
    eng.wait_ge(sem, value)


def carried_wait(eng, passed, sem, value):
    eng.wait_ge(sem, value)
    eng.sem_inc(passed, 1)


class Kit:

    def __init__(self, nc, ctx, phase=""):
        self.nc, self.ctx, self.phase, self.made = nc, ctx, phase, []

    def sb(self, name, shape, dt=F32):
        return self.ctx.enter_context(self.nc.sbuf_tensor(self.phase + name, shape, dt))

    def ps(self, name, shape=(P, 512), dt=F32):
        return self.ctx.enter_context(self.nc.psum_tensor(self.phase + name, list(shape), dt))

    def sem(self, name):
        self.made.append(self.ctx.enter_context(self.nc.semaphore(self.phase + name)))
        return self.made[-1]

    def block(self):
        self.ctx.callback(self.clear)
        return self.ctx.enter_context(self.nc.Block())

    def clear(self):
        with self.nc.Block() as block:
            @block.gpsimd
            def _(pool):
                for sem in self.made:
                    pool.sem_clear(sem)

    def sems(self, name, n):
        return [self.sem(f"{name}{i}") for i in range(n)]


def persistent(k):
    s = {}
    s["ident"] = k.sb("ident", [P, P])
    s["gidx"] = k.sb("gidx", [P, EG * 8], I32)
    s["pos"] = k.sb("pos", [P, EG * 8], I32)
    s["pnode"] = k.sb("pnode", [P, NG * TG], I32)
    s["v1"] = k.sb("v1", [P, 2, 2, KC, HEADS], F32R)
    s["v2"] = k.sb("v2", [P, KC, 64])
    s["b1col"] = k.sb("b1col", [P, KC])
    s["headmap"] = k.sb("headmap", [HEADS, P])
    s["w1s"] = k.sb("w1s", [P, 2, KC, D], F32R)
    s["w2s"] = k.sb("w2s", [P, 2, KC, D], F32R)
    s["f1"] = s["w1s"][:, 0].rearrange("p k (a n) -> p a k n", a=2)
    s["f2"] = s["w1s"][:, 1].rearrange("p (a k) n -> p a k n", a=2)
    return s


def order_edges(nc, a, d, s):
    with ExitStack() as ctx:
        k = Kit(nc, ctx, "o_")
        key = k.sb("key", [P, EP])
        with nc.sbuf_tensor("junk_v", [P, EP], BF16) as junk_v, nc.sbuf_tensor("junk_a", [P, EP], BF16) as junk_a:
            pass
        oh_lo = k.sb("oh_lo", [P, ET, P], BF16)
        oh_hi = k.sb("oh_hi", [P, ET, 4, ET], BF16)
        wraw = k.sb("wraw", [P, KC, D])
        w2raw = k.sb("w2raw", [P, KC, D])
        prod = k.sb("prod", [P, KC, D])
        avec = k.sb("avec", [P, 4, D])
        col_i = k.sb("col_i", [P, 2, ET], I32)
        dst_f = k.sb("dst_f", [P, ET])
        frac_i = k.sb("frac_i", [P, P], I32)
        frac = k.sb("frac", [P, P])
        iota_f = k.sb("iota_f", [P, P])
        rowp_i = k.sb("rowp_i", [P, 1], I32)
        rowp = k.sb("rowp", [P, 1])
        thr = k.sb("thr", [P, 3, ET])
        nthr = k.sb("nthr", [P, 3, ET])
        less = k.sb("less", [P, 3, ET])
        rank = k.sb("rank", [P, 4, ET])
        rank_i = k.sb("rank_i", [P, 3, ET], I32)
        part_i = k.sb("part_i", [P, 4, ET], I32)
        part_f = k.sb("part_f", [P, 4, ET])
        hl_f = k.sb("hl_f", [P, 2, ET])
        ohr = k.sb("ohr", [P, ET, ET])
        sorted4 = k.sb("sorted4", [P, 4, ET])
        col_f = k.sb("col_f", [P, 2, ET])
        clip_f = k.sb("clip_f", [P, ET])
        dst_row = k.sb("dst_row", [ET, P])
        window = k.sb("window", [ET, P + 2])
        eq = k.sb("eq", [ET, 2, P])
        masks = k.sb("masks", [ET, 2, P])
        end_row = k.sb("end_row", [ET, P])
        end_i = k.sb("end_i", [P, ET], I32)
        place_i = k.sb("place_i", [P, ET], I32)
        none_i = k.sb("none_i", [P, 80], I32)
        edge_f = k.sb("edge_f", [1, 2])
        v_f = k.sb("v_f", [P, 2, KC, HEADS])
        p_sort = k.ps("p_sort")
        p_row = k.ps("p_row")
        p_end = k.ps("p_end")
        (s_key, s_col, s_w1, s_av, s_w2, s_b, s_none, s_iota, s_prep, s_cnt_v, s_cnt_a, s_dve, s_oh, s_sorted,
         s_row, s_rowst, s_win, s_maskst, s_endT, s_endi, s_scat, s_pn, s_prod, s_red, s_split, s_id, s_vec,
         s_colr, s_hm) = [k.sem(f"s_o{i}") for i in range(29)]
        ACT_TILES = range(24, ET)
        block = k.block()

        src_d, dst_d = a["src"], a["dst"]
        full = (E // P) * P

        @block.sync
        def _(sp):
            sp.dma_start(key[:, 0:E].bitcast(I32), dst_d.partition_broadcast(P)).then_inc(s_key, 16)
            sp.wait_ge(s_prep, 1)
            for n, v in enumerate((src_d, dst_d)):
                sp.dma_start(col_i[:, n, 0:E // P], v[0:full].rearrange("(t p) -> p t", p=P), allow_slow_non_contiguous=True).then_inc(s_col, 16)
                sp.dma_start(col_i[0:E - full, n, E // P:ET],
                             v[full:E].rearrange("(p o) -> p o", o=1), allow_slow_non_contiguous=True).then_inc(s_col, 16)
            sp.dma_start(wraw[:], a["L0_gnn_W1"].rearrange("(k p) n -> p k n", p=P)).then_inc(s_w1, 16)
            for n, name in enumerate(("a_src1", "a_dst1", "a_src2", "a_dst2")):
                sp.dma_start(avec[:, n, :], a["L0_gnn_" + name].rearrange("h c -> (h c)").partition_broadcast(P)).then_inc(s_av, 16)
            for h in range(HEADS):
                sp.dma_start(w2raw[h * HR:(h + 1) * HR, :, :],
                             a["L0_gnn_W2"][h * HC:(h + 1) * HC, :].rearrange("(m r) n -> r m n", r=HR)).then_inc(s_w2, 16)
                sp.dma_start(s["b1col"][h * HR:(h + 1) * HR, :],
                             a["L0_gnn_b1"][h * HC:(h + 1) * HC].rearrange("(m r) -> r m", r=HR), allow_slow_non_contiguous=True).then_inc(s_b, 16)
            sp.wait_ge(s_none, 2)
            sp.dma_start(d["node_pos"][0:10240, :].rearrange("(p n) o -> p (n o)", p=P), none_i[:]).then_inc(s_none, 16)
            sp.dma_start(d["sorted_dst"][0:1, :], edge_f[0:1, 0:1]).then_inc(s_rowst, 16)
            sp.dma_start(d["sorted_dst"][EP + 1:EP + 2, :], edge_f[0:1, 1:2]).then_inc(s_rowst, 16)
            sp.wait_ge(s_row, 2)
            sp.dma_start(d["sorted_dst"][1:EP + 1, :].rearrange("(t j) o -> t (j o)", j=P), dst_row[:]).then_inc(s_rowst, 16)
            sp.wait_ge(s_rowst, 48)
            sp.dma_start(window[:], bass.AP(d["sorted_dst"].tensor, 0, [[P, ET], [1, P + 2]])).then_inc(s_win, 16)
            sp.wait_ge(s_maskst, 1)
            for n in range(2):
                sp.dma_start(d["masks"][n, :].rearrange("(t j) -> t j", j=P), masks[:, n, :]).then_inc(s_maskst, 16)
            sp.wait_ge(s_scat, 16 * ET)
            last = N - (NG - 1) * GE
            sp.dma_start(s["pnode"][:, 0:(NG - 1) * TG],
                         d["node_pos"][0:(NG - 1) * GE, :].rearrange("(t p) o -> p (t o)", p=P), allow_slow_non_contiguous=True).then_inc(s_pn, 16)
            sp.dma_start(s["pnode"][:, (NG - 1) * TG:NG * TG],
                         d["node_pos"][N - GE:N, :].rearrange("(t p) o -> p (t o)", p=P), allow_slow_non_contiguous=True).then_inc(s_pn, 16)
            sp.wait_ge(s_pn, 32)
            sp.wait_ge(s_maskst, 33)
            sp.wait_ge(s_b, 16 * HEADS)

        @block.gpsimd
        def _(pool):
            pool.memset(col_i[:, 0, ET - 1:ET], 0)
            pool.memset(col_i[:, 1, ET - 1:ET], N).then_inc(s_prep, 1)
            pool.iota(frac_i[:], [[1, P]], base=0, channel_multiplier=0)
            pool.iota(rowp_i[:], [[1, 1]], base=0, channel_multiplier=1)
            pool.iota(place_i[:], [[P, ET]], base=0, channel_multiplier=1).then_inc(s_iota, 1)
            pool.memset(none_i[:], EP).then_inc(s_none, 1)
            pool.memset(edge_f[:], -1.0).then_inc(s_none, 1)
            pool.memset(s["ident"][:], 0.0).then_inc(s_id, 1)
            pool.wait_ge(s_id, 1)
            pool.affine_select(out=s["ident"][:], in_=s["ident"][:], compare_op=ALU.not_equal, fill=1.0, base=0,
                               pattern=[[-1, P]], channel_multiplier=1).then_inc(s_id, 1)
            pool.memset(s["headmap"][:], 1.0).then_inc(s_hm, 1)
            pool.wait_ge(s_hm, 1)
            pool.affine_select(out=s["headmap"][:], in_=s["headmap"][:], compare_op=ALU.is_ge, fill=0.0, base=0,
                               pattern=[[1, P]], channel_multiplier=-HR).then_inc(s_hm, 1)
            pool.wait_ge(s_hm, 2)
            pool.affine_select(out=s["headmap"][:], in_=s["headmap"][:], compare_op=ALU.is_ge, fill=0.0, base=HR - 1,
                               pattern=[[-1, P]], channel_multiplier=HR).then_inc(s_hm, 1)
            pool.wait_ge(s_av, 64)
            for n in range(4):
                if n == 0:
                    pool.wait_ge(s_w1, 16)
                if n == 2:
                    pool.wait_ge(s_w2, 16 * HEADS)
                if n >= 1:
                    pool.wait_ge(s_red, n)
                w = wraw if n < 2 else w2raw
                pool.tensor_tensor(prod[:], w[:], avec[:, n, :].unsqueeze(1).broadcast_to([P, KC, D]),
                                   ALU.mult).then_inc(s_prod, 1)
                if n == 1 or n == 3:
                    part = n // 2
                    pool.wait_ge(s_split, part + 1)
                    if part == 0:
                        for kk in range(KC):
                            pool.tensor_tensor(s["w1s"][:, 1, kk, :].rearrange("p (m h r) -> p m h r", h=HEADS, r=HR),
                                               wraw[:, kk, :].rearrange("p (h m r) -> p m h r", h=HEADS, r=HR),
                                               s["w1s"][:, 0, kk, :].bitcast(F32).rearrange("p (m h r) -> p m h r", h=HEADS, r=HR),
                                               ALU.subtract)
                    else:
                        pool.tensor_tensor(s["w2s"][:, 1, :, :], w2raw[:], s["w2s"][:, 0, :, :].bitcast(F32), ALU.subtract)
            pool.wait_ge(s_none, 18)
            pool.wait_ge(s_endi, 1)
            for t in range(ET):
                pool.indirect_dma_start(d["node_pos"], bass.IndirectOffsetOnAxis(ap=end_i[:, t:t + 1], axis=0),
                                        place_i[:, t:t + 1], None, bounds_check=N - 1,
                                        oob_is_err=False).then_inc(s_scat, 16)

        @block.vector
        def _(dve):
            n_done = [0]

            def step(ins):
                n_done[0] += 1
                ins.then_inc(s_dve, 1)
                dve.wait_ge(s_dve, n_done[0])

            dve.wait_ge(s_iota, 1)
            dve.tensor_copy(frac[:], frac_i[:])
            step(dve.tensor_copy(rowp[:], rowp_i[:]))
            dve.tensor_copy(iota_f[:], frac[:])
            dve.memset(key[:, E:EP], float(N))
            dve.memset(less[:], 0.0)
            step(dve.tensor_scalar(frac[:], frac[:], 1.0 / 256, None, ALU.mult))
            step(dve.tensor_scalar(rowp[:], rowp[:], 1.0 / 256, None, ALU.mult))
            dve.wait_ge(s_col, 64)
            step(dve.tensor_copy(dst_f[:], col_i[:, 1, :]))
            dve.tensor_scalar(thr[:, 0, :], dst_f[:], 0.75, None, ALU.add)
            dve.tensor_scalar(thr[:, 1, :], dst_f[:], -0.25, None, ALU.add)
            step(dve.tensor_scalar(thr[:, 2, :], dst_f[:], rowp[:, 0:1], None, ALU.add))
            dve.tensor_scalar(nthr[:, 0:2, :], thr[:, 0:2, :], -1.0, None, ALU.mult)
            dve.tensor_scalar(nthr[:, 2, :], thr[:, 2, :], -1.0, 1.0 / 512, ALU.mult, ALU.add)
            dve.wait_ge(s_key, 16)
            step(dve.tensor_copy(key[:, 0:E], key[:, 0:E].bitcast(I32)))
            dve.tensor_tensor(key[:].rearrange("p (t j) -> p t j", j=P), key[:].rearrange("p (t j) -> p t j", j=P),
                              frac[:].unsqueeze(1).broadcast_to([P, ET, P]), ALU.add).then_inc(s_colr, 1)
            dve.wait_ge(s_colr, 1)
            for t in range(ET):
                if t in ACT_TILES:
                    continue
                for n, (lo, hi) in enumerate(((0, t * P), ((t + 1) * P, EP), (t * P, (t + 1) * P))):
                    if hi > lo:
                        step(dve.tensor_scalar(junk_v[:, lo:hi], key[:, lo:hi], thr[:, n, t:t + 1], None, ALU.is_lt,
                                               ALU.add, accum_out=less[:, n, t:t + 1]))
            for n in range(2):
                dve.tensor_scalar(part_i[:, 2 * n, :], col_i[:, n, :], 7, None, ALU.logical_shift_right)
                dve.tensor_scalar(part_i[:, 2 * n + 1, :], col_i[:, n, :], P - 1, None, ALU.bitwise_and)
            dve.wait_ge(s_cnt_a, 1)
            step(dve.tensor_tensor(rank[:, 0, :], less[:, 0, :], less[:, 1, :], ALU.add))
            step(dve.tensor_tensor(rank[:, 1, :], rank[:, 0, :], less[:, 2, :], ALU.add))
            t0 = ACT_TILES[0]
            step(dve.tensor_scalar(rank[:, 2, t0:ET], rank[:, 1, t0:ET], -0.5, EP / 2.0, ALU.mult, ALU.add))
            dve.tensor_copy(rank_i[:, 0, 0:t0], rank[:, 1, 0:t0])
            dve.tensor_copy(rank_i[:, 0, t0:ET], rank[:, 2, t0:ET])
            step(dve.tensor_copy(part_f[:], part_i[:]))
            dve.tensor_scalar(rank_i[:, 1, :], rank_i[:, 0, :], 7, None, ALU.logical_shift_right)
            step(dve.tensor_scalar(rank_i[:, 2, :], rank_i[:, 0, :], P - 1, None, ALU.bitwise_and))
            step(dve.tensor_copy(hl_f[:], rank_i[:, 1:3, :]))
            dve.tensor_tensor(oh_lo[:], iota_f[:].unsqueeze(1).broadcast_to([P, ET, P]),
                              hl_f[:, 1, :].unsqueeze(2).broadcast_to([P, ET, P]), ALU.is_equal)
            step(dve.tensor_tensor(ohr[:], iota_f[:, 0:ET].unsqueeze(1).broadcast_to([P, ET, ET]),
                                   hl_f[:, 0, :].unsqueeze(2).broadcast_to([P, ET, ET]), ALU.is_equal))
            for n in range(4):
                last = dve.tensor_tensor(oh_hi[:, :, n, :], ohr[:],
                                         part_f[:, n, :].unsqueeze(2).broadcast_to([P, ET, ET]), ALU.mult)
            last.then_inc(s_oh, 1)
            dve.wait_ge(s_sorted, 1)
            step(dve.tensor_copy(sorted4[:], p_sort[:, 0:4 * ET].rearrange("p (n t) -> p n t", t=ET)))
            for n in range(2):
                ins = dve.scalar_tensor_tensor(col_f[:, n, :], sorted4[:, 2 * n, :], float(P), sorted4[:, 2 * n + 1, :],
                                               ALU.mult, ALU.add)
            n_done[0] += 1
            ins.then_inc(s_dve, 1)
            dve.wait_ge(s_dve, n_done[0])
            dve.tensor_scalar(clip_f[:], col_f[:, 1, :], float(N - 1), None, ALU.min).then_inc(s_vec, 1)
            dve.wait_ge(s_vec, 1)
            gi = s["gidx"][:].rearrange("p (g n j) -> p g n j", n=2, j=TG)
            dve.tensor_copy(gi[:, :, 1, :], col_f[:, 0, :].rearrange("p (g j) -> p g j", j=TG))
            dve.tensor_copy(gi[:, :, 0, :], clip_f[:].rearrange("p (g j) -> p g j", j=TG))
            dve.wait_ge(s_row, 1)
            dve.tensor_copy(dst_row[:], p_row[0:ET, 0:P]).then_inc(s_row, 1)
            for n in range(2):
                dve.wait_ge(s_prod, n + 1)
                dve.tensor_reduce(v_f[:, n, :, :].rearrange("p k h -> p (k h)"),
                                  prod[:].rearrange("p k (h c) -> p (k h) c", c=HC), AX.X, ALU.add).then_inc(s_red, 1)
            dve.wait_ge(s_red, 2)
            step(dve.tensor_copy(s["v1"][:, :, 0, :, :], v_f[:]))
            dve.tensor_tensor(s["v1"][:, :, 1, :, :], v_f[:], s["v1"][:, :, 0, :, :].bitcast(F32), ALU.subtract)
            step(dve.memset(s["v2"][:], 0.0))
            dve.wait_ge(s_win, 16)
            dve.tensor_tensor(eq[:, 0, :], window[:, 1:P + 1], window[:, 0:P], ALU.is_equal)
            step(dve.tensor_tensor(eq[:, 1, :], window[:, 1:P + 1], window[:, 2:P + 2], ALU.is_equal))
            dve.tensor_scalar(masks[:, 0, :], eq[:, 0, :], 0.5, BIG, ALU.subtract, ALU.mult)
            dve.tensor_scalar(masks[:, 1, :], eq[:, 0, :], 1.0, 1e30, ALU.subtract, ALU.mult).then_inc(s_maskst, 1)
            dve.scalar_tensor_tensor(end_row[:], eq[:, 1, :], 20000.0, window[:, 1:P + 1], ALU.mult, ALU.add).then_inc(s_endT, 1)
            dve.wait_ge(s_endT, 2)
            dve.tensor_copy(end_i[:], p_end[:, 0:ET]).then_inc(s_endi, 1)
            for n in range(2):
                dve.wait_ge(s_prod, n + 3)
                dve.tensor_reduce(s["v2"][:, :, 32 * n], prod[:], AX.X, ALU.add).then_inc(s_red, 1)

        @block.tensor
        def _(pe):
            pe.wait_ge(s_oh, 1)
            for t in range(ET):
                mm = pe.matmul(p_sort[:, 0:4 * ET], oh_lo[:, t, :], oh_hi[:, t, :, :], start=(t == 0), stop=(t == ET - 1))
            mm.then_inc(s_sorted, 1)
            pe.wait_ge(s_id, 2)
            pe.wait_ge(s_vec, 1)
            pe.transpose(p_row[0:ET, 0:P], col_f[:, 1, :], s["ident"][:]).then_inc(s_row, 1)
            pe.wait_ge(s_endT, 1)
            pe.transpose(p_end[:, 0:ET], end_row[:], s["ident"][0:ET, 0:ET]).then_inc(s_endT, 1)

        @block.scalar
        def _(act):
            act.wait_ge(s_w1, 16)
            for kk in range(KC):
                hi = act.activation(s["w1s"][:, 0, kk, :].rearrange("p (m h r) -> p m h r", h=HEADS, r=HR),
                                    wraw[:, kk, :].rearrange("p (h m r) -> p m h r", h=HEADS, r=HR), ACT.Copy)
            hi.then_inc(s_split, 1)
            act.wait_ge(s_colr, 1)
            n = 0
            for t in ACT_TILES:
                for j, (lo, hi_) in enumerate(((0, t * P), ((t + 1) * P, EP), (t * P, (t + 1) * P))):
                    if hi_ > lo:
                        wait(act, s_cnt_v, n)
                        n += 1
                        act.activation(junk_a[:, lo:hi_], key[:, lo:hi_], ACT.Sign, bias=nthr[:, j, t:t + 1],
                                       accum_out=less[:, j, t:t + 1]).then_inc(s_cnt_v, 1)
            act.wait_ge(s_cnt_v, n)
            act.sem_inc(s_cnt_a, 1)
            act.wait_ge(s_w2, 16 * HEADS)
            act.activation(s["w2s"][:, 0, :, :], w2raw[:], ACT.Copy).then_inc(s_split, 1)



def softmax_steps(dve, b, sem, g, np_, mask, mask_in, x_read):
    def first():
        dve.wait_ge(*mask_in)
        dve.wait_ge(sem["e_out"], g + 1)
        if sem["carry"](g):
            wait(dve, sem["z"], g)
            dve.tensor_copy(b["m"][:, 0:1], b["m"][:, GE:GE + 1])
        dve.scalar_tensor_tensor(b["e"][:], b["e"][:], SLOPE, b["e"][:], ALU.mult, ALU.max).then_inc(sem["lrelu"], 1)
        dve.wait_ge(sem["lrelu"], g + 1)
        dve.tensor_tensor_scan(b["m"][:, 1:GE + 1], mask[:, 0, :], b["e"][:], b["m"][:, 0:1],
                               ALU.min, ALU.max).then_inc(sem["m"], 1)
        dve.wait_ge(sem["m"], g + 1)
        wait(dve, *x_read)
        dve.tensor_tensor(b["x"][:, 1, :], b["e"][:], b["m"][:, 1:GE + 1], ALU.subtract)
        dve.tensor_tensor(b["x"][:, 0, :], b["m"][:, 0:GE], b["m"][:, 1:GE + 1], ALU.subtract).then_inc(sem["diff"], 1)
        dve.wait_ge(sem["diff"], g + 1)
        dve.scalar_tensor_tensor(b["x"][:, 0, :], b["x"][:, 0, :], 0.0, mask[:, 1, :], ALU.min,
                                 ALU.add).then_inc(sem["x"], 1)

    def second():
        dve.wait_ge(sem["exp"], g + 1)
        if sem["carry"](g):
            dve.tensor_copy(b["z"][:, 0:1], b["z"][:, GE:GE + 1]).then_inc(sem["zc"], 1)
            dve.wait_ge(sem["zc"], g)
        dve.tensor_tensor_scan(b["z"][:, 1:GE + 1], b["x"][:, 0, :], b["x"][:, 1, :], b["z"][:, 0:1],
                               ALU.mult, ALU.add).then_inc(sem["z"], 1)
        dve.wait_ge(sem["z"], g + 1)
        dve.tensor_tensor(b["x"][:, 0, :], b["x"][:, 0, :], b["z"][:, 0:GE], ALU.mult)
        dve.tensor_scalar(b["r"][:], b["z"][:, 1:GE + 1], 1e-16, None, ALU.add).then_inc(sem["zz"], 1)
        dve.wait_ge(sem["zz"], g + 1)
        dve.reciprocal(b["r"][:], b["r"][:]).then_inc(sem["rz"], 1)
        dve.wait_ge(sem["rz"], g + 1)
        dve.tensor_tensor(b["x"][:], b["x"][:], b["r"][:].unsqueeze(1).broadcast_to([np_, 2, GE]),
                          ALU.mult).then_inc(sem["ab"], 1)

    return first, second


def softmax_kit(k, np_):
    b = {"m": k.sb("run_max", [np_, GE + 1]), "z": k.sb("run_sum", [np_, GE + 1]), "e": k.sb("logit", [np_, GE]),
         "x": k.sb("expo", [np_, 2, GE]), "r": k.sb("rcp", [np_, GE])}
    sem = {n: k.sem("s_sm_" + n) for n in ("e_out", "lrelu", "m", "diff", "x", "exp", "zc", "z", "zz", "rz", "ab")}
    return b, sem


def gat_layer_1(nc, a, d, s):
    with ExitStack() as ctx:
        k = Kit(nc, ctx, "a_")
        xt = k.sb("xt", [P, 2, 2, KC, GE], F32R)
        xd = k.sb("xd", [P, 2, KC, 2 * P], F32R)
        raw = k.sb("raw", [P, 4, D])
        msg = k.sb("msg", [P, 2, GE])
        agg = k.sb("agg", [P, 2, GE])
        pos_part = k.sb("pos_part", [P, 2, GE])
        neg_part = k.sb("neg_part", [P, 2, GE])
        g1 = k.sb("g1", [P, 2, GE])
        rows = k.sb("rows", [P, 2, TG, P])
        ab = k.sb("ab", [P, 2, GE])
        carry = k.sb("carry", [P, KC])
        mask = k.sb("mask", [HEADS, 2, 2, GE])
        b, sem = softmax_kit(k, HEADS)
        stage = k.sb("stage", [P, 8], I32)
        pstage = k.sb("pstage", [P, 8], I32)
        stats = k.sb("stats", [P, 2, 2, 2, 6])
        mv = k.sb("mv", [P, 2, 2, 2])
        rstd = k.sb("rstd", [P, 2, 2])
        nmr = k.sb("nmr", [P, 2, 2])
        consts = k.sb("consts", [P, 6])
        logit2 = k.sb("logit2", [64, GE])
        bdef = k.sb("bdef", [P, 3, KC])
        ldef = k.sb("ldef", [64, 1])
        T = [k.ps("p_t0"), k.ps("p_t1")]
        H = [k.ps("p_h0"), k.ps("p_h1")]
        LG, EX, AS, RO = k.ps("p_lg"), k.ps("p_ex"), k.ps("p_as"), k.ps("p_ro")
        raw_in, st, mask_in = k.sems("s_raw", 4), k.sems("s_st", 2), k.sems("s_mask", 2)
        (passed_p, passed_v, pos_in, staged, stat, mvr, vv, pw, ln, normed, turned, hi_out, lo_out, dlog, lg_done, ab_ex, ab_out,
         h_done, msg_done, agg_done, car, neg_done, elu_done, g_done, tail_done, rows_out, as_done, as_out, st_as,
         dflt, init) = [k.sem(f"s_a{i}") for i in range(31)]
        sem["carry"] = lambda g: not (isinstance(g, int) and g == 0)
        block = k.block()

        def groups(eng, body):
            body(0, 0, True, False)
            with eng.Fori(0, (EG - 2) // 2) as i:
                body(2 * i + 1, 1, False, False)
                body(2 * i + 2, 0, False, False)
            body(EG - 1, (EG - 1) % 2, False, True)

        @block.gpsimd
        def _(pool):
            for n, v in enumerate((-0.5, EPS, -1.0)):
                pool.memset(consts[:, 2 * n:2 * n + 2], v)
            pool.memset(b["m"][:, 0:1], 0.0)
            pool.memset(b["z"][:, 0:1], 0.0)
            pool.memset(carry[:], 0.0).then_inc(init, 1)
            pool.wait_ge(init, 1)

            def tile_pair(g, u):
                for j in (2 * u, 2 * u + 1):
                    q = 8 * g + j
                    wait(pool, turned, 2 * q - 6)
                    pool.tensor_copy(stage[:, j:j + 1], s["gidx"][:, bass.ds(q, 1)]).then_inc(staged, 1)
                    carried_wait(pool, passed_p, staged, q + 1)
                    pool.indirect_dma_start(raw[:, j % 4, :], None, a["x"],
                                            bass.IndirectOffsetOnAxis(ap=stage[:, j:j + 1], axis=0)).then_inc(raw_in[j % 4], 16)
                    pool.indirect_dma_start(pstage[:, j:j + 1], None, d["node_pos"],
                                            bass.IndirectOffsetOnAxis(ap=stage[:, j:j + 1], axis=0)).then_inc(pos_in, 16)
                r = 4 * g + u
                w = u % 2
                pool.wait_ge(mvr, r + 1)
                pool.tensor_tensor(rstd[:, w, :], mv[:, w, :, 1], consts[:, 2:4], ALU.add)
                pool.tensor_tensor(nmr[:, w, :], mv[:, w, :, 0], consts[:, 4:6], ALU.mult).then_inc(vv, 1)
                pool.wait_ge(vv, r + 1)
                pool.tensor_tensor(rstd[:, w, :], rstd[:, w, :], consts[:, 0:2], ALU.pow).then_inc(pw, 1)
                pool.wait_ge(pw, r + 1)
                pool.tensor_tensor(nmr[:, w, :], nmr[:, w, :], rstd[:, w, :], ALU.mult).then_inc(ln, 1)

            def body(g):
                for u in range(4):
                    tile_pair(g, u)
                pool.wait_ge(pos_in, 128 * g + 128)
                pool.tensor_copy(s["pos"][:, bass.ds(8 * g, 8)], pstage[:]).then_inc(init, 1)
                pool.wait_ge(init, g + 2)

            body(0)
            with pool.Fori(1, EG) as g:
                body(g)

        @block.sync
        def _(sp):
            def mask_load(g, w):
                wait(sp, sem["ab"], g - 1)
                sp.dma_start(mask[:, w, :, :], d["masks"][:, bass.ds(g * GE, GE)].partition_broadcast(HEADS)).then_inc(mask_in[w], 16)

            def row_store(g, m):
                c = 6 * g + m
                sp.wait_ge(rows_out, c + 1)
                sp.dma_start(d["layer1"][bass.ds(g * GE, GE), m * P:(m + 1) * P].rearrange("(t p) j -> p t j", p=P),
                             rows[:, m % 2, :, :]).then_inc(st[m % 2], 16)

            def logit_store(g):
                sp.wait_ge(as_out, g + 1)
                sp.dma_start(d["layer1"][bass.ds(g * GE, GE), D:D + 1].rearrange("n o -> o n"), logit2[0:1, :], allow_slow_non_contiguous=True).then_inc(st_as, 16)
                sp.dma_start(d["dst_logit"][bass.ds(g * GE, GE), :].rearrange("n o -> o n"), logit2[32:33, :], allow_slow_non_contiguous=True).then_inc(st_as, 16)

            mask_load(0, 0)
            mask_load(1, 1)
            sp.wait_ge(dflt, 5)
            sp.dma_start(d["layer1"][EP:EP + 1, 0:D].rearrange("o (m p) -> p (o m)", p=P), bdef[:, 0, :], allow_slow_non_contiguous=True).then_inc(dflt, 16)
            sp.dma_start(d["layer1"][EP:EP + 1, D:D + 1], ldef[0:1, :]).then_inc(dflt, 16)
            sp.dma_start(d["dst_logit"][EP:EP + 1, :], ldef[32:33, :]).then_inc(dflt, 16)

            def body(g, w, first, last):
                if not first and not last:
                    mask_load(g + 1, 1 - w)
                for m in range(6):
                    if m >= 2:
                        row_store(g, m - 2)
                    elif not first:
                        row_store(g - 1, m + 4)
                        if m == 1:
                            logit_store(g - 1)

            groups(sp, body)
            row_store(EG - 1, 4)
            row_store(EG - 1, 5)
            logit_store(EG - 1)
            for w in range(2):
                sp.wait_ge(st[w], 16 * 3 * EG)
            sp.wait_ge(st_as, 32 * EG)
            sp.wait_ge(dflt, 53)

        @block.scalar
        def _(act):
            def normalise(G, u):
                r = 4 * G + u
                act.wait_ge(ln, r + 1)
                for n in range(2):
                    act.activation(raw[:, (2 * u + n) % 4, :], raw[:, (2 * u + n) % 4, :], ACT.Identity,
                                   bias=nmr[:, u % 2, n:n + 1], scale=rstd[:, u % 2, n:n + 1]).then_inc(normed, 1)

            def high(G, W, j):
                q = 8 * G + j
                if j in (0, 1):
                    wait(act, dlog, 2 * G)
                elif j in (2, 3):
                    act.wait_ge(dlog, 2 * G + 1)
                else:
                    wait(act, h_done, 6 * G - 6)
                for h in range(2):
                    act.wait_ge(turned, 2 * q + h + 1)
                    if j < 4:
                        out = xd[:, 0, 3 * h:3 * h + 3, (j % 2) * P:(j % 2 + 1) * P]
                    else:
                        out = xt[:, W, 0, 3 * h:3 * h + 3, (j - 4) * P:(j - 3) * P]
                    act.activation(out, T[h][:, 0:3 * P].rearrange("p (k j) -> p k j", k=3), ACT.Copy).then_inc(hi_out, 1)

            def logit_copy(G):
                act.wait_ge(lg_done, G + 1)
                wait(act, sem["ab"], G)
                act.activation(b["e"][:], LG[0:HEADS, :], ACT.Copy).then_inc(sem["e_out"], 1)

            def exps(G):
                act.wait_ge(sem["x"], G + 1)
                act.activation(b["x"][:], b["x"][:], ACT.Exp).then_inc(sem["exp"], 1)

            def ab_copy(g):
                wait(act, agg_done, 6 * g)
                act.wait_ge(ab_ex, 2 * g + 1)
                act.activation(ab[:, 0, :], EX[:], ACT.Copy).then_inc(ab_out, 1)
                act.wait_ge(ab_ex, 2 * g + 2)
                act.activation(ab[:, 1, :], LG[:], ACT.Copy).then_inc(ab_out, 1)

            def elu(g, m):
                c = 6 * g + m
                act.wait_ge(neg_done, c + 1)
                wait(act, g_done, c - 1)
                act.activation(pos_part[:, m % 2, :], agg[:, m % 2, :], ACT.Relu, bias=s["b1col"][:, m:m + 1])
                act.activation(neg_part[:, m % 2, :], neg_part[:, m % 2, :], ACT.Exp).then_inc(elu_done, 1)

            def rows_copy(g, m):
                c = 6 * g + m
                act.wait_ge(tail_done, c + 1)
                wait(act, st[m % 2], 16 * (3 * g + m // 2))
                act.activation(rows[:, m % 2, :, :], RO[:].rearrange("p (t j) -> p t j", t=TG), ACT.Copy).then_inc(rows_out, 1)

            def logit2_copy(g):
                act.wait_ge(as_done, g + 1)
                wait(act, st_as, 32 * g)
                act.activation(logit2[:], AS[0:64, :], ACT.Copy).then_inc(as_out, 1)

            act.activation(bdef[:, 0, :], s["b1col"][:], ACT.Relu)
            act.wait_ge(dflt, 1)
            act.activation(bdef[:, 1, :], bdef[:, 1, :], ACT.Exp).then_inc(dflt, 1)
            act.wait_ge(dflt, 4)
            act.activation(ldef[:], AS[0:64, 0:1], ACT.Copy).then_inc(dflt, 1)
            for u in range(4):
                normalise(0, u)
                high(0, 0, 2 * u)
                high(0, 0, 2 * u + 1)
            logit_copy(0)
            exps(0)

            def body(g, w, first, last):
                for m in range(6):
                    if not (first and m == 0):
                        elu(g if m else g - 1, (m - 1) % 6)
                    if m == 0:
                        ab_copy(g)
                    if not last:
                        if m in (1, 2, 3, 4):
                            high(g + 1, 1 - w, {1: 1, 2: 3, 3: 5, 4: 7}[m])
                        if m < 4:
                            normalise(g + 1, m)
                    if not last and m == 5:
                        exps(g + 1)
                    if m >= 2:
                        rows_copy(g, m - 2)
                    elif not first:
                        rows_copy(g - 1, m + 4)
                        if m == 1:
                            logit2_copy(g - 1)
                    if not last:
                        if m < 4:
                            high(g + 1, 1 - w, 2 * m)
                        if m == 4:
                            logit_copy(g + 1)

            groups(act, body)
            elu(EG - 1, 5)
            rows_copy(EG - 1, 4)
            rows_copy(EG - 1, 5)
            logit2_copy(EG - 1)

        @block.vector
        def _(dve):
            def moments(G, u):
                r, w = 4 * G + u, u % 2
                wait(dve, ln, r - 1)
                wait(dve, normed, 2 * r - 2)
                for n in range(2):
                    j = 2 * u + n
                    dve.wait_ge(raw_in[j % 4], 16 * (2 * G + j // 4 + 1))
                    for h in range(2):
                        last = dve.bn_stats(stats[:, w, n, h, :], raw[:, j % 4, h * HALF:(h + 1) * HALF])
                last.then_inc(stat, 1)
                carried_wait(dve, passed_v, stat, r + 1)
                dve.bn_aggr(mv[:, w, 0, :], stats[:, w, 0, :, :])
                dve.bn_aggr(mv[:, w, 1, :], stats[:, w, 1, :, :]).then_inc(mvr, 1)

            def low(G, W, j):
                q = 8 * G + j
                for h in range(2):
                    dve.wait_ge(hi_out, 2 * q + h + 1)
                    if j < 4:
                        v = xd[:, :, 3 * h:3 * h + 3, (j % 2) * P:(j % 2 + 1) * P]
                    else:
                        v = xt[:, W, :, 3 * h:3 * h + 3, (j - 4) * P:(j - 3) * P]
                    dve.tensor_tensor(v[:, 1], T[h][:, 0:3 * P].rearrange("p (k j) -> p k j", k=3), v[:, 0].bitcast(F32),
                                      ALU.subtract).then_inc(lo_out, 1)

            def scan_chunk(g, m):
                c = 6 * g + m
                if m == 0:
                    dve.wait_ge(ab_out, 2 * g + 2)
                dve.wait_ge(h_done, c + 1)
                dve.tensor_tensor(msg[:, m % 2, :], H[m % 2][:], ab[:, 1, :], ALU.mult).then_inc(msg_done, 1)
                wait(dve, elu_done, c - 1)
                dve.wait_ge(msg_done, c + 1)
                dve.tensor_tensor_scan(agg[:, m % 2, :], ab[:, 0, :], msg[:, m % 2, :], carry[:, m:m + 1],
                                       ALU.mult, ALU.add).then_inc(agg_done, 1)
                dve.wait_ge(agg_done, c + 1)
                dve.tensor_copy(carry[:, m:m + 1], agg[:, m % 2, GE - 1:GE]).then_inc(car, 1)
                wait(dve, g_done, c - 1)
                dve.tensor_scalar(neg_part[:, m % 2, :], agg[:, m % 2, :], s["b1col"][:, m:m + 1], 0.0, ALU.add,
                                  ALU.min).then_inc(neg_done, 1)

            def join(g, m):
                c = 6 * g + m
                dve.wait_ge(elu_done, c + 1)
                wait(dve, tail_done, c - 1)
                dve.scalar_tensor_tensor(g1[:, m % 2, :], neg_part[:, m % 2, :], -1.0, pos_part[:, m % 2, :], ALU.add,
                                         ALU.add).then_inc(g_done, 1)

            def softmax(G, W, loaded):
                return softmax_steps(dve, b, sem, G, HEADS, mask[:, W, :, :], (mask_in[W], loaded), (ab_ex, 2 * G))

            dve.wait_ge(init, 1)
            dve.tensor_scalar(bdef[:, 1, :], s["b1col"][:], 0.0, None, ALU.min).then_inc(dflt, 1)
            dve.wait_ge(dflt, 2)
            dve.scalar_tensor_tensor(bdef[:, 0, :], bdef[:, 1, :], -1.0, bdef[:, 0, :], ALU.add, ALU.add).then_inc(dflt, 1)
            for u in range(4):
                moments(0, u)
                low(0, 0, 2 * u)
                low(0, 0, 2 * u + 1)
            first_, second_ = softmax(0, 0, 16)
            first_()
            second_()

            def body(g, w, first, last):
                for m in range(6):
                    if not last:
                        if m in (1, 2, 3, 4):
                            low(g + 1, 1 - w, {1: 1, 2: 3, 3: 5, 4: 7}[m])
                        if m < 4:
                            moments(g + 1, m)
                    if not (first and m == 0):
                        join(g if m else g - 1, (m - 1) % 6)
                    if not last and m == 5:
                        first_, second_ = softmax(g + 1, 1 - w, 8 * g + (24 if w else 16))
                        first_()
                    scan_chunk(g, m)
                    if not last and m == 5:
                        second_()
                    if not last and m < 4:
                        low(g + 1, 1 - w, 2 * m)

            groups(dve, body)
            join(EG - 1, 5)

        @block.tensor
        def _(pe):
            def turn(G, j):
                q = 8 * G + j
                pe.wait_ge(normed, q + 1)
                for h in range(2):
                    wait(pe, lo_out, 2 * q + h - 1)
                    for kk in range(3):
                        mm = pe.transpose(T[h][:, kk * P:(kk + 1) * P],
                                          raw[:, j % 4, (3 * h + kk) * P:(3 * h + kk + 1) * P], s["ident"][:])
                    mm.then_inc(turned, 1)

            def passes(out, lhs, rhs, start, stop, lint=False):
                for i, (x, y) in enumerate(((0, 0), (1, 0), (0, 1))):
                    mm = pe.matmul(out, lhs(x), rhs(y), start=start and i == 0, stop=stop and i == 2, skip_group_check=lint)
                return mm

            def dst_logits(G, hh):
                pe.wait_ge(lo_out, 16 * G + 4 * hh + 4)
                if hh == 0:
                    wait(pe, ab_out, 2 * G)
                for kk in range(KC):
                    mm = passes(LG[0:HEADS, hh * 2 * P:(hh + 1) * 2 * P], lambda i: s["v1"][:, 1, i, kk, :],
                                lambda i: xd[:, i, kk, :], hh == 0 and kk == 0, False, True)
                mm.then_inc(dlog, 1)

            def src_logits(G, W):
                pe.wait_ge(lo_out, 16 * G + 16)
                for kk in range(KC):
                    mm = passes(LG[0:HEADS, :], lambda i: s["v1"][:, 0, i, kk, :], lambda i: xt[:, W, i, kk, :],
                                False, kk == KC - 1, True)
                mm.then_inc(lg_done, 1)

            def spread(g):
                pe.wait_ge(sem["ab"], g + 1)
                pe.matmul(EX[:], s["headmap"][:], b["x"][:, 0, :], start=True, stop=True).then_inc(ab_ex, 1)
                pe.matmul(LG[:], s["headmap"][:], b["x"][:, 1, :], start=True, stop=True).then_inc(ab_ex, 1)

            def products(g, w, m, part):
                c = 6 * g + m
                if part == 0:
                    wait(pe, msg_done, c - 1)
                for kk in (range(0, 3), range(3, KC))[part]:
                    mm = passes(H[m % 2][:], lambda i: s["w1s"][:, i, kk, m * P:(m + 1) * P],
                                lambda i: xt[:, w, i, kk, :], kk == 0, kk == KC - 1, True)
                if part == 1:
                    mm.then_inc(h_done, 1)

            def tail(g, m):
                c = 6 * g + m
                pe.wait_ge(g_done, c + 1)
                wait(pe, rows_out, c)
                if m == 0:
                    wait(pe, as_out, g)
                mm = pe.matmul(AS[0:64, :], s["v2"][:, m, :], g1[:, m % 2, :], start=(m == 0), stop=(m == 5), skip_group_check=True)
                if m == 5:
                    mm.then_inc(as_done, 1)
                for t in range(TG):
                    mm = pe.transpose(RO[:, t * P:(t + 1) * P], g1[:, m % 2, t * P:(t + 1) * P], s["ident"][:])
                mm.then_inc(tail_done, 1)

            pe.wait_ge(dflt, 3)
            for m in range(KC):
                mm = pe.matmul(AS[0:64, 0:1], s["v2"][:, m, :], bdef[:, 0, m:m + 1], start=(m == 0), stop=(m == KC - 1))
            mm.then_inc(dflt, 1)
            pe.wait_ge(dflt, 5)
            for j in range(8):
                turn(0, j)
                if j in (1, 3):
                    dst_logits(0, j // 2)
            src_logits(0, 0)

            def body(g, w, first, last):
                for m in range(6):
                    products(g, w, m, 0)
                    if m == 0:
                        spread(g)
                    if not last and m in (1, 2, 3, 4):
                        turn(g + 1, {1: 1, 2: 3, 3: 5, 4: 7}[m])
                    products(g, w, m, 1)
                    if m >= 2:
                        tail(g, m - 2)
                    elif not first:
                        tail(g - 1, m + 4)
                    if not last:
                        if m in (1, 2):
                            dst_logits(g + 1, m - 1)
                        if m < 4:
                            turn(g + 1, 2 * m)
                        if m == 4:
                            src_logits(g + 1, 1 - w)

            groups(pe, body)
            tail(EG - 1, 4)
            tail(EG - 1, 5)


def gat_layer_2(nc, a, d, s):
    with ExitStack() as ctx:
        k = Kit(nc, ctx, "b_")
        xt = k.sb("xt", [P, 2, 2, KC, GE], F32R)
        raw = k.sb("raw", [P, 2, TG, RW])
        dlog = k.sb("dlog", [P, 2, TG])
        lcol = k.sb("lcol", [P, 2, TG, HEADS])
        msg = k.sb("msg", [P, 2, GE])
        agg = k.sb("agg", [P, 2, GE])
        ab = k.sb("ab", [P, 2, GE])
        carry = k.sb("carry", [P, KC])
        mask = k.sb("mask", [HEADS, 2, 2, GE])
        b, sem = softmax_kit(k, HEADS)
        sem["carry"] = lambda g: not (isinstance(g, int) and g == 0)
        stage = k.sb("stage", [P, 2, 8], I32)
        bias = k.sb("bias", [P, D])
        rows = k.sb("rows", [P, 2, D])
        w1raw = k.sb("w1raw", [P, KC, EXPERTS, HID])
        w2raw = k.sb("w2raw", [P, FC, D])
        T = [k.ps("p_t0"), k.ps("p_t1")]
        LG, EX = k.ps("p_lg"), k.ps("p_ex")
        ROW = [k.ps(f"p_row{i}") for i in range(4)]
        raw_in, st, mask_in = k.sems("s_raw", 2), k.sems("s_st", 2), k.sems("s_mask", 2)
        (passed_p, staged, init, lcol_done, lg_done, ab_ex, ab_out, turned, msg_done, agg_done, car, hi_out, lo_out,
         unit_done, row_out, bias_in, dflt, ffn_in, ffn_hi, ffn_lo) = [
            k.sem("s_" + n) for n in ("passed_p", "staged", "init", "lcol", "lg", "ab_ex", "ab_out", "turned", "msg", "agg",
                                      "car", "hi", "lo", "unit", "row", "bias", "dflt", "ffn_in", "ffn_hi", "ffn_lo")]
        block = k.block()

        def groups(eng, body):
            body(0, 0, True, True)
            with eng.Fori(0, (EG - 4) // 2) as i:
                body(2 * i + 1, 1, True, True)
                body(2 * i + 2, 0, True, True)
            body(EG - 3, (EG - 3) % 2, True, True)
            body(EG - 2, EG % 2, True, False)
            body(EG - 1, (EG - 1) % 2, False, False)

        @block.gpsimd
        def _(pool):
            pool.memset(b["m"][:, 0:1], 0.0)
            pool.memset(b["z"][:, 0:1], 0.0)
            pool.memset(carry[:], 0.0).then_inc(init, 1)

            def gather(g, w):
                wait(pool, turned, 6 * g - 6)
                pool.tensor_copy(stage[:, w, :], s["pos"][:, bass.ds(8 * g, 8)]).then_inc(staged, 1)
                carried_wait(pool, passed_p, staged, g + 1)
                for j in range(TG):
                    pool.indirect_dma_start(dlog[:, w, j:j + 1], None, d["dst_logit"],
                                            bass.IndirectOffsetOnAxis(ap=stage[:, w, j:j + 1], axis=0)).then_inc(raw_in[w], 16)
                    pool.indirect_dma_start(raw[:, w, j, :], None, d["layer1"],
                                            bass.IndirectOffsetOnAxis(ap=stage[:, w, 4 + j:5 + j], axis=0)).then_inc(raw_in[w], 16)

            gather(0, 0)
            gather(1, 1)
            gather(2, 0)
            gather(3, 1)
            pool.wait_ge(ffn_hi, 1)
            for kk in range(KC):
                pool.tensor_tensor(s["f1"][:, 1, kk, :].rearrange("p (m h r) -> p m h r", h=EXPERTS, r=HR),
                                   w1raw[:, kk, :, :].rearrange("p h (m r) -> p m h r", r=HR),
                                   s["f1"][:, 0, kk, :].bitcast(F32).rearrange("p (m h r) -> p m h r", h=EXPERTS, r=HR),
                                   ALU.subtract)
            pool.tensor_tensor(s["f2"][:, 1, :, :], w2raw[:], s["f2"][:, 0, :, :].bitcast(F32), ALU.subtract).then_inc(ffn_lo, 1)
            with pool.Fori(2, EG // 2) as i:
                gather(2 * i, 0)
                gather(2 * i + 1, 1)

        @block.sync
        def _(sp):
            def mask_load(g, w):
                wait(sp, sem["ab"], g - 1)
                sp.dma_start(mask[:, w, :, :], d["masks"][:, bass.ds(g * GE, GE)].partition_broadcast(HEADS)).then_inc(mask_in[w], 16)

            mask_load(0, 0)
            mask_load(1, 1)
            sp.dma_start(bias[:], a["L0_gnn_b2"].partition_broadcast(P)).then_inc(bias_in, 16)
            sp.dma_start(d["layer2"][EP, :], a["L0_gnn_b2"]).then_inc(dflt, 16)
            for h in range(EXPERTS):
                sp.dma_start(w1raw[:, :, h, :], a["L0_ffn_w1"][h].rearrange("(k p) u -> p k u", p=P)).then_inc(ffn_in, 16)
                sp.dma_start(w2raw[h * HR:(h + 1) * HR, :, :],
                             a["L0_ffn_w2"][h].rearrange("(m r) n -> r m n", r=HR)).then_inc(ffn_in, 16)

            def body(g, w, nxt, chain):
                if chain:
                    mask_load(g + 2, w)
                for t in range(TG):
                    sp.wait_ge(row_out, 8 * g + 2 * t + 2)
                    sp.dma_start(d["layer2"][bass.ds(g * GE + t * P, P), :], rows[:, t % 2, :]).then_inc(st[t % 2], 16)

            groups(sp, body)
            for w in range(2):
                sp.wait_ge(st[w], 16 * 2 * EG)
            sp.wait_ge(dflt, 16)

        @block.scalar
        def _(act):
            def logit_copy(G):
                act.wait_ge(lg_done, G + 1)
                wait(act, sem["ab"], G)
                act.activation(b["e"][:], LG[0:HEADS, :], ACT.Copy).then_inc(sem["e_out"], 1)

            def exps(G):
                act.wait_ge(sem["x"], G + 1)
                act.activation(b["x"][:], b["x"][:], ACT.Exp).then_inc(sem["exp"], 1)

            def ab_copy(G):
                wait(act, agg_done, 6 * G)
                act.wait_ge(ab_ex, 2 * G + 2)
                act.activation(ab[:, 0, :], EX[:], ACT.Copy)
                act.activation(ab[:, 1, :], LG[:], ACT.Copy).then_inc(ab_out, 1)

            def high(G, W, kk):
                act.wait_ge(agg_done, 6 * G + kk + 1)
                wait(act, unit_done, 8 * G - 8)
                act.activation(xt[:, W, 0, kk, :], agg[:, kk % 2, :], ACT.Copy).then_inc(hi_out, 1)

            for G in range(2):
                logit_copy(G)
                exps(G)
                if G == 0:
                    ab_copy(0)
                    for kk in range(KC):
                        high(0, 0, kk)

            def body(g, w, nxt, chain):
                for u in range(8):
                    if nxt and u == 1:
                        ab_copy(g + 1)
                    if nxt and 2 <= u + 1 < 8 and u >= 1:
                        high(g + 1, 1 - w, u - 1)
                    if chain and u == 4:
                        logit_copy(g + 2)
                    if chain and u == 5:
                        exps(g + 2)
                if isinstance(g, int) and g == 0:
                    act.wait_ge(ffn_in, 16 * 2 * EXPERTS)
                    for kk in range(KC):
                        act.activation(s["f1"][:, 0, kk, :].rearrange("p (m h r) -> p m h r", h=EXPERTS, r=HR),
                                       w1raw[:, kk, :, :].rearrange("p h (m r) -> p m h r", r=HR), ACT.Copy)
                    act.activation(s["f2"][:, 0, :, :], w2raw[:], ACT.Copy).then_inc(ffn_hi, 1)

            groups(act, body)

        @block.vector
        def _(dve):
            def logit_columns(G, W):
                dve.wait_ge(raw_in[W], 64 * (G - W) + 128)
                wait(dve, lg_done, G - 1)
                dve.tensor_tensor(lcol[:, W, :, :], raw[:, W, :, D:D + 1].broadcast_to([P, TG, HEADS]),
                                  dlog[:, W, :].unsqueeze(2).broadcast_to([P, TG, HEADS]), ALU.add).then_inc(lcol_done, 1)

            def scan_chunk(G, kk):
                c = 6 * G + kk
                if kk == 0:
                    dve.wait_ge(ab_out, G + 1)
                dve.wait_ge(turned, c + 1)
                dve.tensor_tensor(msg[:, kk % 2, :], T[kk % 2][:], ab[:, 1, :], ALU.mult).then_inc(msg_done, 1)
                wait(dve, hi_out, c - 1)
                wait(dve, lo_out, c - 1)
                dve.wait_ge(msg_done, c + 1)
                dve.tensor_tensor_scan(agg[:, kk % 2, :], ab[:, 0, :], msg[:, kk % 2, :], carry[:, kk:kk + 1],
                                       ALU.mult, ALU.add).then_inc(agg_done, 1)
                dve.wait_ge(agg_done, c + 1)
                dve.tensor_copy(carry[:, kk:kk + 1], agg[:, kk % 2, GE - 1:GE]).then_inc(car, 1)

            def low(G, W, kk):
                dve.wait_ge(hi_out, 6 * G + kk + 1)
                dve.tensor_tensor(xt[:, W, 1, kk, :], agg[:, kk % 2, :], xt[:, W, 0, kk, :].bitcast(F32),
                                  ALU.subtract).then_inc(lo_out, 1)

            def add_bias(g, u):
                t, h = u // 2, u % 2
                dve.wait_ge(unit_done, 8 * g + u + 1)
                if h == 0:
                    wait(dve, st[t % 2], 16 * (2 * g + t // 2))
                dve.tensor_tensor(rows[:, t % 2, h * HALF:(h + 1) * HALF], ROW[u % 4][:, 0:HALF],
                                  bias[:, h * HALF:(h + 1) * HALF], ALU.add).then_inc(row_out, 1)

            def softmax(G, W):
                return softmax_steps(dve, b, sem, G, HEADS, mask[:, W, :, :], (mask_in[W], 8 * (G - W) + 16), (ab_ex, 2 * G))

            dve.wait_ge(init, 1)
            dve.wait_ge(bias_in, 16)
            for G in range(2):
                logit_columns(G, G)
                first_, second_ = softmax(G, G)
                first_()
                second_()
                if G == 0:
                    for kk in range(KC):
                        scan_chunk(0, kk)
                        low(0, 0, kk)

            def body(g, w, nxt, chain):
                for u in range(8):
                    if nxt and u >= 2:
                        low(g + 1, 1 - w, u - 2)
                    if nxt and 1 <= u < 7:
                        scan_chunk(g + 1, u - 1)
                    if u >= 1:
                        add_bias(g, u - 1)
                    if chain:
                        if u == 2:
                            logit_columns(g + 2, w)
                        if u == 4:
                            first_, second_ = softmax(g + 2, w)
                            first_()
                        if u == 6:
                            second_()
                add_bias(g, 7)

            groups(dve, body)

        @block.tensor
        def _(pe):
            def logits(G, W):
                pe.wait_ge(lcol_done, G + 1)
                wait(pe, ab_out, G)
                for t in range(TG):
                    mm = pe.transpose(LG[0:HEADS, t * P:(t + 1) * P], lcol[:, W, t, :], s["ident"][:])
                mm.then_inc(lg_done, 1)

            def spread(G):
                pe.wait_ge(sem["ab"], G + 1)
                pe.matmul(EX[:], s["headmap"][:], b["x"][:, 0, :], start=True, stop=True).then_inc(ab_ex, 1)
                pe.matmul(LG[:], s["headmap"][:], b["x"][:, 1, :], start=True, stop=True).then_inc(ab_ex, 1)

            def turn(G, W, kk):
                wait(pe, msg_done, 6 * G + kk - 1)
                for t in range(TG):
                    mm = pe.transpose(T[kk % 2][:, t * P:(t + 1) * P], raw[:, W, t, kk * P:(kk + 1) * P], s["ident"][:])
                mm.then_inc(turned, 1)

            def unit(g, w, u):
                t, h = u // 2, u % 2
                if u == 0:
                    pe.wait_ge(lo_out, 6 * g + 6)
                wait(pe, row_out, 8 * g + u - 3)
                for kk in range(KC):
                    for i, (x, y) in enumerate(((0, 0), (1, 0), (0, 1))):
                        mm = pe.matmul(ROW[u % 4][:, 0:HALF], xt[:, w, x, kk, t * P:(t + 1) * P],
                                       s["w2s"][:, y, kk, h * HALF:(h + 1) * HALF], start=kk == 0 and i == 0,
                                       stop=kk == KC - 1 and i == 2)
                mm.then_inc(unit_done, 1)

            logits(0, 0)
            spread(0)
            for kk in range(KC):
                turn(0, 0, kk)
            logits(1, 1)

            def body(g, w, nxt, chain):
                for u in range(8):
                    unit(g, w, u)
                    if nxt and u == 0:
                        spread(g + 1)
                    if nxt and u < 6:
                        turn(g + 1, 1 - w, u)
                    if chain and u == 3:
                        logits(g + 2, w)

            groups(pe, body)


def moe_ffn(nc, a, d, s, out):
    with ExitStack() as ctx:
        k = Kit(nc, ctx, "f_")
        xt = k.sb("xt", [P, 2, 2, KC, GE], F32R)
        x1 = k.sb("x1", [P, 2, TG, D])
        raw = k.sb("raw", [P, TG, D])
        hid = k.sb("hid", [P, FC, GE])
        hs = k.sb("hs", [P, 2, FC, GE], F32R)
        stage = k.sb("stage", [P, 2, TG], I32)
        stats = k.sb("stats", [P, 2, 2, 2, 6])
        mv = k.sb("mv", [P, 2, 2, 2])
        rstd = k.sb("rstd", [P, 2, 2])
        nmr = k.sb("nmr", [P, 2, 2])
        ln_const = k.sb("ln_const", [P, 6])
        b1 = k.sb("b1", [P, FC])
        graw = k.sb("graw", [P, KC, EXPERTS])
        gate = k.sb("gate", [P, KC, 2, EXPERTS], F32R)
        sel = k.sb("sel", [2 * EXPERTS, EXPERTS])
        b2raw = k.sb("b2raw", [96, D])
        b2s = k.sb("b2s", [96, D], F32R)
        spread_f = k.sb("spread_f", [96, P])
        spread_w = k.sb("spread_w", [96, P], F32R)
        cpad = k.sb("cpad", [P, TG, 96])
        ct = k.sb("ct", [96, GE], F32R)
        lg16 = k.sb("lg16", [2 * EXPERTS, GE])
        lg = k.sb("lg", [P, TG, EXPERTS])
        top = k.sb("top", [P, TG, 8])
        top_i = k.sb("top_i", [P, TG, 8], mybir.dt.uint32)
        top_f = k.sb("top_f", [P, TG, 2])
        iota_i = k.sb("iota_i", [P, EXPERTS], I32)
        iota_f = k.sb("iota_f", [P, EXPERTS])
        gap = k.sb("gap", [P, TG])
        wgt = k.sb("wgt", [P, 2, TG])
        onehot = k.sb("onehot", [P, 2, TG, EXPERTS])
        comb = k.sb("comb", [P, TG, EXPERTS])
        comb_hi = k.sb("comb_hi", [P, TG, EXPERTS], F32R)
        T = [k.ps("p_t0"), k.ps("p_t1")]
        H = [k.ps("p_h0"), k.ps("p_h1")]
        R = k.ps("p_r")
        ROW = [k.ps(f"p_row{i}") for i in range(3)]
        raw_in, st = k.sems("s_raw", TG), k.sems("s_st", TG)
        x_in = [k.sems(f"s_x{w}_", TG) for w in range(2)]
        (passed_p, passed_v, staged, init, added, stat, mvr, vv, pw, ln, normed, turned, hi_out, lo_out, router_done, lg16_out,
         sums_done, dv, gap_done, tanh_done, comb_done, ct_done, ct_out, ce_done, h_done, gelu_done, scaled, hhi, hlo,
         unit_done, row_out, small_in, consts) = [
            k.sem("s_" + n) for n in ("passed_p", "passed_v", "staged", "init", "added", "stat", "mvr", "vv", "pw", "ln", "normed", "turned",
                                      "hi", "lo", "router", "lg16", "sums", "dv", "gap", "tanh", "comb", "ct", "ct_out",
                                      "ce", "h", "gelu", "scaled", "hhi", "hlo", "unit", "row", "small", "consts")]
        block = k.block()

        def groups(eng, body):
            body(0, 0, True, False)
            with eng.Fori(0, (NG - 2) // 2) as i:
                body(2 * i + 1, 1, False, False)
                body(2 * i + 2, 0, False, False)
            body(NG - 1, (NG - 1) % 2, False, True)

        def rows_of(g, t):
            if isinstance(g, int) and g == NG - 1:
                return bass.ds(N - GE + t * P, P)
            return bass.ds(g * GE + t * P, P)

        @block.sync
        def _(sp):
            def load(G, W, t):
                sp.dma_start(x1[:, W, t, :], a["x"][rows_of(G, t), :]).then_inc(x_in[W][t], 16)

            for t in range(TG):
                load(0, 0, t)
            sp.wait_ge(consts, 1)
            sp.dma_start(graw[:], a["L0_ffn_gate_w"].rearrange("(k p) e -> p k e", p=P)).then_inc(small_in, 16)
            for h in range(EXPERTS):
                sp.dma_start(b1[h * HR:(h + 1) * HR, :], a["L0_ffn_b1"][h, 0, :].rearrange("(m r) -> r m", r=HR),
                             allow_slow_non_contiguous=True).then_inc(small_in, 16)
            for n in range(3):
                sp.dma_start(b2raw[32 * n:32 * n + EXPERTS, :], a["L0_ffn_b2"][:, 0, :]).then_inc(small_in, 16)
            for n in (0, 2):
                sp.dma_start(spread_f[32 * n:32 * n + EXPERTS, :], s["headmap"][:]).then_inc(small_in, 16)
            for t in range(TG):
                load(1, 1, t)

            def body(g, w, first, last):
                if last:
                    for t in range(TG):
                        sp.wait_ge(st[t], 16 * (NG - 1))
                for t in range(TG):
                    sp.wait_ge(row_out, 8 * g + 2 * t + 2)
                    sp.dma_start(out[rows_of(g, t), :], x1[:, w, t, :]).then_inc(st[t], 16)
                    if t >= 1 and not last:
                        again(g, w, t - 1)
                if not last:
                    again(g, w, TG - 1)

            def again(g, w, t):
                sp.wait_ge(st[t], 16 * g + 16)
                load(g + 2, w, t)

            body(0, 0, True, False)
            with sp.Fori(0, (NG - 4) // 2) as i:
                body(2 * i + 1, 1, False, False)
                body(2 * i + 2, 0, False, False)
            g = NG - 3
            for t in range(TG):
                sp.wait_ge(row_out, 8 * g + 2 * t + 2)
                sp.dma_start(out[rows_of(g, t), :], x1[:, g % 2, t, :]).then_inc(st[t], 16)
                sp.wait_ge(st[t], 16 * g + 16)
                load(NG - 1, g % 2, t)
            g = NG - 2
            for t in range(TG):
                sp.wait_ge(row_out, 8 * g + 2 * t + 2)
                sp.dma_start(out[rows_of(g, t), :], x1[:, g % 2, t, :]).then_inc(st[t], 16)
            body(NG - 1, (NG - 1) % 2, False, True)
            for t in range(TG):
                sp.wait_ge(st[t], 16 * NG)

        @block.gpsimd
        def _(pool):
            pool.memset(b2raw[:], 0.0)
            pool.memset(spread_f[:], 0.0)
            for n, v in enumerate((-0.5, EPS, -1.0)):
                pool.memset(ln_const[:, 2 * n:2 * n + 2], v)
            pool.memset(cpad[:], 0.0)
            pool.iota(iota_i[:], [[1, EXPERTS]], base=0, channel_multiplier=0)
            pool.memset(sel[:], 0.0).then_inc(consts, 1)
            pool.wait_ge(consts, 1)
            pool.affine_select(out=sel[:], in_=sel[:], compare_op=ALU.not_equal, fill=1.0, base=0,
                               pattern=[[-1, EXPERTS]], channel_multiplier=1).then_inc(init, 1)
            pool.wait_ge(init, 1)
            pool.affine_select(out=sel[:], in_=sel[:], compare_op=ALU.not_equal, fill=1.0, base=-EXPERTS,
                               pattern=[[-1, EXPERTS]], channel_multiplier=1).then_inc(init, 1)

            def group(G, W):
                wait(pool, ln, 2 * G)
                pool.tensor_copy(stage[:, W, :], s["pnode"][:, bass.ds(TG * G, TG)]).then_inc(staged, 1)
                for t in range(TG):
                    wait(pool, turned, 8 * G - 8 + 2 * t + 2)
                    carried_wait(pool, passed_p, staged, G + 1)
                    pool.indirect_dma_start(raw[:, t, :], None, d["layer2"],
                                            bass.IndirectOffsetOnAxis(ap=stage[:, W, t:t + 1], axis=0)).then_inc(raw_in[t], 16)
                for u in range(2):
                    r = 2 * G + u
                    for t in (2 * u, 2 * u + 1):
                        pool.wait_ge(raw_in[t], 16 * G + 16)
                        pool.wait_ge(x_in[W][t], 8 * (G - W) + 16)
                        pool.tensor_tensor(x1[:, W, t, :], x1[:, W, t, :], raw[:, t, :], ALU.add).then_inc(added, 1)
                    pool.wait_ge(mvr, r + 1)
                    pool.tensor_tensor(rstd[:, u, :], mv[:, u, :, 1], ln_const[:, 2:4], ALU.add)
                    pool.tensor_tensor(nmr[:, u, :], mv[:, u, :, 0], ln_const[:, 4:6], ALU.mult).then_inc(vv, 1)
                    pool.wait_ge(vv, r + 1)
                    pool.tensor_tensor(rstd[:, u, :], rstd[:, u, :], ln_const[:, 0:2], ALU.pow).then_inc(pw, 1)
                    pool.wait_ge(pw, r + 1)
                    pool.tensor_tensor(nmr[:, u, :], nmr[:, u, :], rstd[:, u, :], ALU.mult).then_inc(ln, 1)

            group(0, 0)
            group(1, 1)
            with pool.Fori(1, NG // 2) as i:
                group(2 * i, 0)
                group(2 * i + 1, 1)

        @block.scalar
        def _(act):
            def normalise(G, W, t):
                act.wait_ge(ln, 2 * G + t // 2 + 1)
                act.activation(raw[:, t, :], x1[:, W, t, :], ACT.Identity, bias=nmr[:, t // 2, t % 2:t % 2 + 1],
                               scale=rstd[:, t // 2, t % 2:t % 2 + 1]).then_inc(normed, 1)

            def high(G, W, h):
                act.wait_ge(turned, 8 * G + h + 1)
                wait(act, h_done, 3 * G - 3)
                act.activation(xt[:, W, 0, 3 * (h % 2):3 * (h % 2) + 3, (h // 2) * P:(h // 2 + 1) * P],
                               T[h % 2][:, 0:3 * P].rearrange("p (k j) -> p k j", k=3), ACT.Copy).then_inc(hi_out, 1)

            def router_copy(G):
                act.wait_ge(router_done, G + 1)
                act.activation(lg16[:], R[0:2 * EXPERTS, :], ACT.Copy).then_inc(lg16_out, 1)

            def tanh(g):
                act.wait_ge(gap_done, g + 1)
                act.activation(gap[:], gap[:], ACT.Tanh, scale=0.5).then_inc(tanh_done, 1)

            def weights_copy(g):
                act.wait_ge(ct_done, g + 1)
                wait(act, unit_done, 8 * g)
                act.activation(ct[:], R[0:96, :], ACT.Copy).then_inc(ct_out, 1)

            def gelu(g, w, m):
                c = 3 * g + m
                act.wait_ge(h_done, c + 1)
                wait(act, hlo, 3 * g)
                act.activation(hid[:, m, :], H[(w + m) % 2][:], ACT.Gelu, bias=b1[:, m:m + 1]).then_inc(gelu_done, 1)

            def hidden_high(g, m):
                act.wait_ge(scaled, 3 * g + m + 1)
                wait(act, unit_done, 8 * g)
                act.activation(hs[:, 0, m, :], hid[:, m, :], ACT.Copy).then_inc(hhi, 1)

            act.wait_ge(small_in, 16 * 14)
            act.activation(gate[:, :, 0, :], graw[:], ACT.Copy)
            act.activation(b2s[:], b2raw[:], ACT.Copy)
            act.activation(spread_w[:], spread_f[:], ACT.Copy).then_inc(consts, 1)
            for t in range(TG):
                normalise(0, 0, t)
                high(0, 0, 2 * t)
                high(0, 0, 2 * t + 1)

            def body(g, w, first, last):
                router_copy(g)
                if not last:
                    normalise(g + 1, 1 - w, 0)
                tanh(g)
                gelu(g, w, 0)
                if not last:
                    high(g + 1, 1 - w, 0)
                    normalise(g + 1, 1 - w, 1)
                weights_copy(g)
                gelu(g, w, 1)
                hidden_high(g, 0)
                hidden_high(g, 1)
                gelu(g, w, 2)
                if not last:
                    high(g + 1, 1 - w, 1)
                hidden_high(g, 2)
                if not last:
                    high(g + 1, 1 - w, 2)
                    for t in (2, 3):
                        normalise(g + 1, 1 - w, t)
                    for h in range(3, 8):
                        high(g + 1, 1 - w, h)

            groups(act, body)

        @block.vector
        def _(dve):
            def moments(G, W, u):
                r = 2 * G + u
                wait(dve, normed, 4 * G - 4 + 2 * u + 2)
                for n in range(2):
                    t = 2 * u + n
                    dve.wait_ge(added, 4 * G + t + 1)
                    for h in range(2):
                        ins = dve.bn_stats(stats[:, u, n, h, :], x1[:, W, t, h * HALF:(h + 1) * HALF])
                ins.then_inc(stat, 1)
                carried_wait(dve, passed_v, stat, r + 1)
                dve.bn_aggr(mv[:, u, 0, :], stats[:, u, 0, :, :])
                dve.bn_aggr(mv[:, u, 1, :], stats[:, u, 1, :, :]).then_inc(mvr, 1)

            def low(G, W, h):
                dve.wait_ge(hi_out, 8 * G + h + 1)
                v = xt[:, W, :, 3 * (h % 2):3 * (h % 2) + 3, (h // 2) * P:(h // 2 + 1) * P]
                dve.tensor_tensor(v[:, 1], T[h % 2][:, 0:3 * P].rearrange("p (k j) -> p k j", k=3), v[:, 0].bitcast(F32),
                                  ALU.subtract).then_inc(lo_out, 1)

            DV = 8

            def best_two(g):
                n = [DV * g]

                def step(ins):
                    n[0] = n[0] + 1
                    ins.then_inc(dv, 1)
                    dve.wait_ge(dv, n[0])

                dve.wait_ge(sums_done, g + 1)
                step(dve.tensor_copy(lg[:], R[:, 0:TG * EXPERTS].rearrange("p (t e) -> p t e", e=EXPERTS)))
                dve.sem_inc(passed_v, 1)
                for t in range(TG):
                    ins = dve.max(top[:, t, :], lg[:, t, :])
                step(ins)
                dve.tensor_tensor(gap[:], top[:, :, 0], top[:, :, 1], ALU.subtract).then_inc(gap_done, 1)
                for t in range(TG):
                    ins = dve.max_index(top_i[:, t, :], top[:, t, :], lg[:, t, :])
                step(ins)
                step(dve.tensor_copy(top_f[:], top_i[:, :, 0:2]))
                for j in range(2):
                    ins = dve.tensor_tensor(onehot[:, j, :, :], iota_f[:].unsqueeze(1).broadcast_to([P, TG, EXPERTS]),
                                            top_f[:, :, j:j + 1].broadcast_to([P, TG, EXPERTS]), ALU.is_equal)
                step(ins)

            def combine(g):
                n = [DV * g + 5]

                def step(ins):
                    n[0] = n[0] + 1
                    ins.then_inc(dv, 1)
                    dve.wait_ge(dv, n[0])

                dve.wait_ge(tanh_done, g + 1)
                dve.tensor_scalar(wgt[:, 0, :], gap[:], 0.5, 0.5, ALU.mult, ALU.add)
                step(dve.tensor_scalar(wgt[:, 1, :], gap[:], -0.5, 0.5, ALU.mult, ALU.add))
                step(dve.tensor_tensor(onehot[:], onehot[:], wgt[:].unsqueeze(3).broadcast_to([P, 2, TG, EXPERTS]), ALU.mult))
                step(dve.tensor_tensor(comb[:], onehot[:, 0], onehot[:, 1], ALU.add))
                dve.tensor_copy(comb_hi[:], comb[:]).then_inc(comb_done, 1)
                dve.wait_ge(comb_done, 3 * g + 1)
                dve.tensor_copy(cpad[:, :, 0:2 * 32].rearrange("p t (n e) -> p t n e", n=2)[:, :, :, 0:EXPERTS],
                                comb_hi[:].bitcast(F32).unsqueeze(2).broadcast_to([P, TG, 2, EXPERTS])).then_inc(comb_done, 1)
                dve.tensor_tensor(cpad[:, :, 64:64 + EXPERTS], comb[:], comb_hi[:].bitcast(F32), ALU.subtract).then_inc(comb_done, 1)

            def scale(g, m):
                dve.wait_ge(ce_done, g + 1)
                dve.wait_ge(gelu_done, 3 * g + m + 1)
                dve.tensor_tensor(hid[:, m, :], hid[:, m, :], R[:], ALU.mult).then_inc(scaled, 1)

            def hidden_low(g, m):
                dve.wait_ge(hhi, 3 * g + m + 1)
                dve.tensor_tensor(hs[:, 1, m, :], hid[:, m, :], hs[:, 0, m, :].bitcast(F32), ALU.subtract).then_inc(hlo, 1)

            def residual(g, w, u):
                t, h = u // 2, u % 2
                dve.wait_ge(unit_done, 8 * g + u + 1)
                v = x1[:, w, t, h * HALF:(h + 1) * HALF]
                dve.tensor_tensor(v, ROW[u % 3][:, 0:HALF], v, ALU.add).then_inc(row_out, 1)

            dve.wait_ge(consts, 2)
            dve.tensor_tensor(gate[:, :, 1, :], graw[:], gate[:, :, 0, :].bitcast(F32), ALU.subtract)
            dve.tensor_copy(iota_f[:], iota_i[:])
            dve.tensor_tensor(b2s[32:32 + EXPERTS, :], b2raw[32:32 + EXPERTS, :], b2s[32:32 + EXPERTS, :].bitcast(F32),
                              ALU.subtract).then_inc(consts, 1)
            dve.wait_ge(consts, 3)
            for u in range(2):
                moments(0, 0, u)
            for h in range(8):
                low(0, 0, h)

            def body(g, w, first, last):
                best_two(g)
                if not last:
                    moments(g + 1, 1 - w, 0)
                combine(g)
                if not last:
                    low(g + 1, 1 - w, 0)
                    moments(g + 1, 1 - w, 1)
                scale(g, 0)
                scale(g, 1)
                hidden_low(g, 0)
                hidden_low(g, 1)
                scale(g, 2)
                if not last:
                    low(g + 1, 1 - w, 1)
                hidden_low(g, 2)
                if not last:
                    low(g + 1, 1 - w, 2)
                for u in range(8):
                    if not last and u < 5:
                        low(g + 1, 1 - w, 3 + u)
                    residual(g, w, u)

            groups(dve, body)

        @block.tensor
        def _(pe):
            def turn(G, h):
                t = h // 2
                pe.wait_ge(normed, 4 * G + t + 1)
                wait(pe, lo_out, 8 * G + h - 1)
                for kk in range(3):
                    mm = pe.transpose(T[h % 2][:, kk * P:(kk + 1) * P],
                                      raw[:, t, (3 * (h % 2) + kk) * P:(3 * (h % 2) + kk + 1) * P], s["ident"][:])
                mm.then_inc(turned, 1)

            def router(G, W):
                pe.wait_ge(lo_out, 8 * G + 8)
                wait(pe, scaled, 3 * G)
                for kk in range(KC):
                    pe.matmul(R[0:2 * EXPERTS, :], gate[:, kk, :, :].rearrange("p n e -> p (n e)"), xt[:, W, 0, kk, :],
                              start=kk == 0, stop=False, skip_group_check=True)
                    mm = pe.matmul(R[0:EXPERTS, :], gate[:, kk, 0, :], xt[:, W, 1, kk, :], start=False,
                                   stop=kk == KC - 1, skip_group_check=True)
                mm.then_inc(router_done, 1)

            def sums(g):
                pe.wait_ge(lg16_out, g + 1)
                for t in range(TG):
                    mm = pe.matmul(R[:, t * EXPERTS:(t + 1) * EXPERTS], lg16[:, t * P:(t + 1) * P], sel[:],
                                   start=True, stop=True, skip_group_check=True)
                mm.then_inc(sums_done, 1)

            def weights_turn(g):
                pe.wait_ge(comb_done, 3 * g + 3)
                for t in range(TG):
                    mm = pe.transpose(R[0:96, t * P:(t + 1) * P], cpad[:, t, :], s["ident"][:])
                mm.then_inc(ct_done, 1)

            def weights_spread(g):
                pe.wait_ge(ct_out, g + 1)
                pe.matmul(R[:], spread_w[:], ct[:], start=True, stop=True).then_inc(ce_done, 1)

            def hidden(g, w, m, part):
                if part == 0:
                    wait(pe, gelu_done, 3 * g + m - 1)
                for kk in (range(0, 3), range(3, KC))[part]:
                    for i, (x, y) in enumerate(((0, 0), (1, 0), (0, 1))):
                        mm = pe.matmul(H[(w + m) % 2][:], s["f1"][:, x, kk, m * P:(m + 1) * P], xt[:, w, y, kk, :],
                                       start=kk == 0 and i == 0, stop=kk == KC - 1 and i == 2, skip_group_check=True)
                if part == 1:
                    mm.then_inc(h_done, 1)

            def unit(g, u):
                t, h = u // 2, u % 2
                wait(pe, row_out, 8 * g + (u - 2 if u >= 3 else (-1, 0, 0)[u]))
                cols = slice(h * HALF, (h + 1) * HALF)
                pe.matmul(ROW[u % 3][:, 0:HALF], ct[:, t * P:(t + 1) * P], b2s[:, cols], start=True, stop=False)
                for m in range(FC):
                    if u == 0:
                        pe.wait_ge(hlo, 3 * g + m + 1)
                    for i, (x, y) in enumerate(((0, 0), (1, 0), (0, 1))):
                        mm = pe.matmul(ROW[u % 3][:, 0:HALF], hs[:, x, m, t * P:(t + 1) * P], s["f2"][:, y, m, cols],
                                       start=False, stop=m == FC - 1 and i == 2)
                mm.then_inc(unit_done, 1)

            pe.wait_ge(consts, 3)
            pe.wait_ge(init, 2)
            for h in range(8):
                turn(0, h)
            router(0, 0)

            def body(g, w, first, last):
                hidden(g, w, 0, 0)
                sums(g)
                hidden(g, w, 0, 1)
                hidden(g, w, 1, 0)
                if not last:
                    turn(g + 1, 0)
                hidden(g, w, 1, 1)
                weights_turn(g)
                hidden(g, w, 2, 0)
                weights_spread(g)
                hidden(g, w, 2, 1)
                if not last:
                    turn(g + 1, 1)
                    turn(g + 1, 2)
                for u in range(8):
                    unit(g, u)
                    if not last and u < 5:
                        turn(g + 1, 3 + u)
                if not last:
                    router(g + 1, 1 - w)

            groups(pe, body)


def build(nc, *arrays):
    names = _INS
    a = dict(zip(names, arrays))
    out = arrays[len(names)]
    d = {
        "sorted_dst": nc.dram_tensor("sorted_dst", (EP + 2, 1), F32, kind="Internal").ap(),
        "masks": nc.dram_tensor("edge_masks", (2, EP), F32, kind="Internal").ap(),
        "node_pos": nc.dram_tensor("node_pos", (10240, 1), I32, kind="Internal").ap(),
        "layer1": nc.dram_tensor("layer1", (EP + 1, RW), F32, kind="Internal").ap(),
        "dst_logit": nc.dram_tensor("dst_logit", (EP + 1, 1), F32, kind="Internal").ap(),
        "layer2": nc.dram_tensor("layer2", (EP + 1, D), F32, kind="Internal").ap(),
    }
    with ExitStack() as ctx:
        s = persistent(Kit(nc, ctx))
        order_edges(nc, a, d, s)
        gat_layer_1(nc, a, d, s)
        gat_layer_2(nc, a, d, s)
        moe_ffn(nc, a, d, s, out)


_INS = ["x", "src", "dst", "L0_gnn_W1", "L0_gnn_a_src1", "L0_gnn_a_dst1", "L0_gnn_b1", "L0_gnn_W2", "L0_gnn_a_src2",
        "L0_gnn_a_dst2", "L0_gnn_b2", "L0_ffn_gate_w", "L0_ffn_w1", "L0_ffn_b1", "L0_ffn_w2", "L0_ffn_b2"]
_OUTS = [((N, D), "float32")]


def kernel(**inputs):
    import numpy as _np
    import concourse.bacc as _bacc
    from concourse import mybir as _mybir
    from concourse.bass_utils import run_bass_kernel_spmd as _run

    nc = _bacc.Bacc("TRN2", target_bir_lowering=False, num_devices=1)
    arrays, args = {}, []
    for name in _INS:
        arr = _np.ascontiguousarray(inputs[name])
        arrays[f"in_{name}_dram"] = arr
        args.append(nc.dram_tensor(f"in_{name}_dram", arr.shape, _mybir.dt.from_np(arr.dtype), kind="ExternalInput").ap())
    for i, (shape, dtype) in enumerate(_OUTS):
        dt = _mybir.dt.from_np(_np.dtype(dtype))
        args.append(nc.dram_tensor(f"out_{i}_dram", shape, dt, kind="ExternalOutput").ap())
    build(nc, *args)
    r = _run(nc, [arrays], core_ids=[0])
    return r.results[0]["out_0_dram"]
```

```python
from contextlib import ExitStack

import concourse.bass as bass
from concourse import mybir

ALU = mybir.AluOpType
ACT = mybir.ActivationFunctionType
AX = mybir.AxisListType
F32 = mybir.dt.float32
F32R = mybir.dt.float32r
BF16 = mybir.dt.bfloat16
I32 = mybir.dt.int32

P = 128
N, D = 10000, 768
E = 5000
KC = D // P
HEADS, HC = 8, 96
HR = P // HEADS
GE = 512
TG = GE // P
ET = -(-E // P)
EP = ET * P
EG = EP // GE
NG = -(-N // GE)
EXPERTS, HID = 8, 48
FH = EXPERTS * HID
FC = FH // P
HALF = D // 2
RW = D + 1
SLOPE = 0.2
EPS = 1e-5
BIG = 3e38
assert EP % GE == 0 and FH % P == 0 and EXPERTS == HEADS and KC * HR == HC and FC * HR == HID


def wait(eng, sem, value):
    if isinstance(value, int) and value <= 0:
        return
    eng.wait_ge(sem, value)


def carried_wait(eng, passed, sem, value):
    eng.wait_ge(sem, value)
    eng.sem_inc(passed, 1)


class Kit:

    def __init__(self, nc, ctx, phase=""):
        self.nc, self.ctx, self.phase, self.made = nc, ctx, phase, []

    def sb(self, name, shape, dt=F32):
        return self.ctx.enter_context(self.nc.sbuf_tensor(self.phase + name, shape, dt))

    def ps(self, name, shape=(P, 512), dt=F32):
        return self.ctx.enter_context(self.nc.psum_tensor(self.phase + name, list(shape), dt))

    def sem(self, name):
        self.made.append(self.ctx.enter_context(self.nc.semaphore(self.phase + name)))
        return self.made[-1]

    def block(self, clear=False):
        if clear:
            self.ctx.callback(self.clear)
        return self.ctx.enter_context(self.nc.Block())

    def clear(self):
        with self.nc.Block() as block:
            @block.gpsimd
            def _(pool):
                for sem in self.made:
                    pool.sem_clear(sem)

    def sems(self, name, n):
        return [self.sem(f"{name}{i}") for i in range(n)]


def persistent(k):
    s = {}
    s["ident"] = k.sb("ident", [P, P])
    s["gidx"] = k.sb("gidx", [P, EG * 8], I32)
    s["pos"] = k.sb("pos", [P, EG * 8], I32)
    s["pnode"] = k.sb("pnode", [P, NG * TG], I32)
    s["v1"] = k.sb("v1", [P, 2, 2, KC, HEADS], F32R)
    s["v2"] = k.sb("v2", [P, KC, 2])
    s["b1col"] = k.sb("b1col", [P, KC])
    s["headmap"] = k.sb("headmap", [HEADS, P])
    s["w1s"] = k.sb("w1s", [P, 2, KC, D], F32R)
    return s


def experts_weights(s):
    s["f1"] = s["w1s"][:, 0].rearrange("p k (a n) -> p a k n", a=2)
    s["f2"] = s["w1s"][:, 1].rearrange("p (a k) n -> p a k n", a=2)


def order_edges(nc, a, d, s):
    with ExitStack() as ctx:
        k = Kit(nc, ctx, "o_")
        key = k.sb("key", [P, EP])
        with nc.sbuf_tensor("junk_v", [P, EP], BF16) as junk_v, nc.sbuf_tensor("junk_a", [P, EP], BF16) as junk_a:
            pass
        oh_lo = k.sb("oh_lo", [P, ET, P], BF16)
        oh_hi = k.sb("oh_hi", [P, ET, 4, ET], BF16)
        wraw = k.sb("wraw", [P, KC, D])
        w2raw = k.sb("w2raw", [P, KC, D])
        prod = k.sb("prod", [P, KC, D])
        avec = k.sb("avec", [P, 4, D])
        col_i = k.sb("col_i", [P, 2, ET], I32)
        dst_f = k.sb("dst_f", [P, ET])
        frac_i = k.sb("frac_i", [P, P], I32)
        frac = k.sb("frac", [P, P])
        iota_f = k.sb("iota_f", [P, P])
        rowp_i = k.sb("rowp_i", [P, 1], I32)
        rowp = k.sb("rowp", [P, 1])
        thr = k.sb("thr", [P, 3, ET])
        nthr = k.sb("nthr", [P, 3, ET])
        less = k.sb("less", [P, 3, ET])
        rank = k.sb("rank", [P, 4, ET])
        rank_i = k.sb("rank_i", [P, 3, ET], I32)
        part_i = k.sb("part_i", [P, 4, ET], I32)
        part_f = k.sb("part_f", [P, 4, ET])
        hl_f = k.sb("hl_f", [P, 2, ET])
        ohr = k.sb("ohr", [P, ET, ET])
        sorted4 = k.sb("sorted4", [P, 4, ET])
        col_f = k.sb("col_f", [P, 2, ET])
        clip_f = k.sb("clip_f", [P, ET])
        dst_row = k.sb("dst_row", [ET, P])
        window = k.sb("window", [ET, P + 2])
        eq = k.sb("eq", [ET, 2, P])
        masks = k.sb("masks", [ET, 2, P])
        end_row = k.sb("end_row", [ET, P])
        end_i = k.sb("end_i", [P, ET], I32)
        place_i = k.sb("place_i", [P, ET], I32)
        none_i = k.sb("none_i", [P, 80], I32)
        edge_f = k.sb("edge_f", [1, 2])
        v_f = k.sb("v_f", [P, 2, KC, HEADS])
        p_sort = k.ps("p_sort")
        p_row = k.ps("p_row")
        p_end = k.ps("p_end")
        (s_scat, s_key, s_col, s_w1, s_av, s_w2, s_b, s_none, s_iota, s_prep, s_cnt_v, s_cnt_a, s_dve, s_oh, s_sorted,
         s_row, s_rowst, s_win, s_maskst, s_endT, s_endi, s_pn, s_prod, s_red, s_split, s_id, s_vec,
         s_colr, s_hm) = [k.sem(f"s_o{i}") for i in range(29)]
        ACT_TILES = range(24, ET)
        block = k.block(clear=True)

        src_d, dst_d = a["src"], a["dst"]
        full = (E // P) * P

        @block.sync
        def _(sp):
            sp.dma_start(key[:, 0:E].bitcast(I32), dst_d.partition_broadcast(P)).then_inc(s_key, 16)
            sp.wait_ge(s_prep, 1)
            for n, v in enumerate((src_d, dst_d)):
                sp.dma_start(col_i[:, n, 0:E // P], v[0:full].rearrange("(t p) -> p t", p=P), allow_slow_non_contiguous=True).then_inc(s_col, 16)
                sp.dma_start(col_i[0:E - full, n, E // P:ET],
                             v[full:E].rearrange("(p o) -> p o", o=1), allow_slow_non_contiguous=True).then_inc(s_col, 16)
            sp.dma_start(wraw[:], a["L0_gnn_W1"].rearrange("(k p) n -> p k n", p=P)).then_inc(s_w1, 16)
            for n, name in enumerate(("a_src1", "a_dst1", "a_src2", "a_dst2")):
                sp.dma_start(avec[:, n, :], a["L0_gnn_" + name].rearrange("h c -> (h c)").partition_broadcast(P)).then_inc(s_av, 16)
            for h in range(HEADS):
                sp.dma_start(w2raw[h * HR:(h + 1) * HR, :, :],
                             a["L0_gnn_W2"][h * HC:(h + 1) * HC, :].rearrange("(m r) n -> r m n", r=HR)).then_inc(s_w2, 16)
                sp.dma_start(s["b1col"][h * HR:(h + 1) * HR, :],
                             a["L0_gnn_b1"][h * HC:(h + 1) * HC].rearrange("(m r) -> r m", r=HR), allow_slow_non_contiguous=True).then_inc(s_b, 16)
            sp.wait_ge(s_none, 2)
            sp.dma_start(d["node_pos"][0:10240, :].rearrange("(p n) o -> p (n o)", p=P), none_i[:]).then_inc(s_none, 16)
            sp.dma_start(d["sorted_dst"][0:1, :], edge_f[0:1, 0:1]).then_inc(s_rowst, 16)
            sp.dma_start(d["sorted_dst"][EP + 1:EP + 2, :], edge_f[0:1, 1:2]).then_inc(s_rowst, 16)
            sp.wait_ge(s_row, 2)
            sp.dma_start(d["sorted_dst"][1:EP + 1, :].rearrange("(t j) o -> t (j o)", j=P), dst_row[:]).then_inc(s_rowst, 16)
            sp.wait_ge(s_rowst, 48)
            sp.dma_start(window[:], bass.AP(d["sorted_dst"].tensor, 0, [[P, ET], [1, P + 2]])).then_inc(s_win, 16)
            sp.wait_ge(s_maskst, 1)
            for n in range(2):
                sp.dma_start(d["masks"][n, :].rearrange("(t j) -> t j", j=P), masks[:, n, :]).then_inc(s_maskst, 16)
            sp.wait_ge(s_scat, 16 * ET)
            last = N - (NG - 1) * GE
            sp.dma_start(s["pnode"][:, 0:(NG - 1) * TG],
                         d["node_pos"][0:(NG - 1) * GE, :].rearrange("(t p) o -> p (t o)", p=P), allow_slow_non_contiguous=True).then_inc(s_pn, 16)
            sp.dma_start(s["pnode"][:, (NG - 1) * TG:NG * TG],
                         d["node_pos"][N - GE:N, :].rearrange("(t p) o -> p (t o)", p=P), allow_slow_non_contiguous=True).then_inc(s_pn, 16)
            sp.wait_ge(s_pn, 32)
            sp.wait_ge(s_maskst, 33)
            sp.wait_ge(s_b, 16 * HEADS)

        @block.gpsimd
        def _(pool):
            pool.memset(col_i[:, 0, ET - 1:ET], 0)
            pool.memset(col_i[:, 1, ET - 1:ET], N).then_inc(s_prep, 1)
            pool.iota(frac_i[:], [[1, P]], base=0, channel_multiplier=0)
            pool.iota(rowp_i[:], [[1, 1]], base=0, channel_multiplier=1)
            pool.iota(place_i[:], [[P, ET]], base=0, channel_multiplier=1).then_inc(s_iota, 1)
            pool.memset(none_i[:], EP).then_inc(s_none, 1)
            pool.memset(edge_f[:], -1.0).then_inc(s_none, 1)
            pool.memset(s["ident"][:], 0.0).then_inc(s_id, 1)
            pool.wait_ge(s_id, 1)
            pool.affine_select(out=s["ident"][:], in_=s["ident"][:], compare_op=ALU.not_equal, fill=1.0, base=0,
                               pattern=[[-1, P]], channel_multiplier=1).then_inc(s_id, 1)
            pool.memset(s["headmap"][:], 1.0).then_inc(s_hm, 1)
            pool.wait_ge(s_hm, 1)
            pool.affine_select(out=s["headmap"][:], in_=s["headmap"][:], compare_op=ALU.is_ge, fill=0.0, base=0,
                               pattern=[[1, P]], channel_multiplier=-HR).then_inc(s_hm, 1)
            pool.wait_ge(s_hm, 2)
            pool.affine_select(out=s["headmap"][:], in_=s["headmap"][:], compare_op=ALU.is_ge, fill=0.0, base=HR - 1,
                               pattern=[[-1, P]], channel_multiplier=HR).then_inc(s_hm, 1)
            pool.wait_ge(s_av, 64)
            for n in range(4):
                if n == 0:
                    pool.wait_ge(s_w1, 16)
                if n == 2:
                    pool.wait_ge(s_w2, 16 * HEADS)
                if n >= 1:
                    pool.wait_ge(s_red, n)
                w = wraw if n < 2 else w2raw
                pool.tensor_tensor(prod[:], w[:], avec[:, n, :].unsqueeze(1).broadcast_to([P, KC, D]),
                                   ALU.mult).then_inc(s_prod, 1)
                if n == 1 or n == 3:
                    part = n // 2
                    if part == 0:
                        pool.wait_ge(s_split, 1)
                        for kk in range(KC):
                            pool.tensor_tensor(s["w1s"][:, 1, kk, :].rearrange("p (m h r) -> p m h r", h=HEADS, r=HR),
                                               wraw[:, kk, :].rearrange("p (h m r) -> p m h r", h=HEADS, r=HR),
                                               s["w1s"][:, 0, kk, :].bitcast(F32).rearrange("p (m h r) -> p m h r", h=HEADS, r=HR),
                                               ALU.subtract)
            pool.wait_ge(s_none, 18)
            pool.wait_ge(s_endi, 1)
            for t in range(ET):
                pool.indirect_dma_start(d["node_pos"], bass.IndirectOffsetOnAxis(ap=end_i[:, t:t + 1], axis=0),
                                        place_i[:, t:t + 1], None, bounds_check=N - 1,
                                        oob_is_err=False).then_inc(s_scat, 16)

        @block.vector
        def _(dve):
            n_done = [0]

            def step(ins):
                n_done[0] += 1
                ins.then_inc(s_dve, 1)
                dve.wait_ge(s_dve, n_done[0])

            dve.wait_ge(s_iota, 1)
            dve.tensor_copy(frac[:], frac_i[:])
            step(dve.tensor_copy(rowp[:], rowp_i[:]))
            dve.tensor_copy(iota_f[:], frac[:])
            dve.memset(key[:, E:EP], float(N))
            dve.memset(less[:], 0.0)
            step(dve.tensor_scalar(frac[:], frac[:], 1.0 / 256, None, ALU.mult))
            step(dve.tensor_scalar(rowp[:], rowp[:], 1.0 / 256, None, ALU.mult))
            dve.wait_ge(s_col, 64)
            step(dve.tensor_copy(dst_f[:], col_i[:, 1, :]))
            dve.tensor_scalar(thr[:, 0, :], dst_f[:], 0.75, None, ALU.add)
            dve.tensor_scalar(thr[:, 1, :], dst_f[:], -0.25, None, ALU.add)
            step(dve.tensor_scalar(thr[:, 2, :], dst_f[:], rowp[:, 0:1], None, ALU.add))
            dve.tensor_scalar(nthr[:, 0:2, :], thr[:, 0:2, :], -1.0, None, ALU.mult)
            dve.tensor_scalar(nthr[:, 2, :], thr[:, 2, :], -1.0, 1.0 / 512, ALU.mult, ALU.add)
            dve.wait_ge(s_key, 16)
            step(dve.tensor_copy(key[:, 0:E], key[:, 0:E].bitcast(I32)))
            dve.tensor_tensor(key[:].rearrange("p (t j) -> p t j", j=P), key[:].rearrange("p (t j) -> p t j", j=P),
                              frac[:].unsqueeze(1).broadcast_to([P, ET, P]), ALU.add).then_inc(s_colr, 1)
            dve.wait_ge(s_colr, 1)
            for t in range(ET):
                if t in ACT_TILES:
                    continue
                for n, (lo, hi) in enumerate(((0, t * P), ((t + 1) * P, EP), (t * P, (t + 1) * P))):
                    if hi > lo:
                        step(dve.tensor_scalar(junk_v[:, lo:hi], key[:, lo:hi], thr[:, n, t:t + 1], None, ALU.is_lt,
                                               ALU.add, accum_out=less[:, n, t:t + 1]))
            for n in range(2):
                dve.tensor_scalar(part_i[:, 2 * n, :], col_i[:, n, :], 7, None, ALU.logical_shift_right)
                dve.tensor_scalar(part_i[:, 2 * n + 1, :], col_i[:, n, :], P - 1, None, ALU.bitwise_and)
            dve.wait_ge(s_cnt_a, 1)
            step(dve.tensor_tensor(rank[:, 0, :], less[:, 0, :], less[:, 1, :], ALU.add))
            step(dve.tensor_tensor(rank[:, 1, :], rank[:, 0, :], less[:, 2, :], ALU.add))
            t0 = ACT_TILES[0]
            step(dve.tensor_scalar(rank[:, 2, t0:ET], rank[:, 1, t0:ET], -0.5, EP / 2.0, ALU.mult, ALU.add))
            dve.tensor_copy(rank_i[:, 0, 0:t0], rank[:, 1, 0:t0])
            dve.tensor_copy(rank_i[:, 0, t0:ET], rank[:, 2, t0:ET])
            step(dve.tensor_copy(part_f[:], part_i[:]))
            dve.tensor_scalar(rank_i[:, 1, :], rank_i[:, 0, :], 7, None, ALU.logical_shift_right)
            step(dve.tensor_scalar(rank_i[:, 2, :], rank_i[:, 0, :], P - 1, None, ALU.bitwise_and))
            step(dve.tensor_copy(hl_f[:], rank_i[:, 1:3, :]))
            dve.tensor_tensor(oh_lo[:], iota_f[:].unsqueeze(1).broadcast_to([P, ET, P]),
                              hl_f[:, 1, :].unsqueeze(2).broadcast_to([P, ET, P]), ALU.is_equal)
            step(dve.tensor_tensor(ohr[:], iota_f[:, 0:ET].unsqueeze(1).broadcast_to([P, ET, ET]),
                                   hl_f[:, 0, :].unsqueeze(2).broadcast_to([P, ET, ET]), ALU.is_equal))
            for n in range(4):
                last = dve.tensor_tensor(oh_hi[:, :, n, :], ohr[:],
                                         part_f[:, n, :].unsqueeze(2).broadcast_to([P, ET, ET]), ALU.mult)
            last.then_inc(s_oh, 1)
            dve.wait_ge(s_sorted, 1)
            step(dve.tensor_copy(sorted4[:], p_sort[:, 0:4 * ET].rearrange("p (n t) -> p n t", t=ET)))
            for n in range(2):
                ins = dve.scalar_tensor_tensor(col_f[:, n, :], sorted4[:, 2 * n, :], float(P), sorted4[:, 2 * n + 1, :],
                                               ALU.mult, ALU.add)
            n_done[0] += 1
            ins.then_inc(s_dve, 1)
            dve.wait_ge(s_dve, n_done[0])
            dve.tensor_scalar(clip_f[:], col_f[:, 1, :], float(N - 1), None, ALU.min).then_inc(s_vec, 1)
            dve.wait_ge(s_vec, 1)
            gi = s["gidx"][:].rearrange("p (g n j) -> p g n j", n=2, j=TG)
            dve.tensor_copy(gi[:, :, 1, :], col_f[:, 0, :].rearrange("p (g j) -> p g j", j=TG))
            dve.tensor_copy(gi[:, :, 0, :], clip_f[:].rearrange("p (g j) -> p g j", j=TG))
            dve.wait_ge(s_row, 1)
            dve.tensor_copy(dst_row[:], p_row[0:ET, 0:P]).then_inc(s_row, 1)
            for n in range(2):
                dve.wait_ge(s_prod, n + 1)
                dve.tensor_reduce(v_f[:, n, :, :].rearrange("p k h -> p (k h)"),
                                  prod[:].rearrange("p k (h c) -> p (k h) c", c=HC), AX.X, ALU.add).then_inc(s_red, 1)
            dve.wait_ge(s_red, 2)
            step(dve.tensor_copy(s["v1"][:, :, 0, :, :], v_f[:]))
            dve.tensor_tensor(s["v1"][:, :, 1, :, :], v_f[:], s["v1"][:, :, 0, :, :].bitcast(F32), ALU.subtract)
            dve.wait_ge(s_win, 16)
            dve.tensor_tensor(eq[:, 0, :], window[:, 1:P + 1], window[:, 0:P], ALU.is_equal)
            step(dve.tensor_tensor(eq[:, 1, :], window[:, 1:P + 1], window[:, 2:P + 2], ALU.is_equal))
            dve.tensor_scalar(masks[:, 0, :], eq[:, 0, :], 0.5, BIG, ALU.subtract, ALU.mult)
            dve.tensor_scalar(masks[:, 1, :], eq[:, 0, :], 1.0, 1e30, ALU.subtract, ALU.mult).then_inc(s_maskst, 1)
            dve.scalar_tensor_tensor(end_row[:], eq[:, 1, :], 20000.0, window[:, 1:P + 1], ALU.mult, ALU.add).then_inc(s_endT, 1)
            dve.wait_ge(s_endT, 2)
            dve.tensor_copy(end_i[:], p_end[:, 0:ET]).then_inc(s_endi, 1)
            for n in range(2):
                dve.wait_ge(s_prod, n + 3)
                dve.tensor_reduce(s["v2"][:, :, n], prod[:], AX.X, ALU.add).then_inc(s_red, 1)

        @block.tensor
        def _(pe):
            pe.wait_ge(s_oh, 1)
            for t in range(ET):
                mm = pe.matmul(p_sort[:, 0:4 * ET], oh_lo[:, t, :], oh_hi[:, t, :, :], start=(t == 0), stop=(t == ET - 1))
            mm.then_inc(s_sorted, 1)
            pe.wait_ge(s_id, 2)
            pe.wait_ge(s_vec, 1)
            pe.transpose(p_row[0:ET, 0:P], col_f[:, 1, :], s["ident"][:]).then_inc(s_row, 1)
            pe.wait_ge(s_endT, 1)
            pe.transpose(p_end[:, 0:ET], end_row[:], s["ident"][0:ET, 0:ET]).then_inc(s_endT, 1)

        @block.scalar
        def _(act):
            act.wait_ge(s_w1, 16)
            for kk in range(KC):
                hi = act.activation(s["w1s"][:, 0, kk, :].rearrange("p (m h r) -> p m h r", h=HEADS, r=HR),
                                    wraw[:, kk, :].rearrange("p (h m r) -> p m h r", h=HEADS, r=HR), ACT.Copy)
            hi.then_inc(s_split, 1)
            act.wait_ge(s_colr, 1)
            n = 0
            for t in ACT_TILES:
                for j, (lo, hi_) in enumerate(((0, t * P), ((t + 1) * P, EP), (t * P, (t + 1) * P))):
                    if hi_ > lo:
                        wait(act, s_cnt_v, n)
                        n += 1
                        act.activation(junk_a[:, lo:hi_], key[:, lo:hi_], ACT.Sign, bias=nthr[:, j, t:t + 1],
                                       accum_out=less[:, j, t:t + 1]).then_inc(s_cnt_v, 1)
            act.wait_ge(s_cnt_v, n)
            act.sem_inc(s_cnt_a, 1)



def softmax_steps(dve, b, sem, g, np_, mask, mask_in, x_read):
    def first():
        dve.wait_ge(*mask_in)
        dve.wait_ge(sem["e_out"], g + 1)
        if sem["carry"](g):
            wait(dve, sem["z"], g)
            dve.tensor_copy(b["m"][:, 0:1], b["m"][:, GE:GE + 1])
        dve.scalar_tensor_tensor(b["e"][:], b["e"][:], SLOPE, b["e"][:], ALU.mult, ALU.max).then_inc(sem["lrelu"], 1)
        dve.wait_ge(sem["lrelu"], g + 1)
        dve.tensor_tensor_scan(b["m"][:, 1:GE + 1], mask[:, 0, :], b["e"][:], b["m"][:, 0:1],
                               ALU.min, ALU.max).then_inc(sem["m"], 1)
        dve.wait_ge(sem["m"], g + 1)
        wait(dve, *x_read)
        dve.tensor_tensor(b["x"][:, 1, :], b["e"][:], b["m"][:, 1:GE + 1], ALU.subtract)
        dve.tensor_tensor(b["x"][:, 0, :], b["m"][:, 0:GE], b["m"][:, 1:GE + 1], ALU.subtract).then_inc(sem["diff"], 1)
        dve.wait_ge(sem["diff"], g + 1)
        dve.scalar_tensor_tensor(b["x"][:, 0, :], b["x"][:, 0, :], 0.0, mask[:, 1, :], ALU.min,
                                 ALU.add).then_inc(sem["x"], 1)

    def second():
        dve.wait_ge(sem["exp"], g + 1)
        if sem["carry"](g):
            dve.tensor_copy(b["z"][:, 0:1], b["z"][:, GE:GE + 1]).then_inc(sem["zc"], 1)
            dve.wait_ge(sem["zc"], g)
        dve.tensor_tensor_scan(b["z"][:, 1:GE + 1], b["x"][:, 0, :], b["x"][:, 1, :], b["z"][:, 0:1],
                               ALU.mult, ALU.add).then_inc(sem["z"], 1)
        dve.wait_ge(sem["z"], g + 1)
        dve.tensor_tensor(b["x"][:, 0, :], b["x"][:, 0, :], b["z"][:, 0:GE], ALU.mult)
        dve.tensor_scalar(b["r"][:], b["z"][:, 1:GE + 1], 1e-16, None, ALU.add).then_inc(sem["zz"], 1)
        dve.wait_ge(sem["zz"], g + 1)
        dve.reciprocal(b["r"][:], b["r"][:]).then_inc(sem["rz"], 1)
        dve.wait_ge(sem["rz"], g + 1)
        dve.tensor_tensor(b["x"][:], b["x"][:], b["r"][:].unsqueeze(1).broadcast_to([np_, 2, GE]),
                          ALU.mult).then_inc(sem["ab"], 1)

    return first, second


def softmax_kit(k, np_):
    b = {"m": k.sb("run_max", [np_, GE + 1]), "z": k.sb("run_sum", [np_, GE + 1]), "e": k.sb("logit", [np_, GE]),
         "x": k.sb("expo", [np_, 2, GE]), "r": k.sb("rcp", [np_, GE])}
    sem = {n: k.sem("s_sm_" + n) for n in ("e_out", "lrelu", "m", "diff", "x", "exp", "zc", "z", "zz", "rz", "ab")}
    return b, sem


def gat_layer_1(nc, a, d, s):
    with ExitStack() as ctx:
        k = Kit(nc, ctx, "a_")
        xt = k.sb("xt", [P, 2, 2, KC, GE], F32R)
        xd = k.sb("xd", [P, 2, KC, 2 * P], F32R)
        raw = k.sb("raw", [P, 8, D])
        msg = k.sb("msg", [P, 2, GE])
        agg = k.sb("agg", [P, 2, GE])
        pos_part = k.sb("pos_part", [P, 2, GE])
        neg_part = k.sb("neg_part", [P, 2, GE])
        g1 = k.sb("g1", [P, 2, GE])
        rows = k.sb("rows", [P, 2, TG, P])
        ab = k.sb("ab", [P, 2, GE])
        carry = k.sb("carry", [P, KC])
        mask = k.sb("mask", [HEADS, 2, 2, GE])
        b, sem = softmax_kit(k, HEADS)
        stage = k.sb("stage", [P, 8], I32)
        pstage = k.sb("pstage", [P, 8], I32)
        stats = k.sb("stats", [P, 2, 2, 2, 6])
        mv = k.sb("mv", [P, 2, 2, 2])
        rstd = k.sb("rstd", [P, 2, 2])
        nmr = k.sb("nmr", [P, 2, 2])
        consts = k.sb("consts", [P, 6])
        logit2 = k.sb("logit2", [P, TG, 2])
        bdef = k.sb("bdef", [P, 3, KC])
        ldef = k.sb("ldef", [1, 2])
        negb = k.sb("negb", [P, KC])
        bm1 = k.sb("bm1", [P, KC])
        T = [k.ps("p_t0"), k.ps("p_t1")]
        H = [k.ps("p_h0"), k.ps("p_h1")]
        LG, EX, AS, RO = k.ps("p_lg"), k.ps("p_ex"), k.ps("p_as"), k.ps("p_ro")
        raw_in, st, mask_in = k.sems("s_raw", 8), k.sems("s_st", 2), k.sems("s_mask", 2)
        (pos_ready, passed_p, passed_v, pos_in, staged, stat, mvr, vv, pw, ln, normed, turned, hi_out, lo_out, dlog, lg_done, ab_ex, ab_out,
         h_done, msg_done, agg_done, car, neg_done, elu_done, g_done, tail_done, rows_out, as_done, as_out, st_as,
         dflt, init) = [k.sem(f"s_a{i}") for i in range(32)]
        sem["carry"] = lambda g: not (isinstance(g, int) and g == 0)
        block = k.block()

        def groups(eng, body):
            body(0, 0, True, True)
            with eng.Fori(0, (EG - 4) // 2) as i:
                body(2 * i + 1, 1, True, True)
                body(2 * i + 2, 0, True, True)
            body(EG - 3, (EG - 3) % 2, True, True)
            body(EG - 2, EG % 2, True, False)
            body(EG - 1, (EG - 1) % 2, False, False)

        @block.gpsimd
        def _(pool):
            for n, v in enumerate((-0.5, EPS, -1.0)):
                pool.memset(consts[:, 2 * n:2 * n + 2], v)
            pool.memset(b["m"][:, 0:1], 0.0)
            pool.memset(b["z"][:, 0:1], 0.0)
            pool.memset(carry[:], 0.0).then_inc(init, 1)
            pool.wait_ge(init, 1)

            def gather(G, u):
                for j in (2 * u, 2 * u + 1):
                    q = 8 * G + j
                    wait(pool, turned, 2 * q - 14)
                    pool.tensor_copy(stage[:, j:j + 1], s["gidx"][:, bass.ds(q, 1)]).then_inc(staged, 1)
                    carried_wait(pool, passed_p, staged, q + 1)
                    pool.indirect_dma_start(raw[:, j, :], None, a["x"],
                                            bass.IndirectOffsetOnAxis(ap=stage[:, j:j + 1], axis=0)).then_inc(raw_in[j], 16)
                    pool.indirect_dma_start(pstage[:, j:j + 1], None, d["node_pos"],
                                            bass.IndirectOffsetOnAxis(ap=stage[:, j:j + 1], axis=0)).then_inc(pos_in, 16)

            def positions(G):
                pool.wait_ge(pos_in, 128 * G + 128)
                pool.tensor_copy(s["pos"][:, bass.ds(8 * G, 8)], pstage[:]).then_inc(init, 1)
                pool.wait_ge(init, G + 2)

            def deviations(G, u):
                r, w = 4 * G + u, u % 2
                pool.wait_ge(mvr, r + 1)
                pool.tensor_tensor(rstd[:, w, :], mv[:, w, :, 1], consts[:, 2:4], ALU.add)
                pool.tensor_tensor(nmr[:, w, :], mv[:, w, :, 0], consts[:, 4:6], ALU.mult).then_inc(vv, 1)
                pool.wait_ge(vv, r + 1)
                pool.tensor_tensor(rstd[:, w, :], rstd[:, w, :], consts[:, 0:2], ALU.pow).then_inc(pw, 1)
                pool.wait_ge(pw, r + 1)
                pool.tensor_tensor(nmr[:, w, :], nmr[:, w, :], rstd[:, w, :], ALU.mult).then_inc(ln, 1)

            def join(g, m):
                c = 6 * g + m
                wait(pool, tail_done, c - 1)
                pool.wait_ge(pos_ready, c + 1)
                pool.wait_ge(elu_done, c + 1)
                pool.tensor_tensor(g1[:, m % 2, :], neg_part[:, m % 2, :], pos_part[:, m % 2, :], ALU.add).then_inc(g_done, 1)

            for u in range(4):
                gather(0, u)
            for u in range(4):
                deviations(0, u)
                if u == 1:
                    positions(0)
                if u >= 1:
                    gather(1, u - 1)
            gather(1, 3)
            positions(1)
            deviations(1, 0)
            deviations(1, 1)

            def body(g, w, nxt, chain):
                for m in range(6):
                    if not (isinstance(g, int) and g == 0 and m == 0):
                        join(g if m else g - 1, (m - 1) % 6)
                    if nxt and m < 2:
                        deviations(g + 1, m + 2)
                    if chain and m == 4:
                        deviations(g + 2, 0)
                        deviations(g + 2, 1)
                    if chain and 1 <= m <= 4:
                        gather(g + 2, m - 1)
                    if chain and m == 5:
                        positions(g + 2)

            groups(pool, body)
            join(EG - 1, 5)

        @block.sync
        def _(sp):
            def mask_load(g, w):
                wait(sp, sem["ab"], g - 1)
                sp.dma_start(mask[:, w, :, :], d["masks"][:, bass.ds(g * GE, GE)].partition_broadcast(HEADS)).then_inc(mask_in[w], 16)

            def row_store(g, m):
                c = 6 * g + m
                sp.wait_ge(rows_out, c + 1)
                sp.dma_start(d["layer1"][bass.ds(g * GE, GE), m * P:(m + 1) * P].rearrange("(t p) j -> p t j", p=P),
                             rows[:, m % 2, :, :]).then_inc(st[m % 2], 16)

            def logit_store(g):
                sp.wait_ge(as_out, g + 1)
                sp.dma_start(d["layer1"][bass.ds(g * GE, GE), D:D + 1].rearrange("(t p) o -> p t o", p=P), logit2[:, :, 0:1],
                             allow_slow_non_contiguous=True).then_inc(st_as, 16)
                sp.dma_start(d["dst_logit"][bass.ds(g * GE, GE), :].rearrange("(t p) o -> p t o", p=P), logit2[:, :, 1:2],
                             allow_slow_non_contiguous=True).then_inc(st_as, 16)

            mask_load(0, 0)
            mask_load(1, 1)
            sp.wait_ge(dflt, 5)
            sp.dma_start(d["layer1"][EP:EP + 1, 0:D].rearrange("o (m p) -> p (o m)", p=P), bdef[:, 0, :], allow_slow_non_contiguous=True).then_inc(dflt, 16)
            sp.dma_start(d["layer1"][EP:EP + 1, D:D + 1], ldef[:, 0:1]).then_inc(dflt, 16)
            sp.dma_start(d["dst_logit"][EP:EP + 1, :], ldef[:, 1:2]).then_inc(dflt, 16)

            def body(g, w, nxt, chain):
                first = isinstance(g, int) and g == 0
                if not first and nxt:
                    mask_load(g + 1, 1 - w)
                for m in range(6):
                    if m >= 2:
                        row_store(g, m - 2)
                    elif not first:
                        row_store(g - 1, m + 4)
                        if m == 1:
                            logit_store(g - 1)

            groups(sp, body)
            row_store(EG - 1, 4)
            row_store(EG - 1, 5)
            logit_store(EG - 1)
            for w in range(2):
                sp.wait_ge(st[w], 16 * 3 * EG)
            sp.wait_ge(st_as, 32 * EG)
            sp.wait_ge(dflt, 53)

        @block.scalar
        def _(act):
            def normalise(G, u):
                r = 4 * G + u
                act.wait_ge(ln, r + 1)
                for n in range(2):
                    act.activation(raw[:, 2 * u + n, :], raw[:, 2 * u + n, :], ACT.Identity,
                                   bias=nmr[:, u % 2, n:n + 1], scale=rstd[:, u % 2, n:n + 1]).then_inc(normed, 1)

            def high(G, W, j):
                q = 8 * G + j
                if j in (0, 1):
                    wait(act, dlog, 2 * G)
                elif j in (2, 3):
                    act.wait_ge(dlog, 2 * G + 1)
                else:
                    wait(act, h_done, 6 * G - 6)
                for h in range(2):
                    act.wait_ge(turned, 2 * q + h + 1)
                    if j < 4:
                        out = xd[:, 0, 3 * h:3 * h + 3, (j % 2) * P:(j % 2 + 1) * P]
                    else:
                        out = xt[:, W, 0, 3 * h:3 * h + 3, (j - 4) * P:(j - 3) * P]
                    act.activation(out, T[h][:, 0:3 * P].rearrange("p (k j) -> p k j", k=3), ACT.Copy).then_inc(hi_out, 1)

            def logit_copy(G):
                act.wait_ge(lg_done, G + 1)
                wait(act, sem["ab"], G)
                act.activation(b["e"][:], LG[0:HEADS, :], ACT.Copy).then_inc(sem["e_out"], 1)

            def exps(G):
                act.wait_ge(sem["x"], G + 1)
                act.activation(b["x"][:], b["x"][:], ACT.Exp).then_inc(sem["exp"], 1)

            def ab_copy(g):
                wait(act, agg_done, 6 * g)
                act.wait_ge(ab_ex, 2 * g + 1)
                act.activation(ab[:, 0, :], EX[:], ACT.Copy).then_inc(ab_out, 1)
                act.wait_ge(ab_ex, 2 * g + 2)
                act.activation(ab[:, 1, :], LG[:], ACT.Copy).then_inc(ab_out, 1)

            def elu(g, m):
                c = 6 * g + m
                act.wait_ge(agg_done, c + 1)
                wait(act, g_done, c - 1)
                act.activation(neg_part[:, m % 2, :], agg[:, m % 2, :], ACT.Relu, bias=negb[:, m:m + 1], scale=-1.0).then_inc(neg_done, 1)
                act.wait_ge(neg_done, c + 1)
                act.activation(neg_part[:, m % 2, :], neg_part[:, m % 2, :], ACT.Exp, scale=-1.0).then_inc(elu_done, 1)

            def rows_copy(g, m):
                c = 6 * g + m
                act.wait_ge(tail_done, c + 1)
                wait(act, st[m % 2], 16 * (3 * g + m // 2))
                act.activation(rows[:, m % 2, :, :], RO[:].rearrange("p (t j) -> p t j", t=TG), ACT.Copy).then_inc(rows_out, 1)

            def logit2_copy(g):
                act.wait_ge(as_done, g + 1)
                wait(act, st_as, 32 * g)
                act.activation(logit2[:], AS[:, 0:2 * TG].rearrange("p (t n) -> p t n", n=2), ACT.Copy).then_inc(as_out, 1)

            act.activation(negb[:], s["b1col"][:], ACT.Copy, scale=-1.0)
            act.activation(bdef[:, 0, :], s["b1col"][:], ACT.Relu)
            act.wait_ge(dflt, 1)
            act.activation(bdef[:, 1, :], bdef[:, 1, :], ACT.Exp).then_inc(dflt, 1)
            act.wait_ge(dflt, 4)
            act.activation(ldef[:], AS[0:1, 0:2], ACT.Copy).then_inc(dflt, 1)
            for u in range(4):
                normalise(0, u)
                high(0, 0, 2 * u)
                high(0, 0, 2 * u + 1)
            logit_copy(0)
            exps(0)
            normalise(1, 0)
            normalise(1, 1)

            def body(g, w, nxt, chain):
                first = isinstance(g, int) and g == 0
                for m in range(6):
                    if nxt and 1 <= m <= 4:
                        high(g + 1, 1 - w, 2 * m - 1)
                    if nxt and m == 0:
                        high(g + 1, 1 - w, 0)
                    if not (first and m == 0):
                        elu(g if m else g - 1, (m - 1) % 6)
                    if nxt and 1 <= m < 4:
                        high(g + 1, 1 - w, 2 * m)
                    if m == 0:
                        ab_copy(g)
                    if nxt and m < 2:
                        normalise(g + 1, m + 2)
                    if nxt and m == 4:
                        logit_copy(g + 1)
                    if chain and m == 5:
                        normalise(g + 2, 1)
                    if m >= 2:
                        rows_copy(g, m - 2)
                    elif not first:
                        rows_copy(g - 1, m + 4)
                        if m == 1:
                            logit2_copy(g - 1)
                    if nxt and m == 4:
                        exps(g + 1)
                    if chain and m == 4:
                        normalise(g + 2, 0)

            groups(act, body)
            elu(EG - 1, 5)
            rows_copy(EG - 1, 4)
            rows_copy(EG - 1, 5)
            logit2_copy(EG - 1)

        @block.vector
        def _(dve):
            def moments(G, u):
                r, w = 4 * G + u, u % 2
                wait(dve, ln, r - 1)
                wait(dve, normed, 2 * r - 2)
                for n in range(2):
                    j = 2 * u + n
                    dve.wait_ge(raw_in[j], 16 * (G + 1))
                    for h in range(2):
                        last = dve.bn_stats(stats[:, w, n, h, :], raw[:, j, h * HALF:(h + 1) * HALF])
                last.then_inc(stat, 1)
                carried_wait(dve, passed_v, stat, r + 1)
                dve.bn_aggr(mv[:, w, 0, :], stats[:, w, 0, :, :])
                dve.bn_aggr(mv[:, w, 1, :], stats[:, w, 1, :, :]).then_inc(mvr, 1)

            def low(G, W, j):
                q = 8 * G + j
                for h in range(2):
                    dve.wait_ge(hi_out, 2 * q + h + 1)
                    if j < 4:
                        v = xd[:, :, 3 * h:3 * h + 3, (j % 2) * P:(j % 2 + 1) * P]
                    else:
                        v = xt[:, W, :, 3 * h:3 * h + 3, (j - 4) * P:(j - 3) * P]
                    dve.tensor_tensor(v[:, 1], T[h][:, 0:3 * P].rearrange("p (k j) -> p k j", k=3), v[:, 0].bitcast(F32),
                                      ALU.subtract).then_inc(lo_out, 1)

            def scan_chunk(g, m):
                c = 6 * g + m
                if m == 0:
                    dve.wait_ge(ab_out, 2 * g + 2)
                dve.wait_ge(h_done, c + 1)
                dve.tensor_tensor(msg[:, m % 2, :], H[m % 2][:], ab[:, 1, :], ALU.mult).then_inc(msg_done, 1)
                wait(dve, elu_done, c - 1)
                wait(dve, pos_ready, c - 1)
                dve.wait_ge(msg_done, c + 1)
                dve.tensor_tensor_scan(agg[:, m % 2, :], ab[:, 0, :], msg[:, m % 2, :], carry[:, m:m + 1],
                                       ALU.mult, ALU.add).then_inc(agg_done, 1)
                dve.wait_ge(agg_done, c + 1)
                dve.tensor_copy(carry[:, m:m + 1], agg[:, m % 2, GE - 1:GE]).then_inc(car, 1)
                wait(dve, g_done, c - 1)
                dve.tensor_scalar(pos_part[:, m % 2, :], agg[:, m % 2, :], bm1[:, m:m + 1], -1.0, ALU.add,
                                  ALU.max).then_inc(pos_ready, 1)

            def softmax(G, W, loaded):
                return softmax_steps(dve, b, sem, G, HEADS, mask[:, W, :, :], (mask_in[W], loaded), (ab_ex, 2 * G))

            dve.wait_ge(init, 1)
            dve.tensor_scalar(bm1[:], s["b1col"][:], -1.0, None, ALU.add)
            dve.tensor_scalar(bdef[:, 1, :], s["b1col"][:], 0.0, None, ALU.min).then_inc(dflt, 1)
            dve.wait_ge(dflt, 2)
            dve.scalar_tensor_tensor(bdef[:, 0, :], bdef[:, 1, :], -1.0, bdef[:, 0, :], ALU.add, ALU.add).then_inc(dflt, 1)
            for u in range(4):
                moments(0, u)
                low(0, 0, 2 * u)
                low(0, 0, 2 * u + 1)
            first_, second_ = softmax(0, 0, 16)
            first_()
            second_()
            moments(1, 0)
            moments(1, 1)

            def body(g, w, nxt, chain):
                for m in range(6):
                    if nxt and 1 <= m <= 4:
                        low(g + 1, 1 - w, 2 * m - 1)
                    if nxt and m == 0:
                        low(g + 1, 1 - w, 0)
                    if nxt and m < 2:
                        moments(g + 1, m + 2)
                    if chain and m == 4:
                        moments(g + 2, 0)
                        moments(g + 2, 1)
                    if nxt and m == 4:
                        first_, second_ = softmax(g + 1, 1 - w, 8 * g + (24 if w else 16))
                        first_()
                    if nxt and 1 <= m < 4:
                        low(g + 1, 1 - w, 2 * m)
                    scan_chunk(g, m)
                    if nxt and m == 4:
                        second_()

            groups(dve, body)

        @block.tensor
        def _(pe):
            def turn(G, j):
                q = 8 * G + j
                pe.wait_ge(normed, q + 1)
                for h in range(2):
                    wait(pe, lo_out, 2 * q + h - 1)
                    for kk in range(3):
                        mm = pe.transpose(T[h][:, kk * P:(kk + 1) * P],
                                          raw[:, j, (3 * h + kk) * P:(3 * h + kk + 1) * P], s["ident"][:])
                    mm.then_inc(turned, 1)

            def passes(out, lhs, rhs, start, stop, lint=False):
                for i, (x, y) in enumerate(((0, 0), (1, 0), (0, 1))):
                    mm = pe.matmul(out, lhs(x), rhs(y), start=start and i == 0, stop=stop and i == 2, skip_group_check=lint)
                return mm

            def dst_logits(G, hh):
                pe.wait_ge(lo_out, 16 * G + 4 * hh + 4)
                if hh == 0:
                    wait(pe, ab_out, 2 * G)
                for kk in range(KC):
                    mm = passes(LG[0:HEADS, hh * 2 * P:(hh + 1) * 2 * P], lambda i: s["v1"][:, 1, i, kk, :],
                                lambda i: xd[:, i, kk, :], hh == 0 and kk == 0, False, True)
                mm.then_inc(dlog, 1)

            def src_logits(G, W):
                pe.wait_ge(lo_out, 16 * G + 16)
                for kk in range(KC):
                    mm = passes(LG[0:HEADS, :], lambda i: s["v1"][:, 0, i, kk, :], lambda i: xt[:, W, i, kk, :],
                                False, kk == KC - 1, True)
                mm.then_inc(lg_done, 1)

            def spread(g):
                pe.wait_ge(sem["ab"], g + 1)
                pe.matmul(EX[:], s["headmap"][:], b["x"][:, 0, :], start=True, stop=True).then_inc(ab_ex, 1)
                pe.matmul(LG[:], s["headmap"][:], b["x"][:, 1, :], start=True, stop=True).then_inc(ab_ex, 1)

            def products(g, w, m, part):
                c = 6 * g + m
                if part == 0:
                    wait(pe, msg_done, c - 1)
                for kk in (range(0, 3), range(3, KC))[part]:
                    mm = passes(H[m % 2][:], lambda i: s["w1s"][:, i, kk, m * P:(m + 1) * P],
                                lambda i: xt[:, w, i, kk, :], kk == 0, kk == KC - 1, True)
                if part == 1:
                    mm.then_inc(h_done, 1)

            def tail(g, m):
                c = 6 * g + m
                pe.wait_ge(g_done, c + 1)
                wait(pe, rows_out, c)
                if m == 0:
                    wait(pe, as_out, g)
                for t in range(TG):
                    mm = pe.matmul(AS[:, 2 * t:2 * t + 2], g1[:, m % 2, t * P:(t + 1) * P], s["v2"][:, m, :], start=(m == 0 and t == 0),
                                   stop=(m == 5), skip_group_check=True)
                if m == 5:
                    mm.then_inc(as_done, 1)
                for t in range(TG):
                    mm = pe.transpose(RO[:, t * P:(t + 1) * P], g1[:, m % 2, t * P:(t + 1) * P], s["ident"][:])
                mm.then_inc(tail_done, 1)

            pe.wait_ge(dflt, 3)
            for m in range(KC):
                mm = pe.matmul(AS[0:1, 0:2], bdef[:, 0, m:m + 1], s["v2"][:, m, :], start=(m == 0), stop=(m == KC - 1))
            mm.then_inc(dflt, 1)
            pe.wait_ge(dflt, 5)
            for j in range(8):
                turn(0, j)
                if j in (1, 3):
                    dst_logits(0, j // 2)
            src_logits(0, 0)

            def body(g, w, nxt, chain):
                for m in range(6):
                    products(g, w, m, 0)
                    if nxt and m in (1, 2):
                        dst_logits(g + 1, m - 1)
                    if nxt and m < 4:
                        turn(g + 1, 2 * m)
                    if nxt and m == 4:
                        src_logits(g + 1, 1 - w)
                    products(g, w, m, 1)
                    if m == 0:
                        spread(g)
                    if m >= 2:
                        tail(g, m - 2)
                    elif not (isinstance(g, int) and g == 0):
                        tail(g - 1, m + 4)
                    if nxt and m < 4:
                        turn(g + 1, 2 * m + 1)

            groups(pe, body)
            tail(EG - 1, 4)
            tail(EG - 1, 5)


def gat_layer_2(nc, a, d, s):
    with ExitStack() as ctx:
        k = Kit(nc, ctx, "b_")
        xt = k.sb("xt", [P, 2, 2, KC, GE], F32R)
        raw = k.sb("raw", [P, 2, TG, RW])
        dlog = k.sb("dlog", [P, 2, TG])
        lcol = k.sb("lcol", [P, 2, TG, HEADS])
        msg = k.sb("msg", [P, 2, GE])
        agg = k.sb("agg", [P, 2, GE])
        ab = k.sb("ab", [P, 2, GE])
        carry = k.sb("carry", [P, KC])
        mask = k.sb("mask", [HEADS, 2, 2, GE])
        b, sem = softmax_kit(k, HEADS)
        sem["carry"] = lambda g: not (isinstance(g, int) and g == 0)
        stage = k.sb("stage", [P, 2, 8], I32)
        bias = k.sb("bias", [P, D])
        rows = k.sb("rows", [P, 2, D])
        w2s = k.sb("w2s", [P, 2, KC, D], F32R)
        gatw = k.sb("gatw", [P, KC, D])
        w1raw = gatw[:, 0:FC, :].rearrange("p m n -> p (m n)").rearrange("p (k h u) -> p k h u", h=EXPERTS, u=HID)
        w2raw = gatw[:, FC:2 * FC, :]
        T = [k.ps("p_t0"), k.ps("p_t1")]
        LG, EX = k.ps("p_lg"), k.ps("p_ex")
        ROW = [k.ps(f"p_row{i}") for i in range(4)]
        raw_in, st, mask_in = k.sems("s_raw", 2), k.sems("s_st", 2), k.sems("s_mask", 2)
        (passed_p, staged, init, lcol_done, lg_done, ab_ex, ab_out, turned, msg_done, agg_done, car, hi_out, lo_out, lo_p,
         unit_done, unit_out, row_out, bias_in, dflt, ffn_in, ffn_hi, ffn_lo, w2_in, w2_hi, w2_lo) = [
            k.sem("s_" + n) for n in ("passed_p", "staged", "init", "lcol", "lg", "ab_ex", "ab_out", "turned", "msg", "agg",
                                      "car", "hi", "lo", "lo_p", "unit", "unit_out", "row", "bias", "dflt", "ffn_in", "ffn_hi", "ffn_lo", "w2_in", "w2_hi", "w2_lo")]
        block = k.block()

        def groups(eng, body):
            body(0, 0, True, True)
            with eng.Fori(0, (EG - 4) // 2) as i:
                body(2 * i + 1, 1, True, True)
                body(2 * i + 2, 0, True, True)
            body(EG - 3, (EG - 3) % 2, True, True)
            body(EG - 2, EG % 2, True, False)
            body(EG - 1, (EG - 1) % 2, False, False)

        @block.gpsimd
        def _(pool):
            pool.memset(b["m"][:, 0:1], 0.0)
            pool.memset(b["z"][:, 0:1], 0.0)
            pool.memset(carry[:], 0.0).then_inc(init, 1)

            def gather(g, w):
                wait(pool, turned, 6 * g - 6)
                pool.tensor_copy(stage[:, w, :], s["pos"][:, bass.ds(8 * g, 8)]).then_inc(staged, 1)
                carried_wait(pool, passed_p, staged, g + 1)
                for j in range(TG):
                    pool.indirect_dma_start(dlog[:, w, j:j + 1], None, d["dst_logit"],
                                            bass.IndirectOffsetOnAxis(ap=stage[:, w, j:j + 1], axis=0)).then_inc(raw_in[w], 16)
                    pool.indirect_dma_start(raw[:, w, j, :], None, d["layer1"],
                                            bass.IndirectOffsetOnAxis(ap=stage[:, w, 4 + j:5 + j], axis=0)).then_inc(raw_in[w], 16)

            def add_bias(g, tiles):
                for t in tiles:
                    pool.wait_ge(unit_out, 8 * g + 2 * t + 2)
                    pool.tensor_tensor(rows[:, t % 2, :], rows[:, t % 2, :], bias[:], ALU.add).then_inc(row_out, 1)

            gather(0, 0)
            gather(1, 1)
            pool.wait_ge(w2_hi, 1)
            pool.tensor_tensor(w2s[:, 1, :, :], gatw[:], w2s[:, 0, :, :].bitcast(F32), ALU.subtract).then_inc(w2_lo, 1)
            def low(G, W, kk):
                pool.wait_ge(hi_out, 6 * G + kk + 1)
                pool.tensor_tensor(xt[:, W, 1, kk, :], agg[:, kk % 2, :], xt[:, W, 0, kk, :].bitcast(F32),
                                   ALU.subtract).then_inc(lo_p, 1)

            def body(g, w, nxt, chain):
                if nxt:
                    low(g + 1, 1 - w, 0)
                    low(g + 1, 1 - w, 1)
                add_bias(g, [0])
                if nxt:
                    low(g + 1, 1 - w, 2)
                add_bias(g, [1])
                if not isinstance(g, int) or g < EG - 3:
                    gather(g + 3, 1 - w)
                add_bias(g, [2, 3])
                if isinstance(g, int) and g == EG - 2:
                    pool.wait_ge(ffn_hi, 1)
                    for kk in range(KC):
                        pool.tensor_tensor(s["f1"][:, 1, kk, :].rearrange("p (m h r) -> p m h r", h=EXPERTS, r=HR),
                                           w1raw[:, kk, :, :].rearrange("p h (m r) -> p m h r", r=HR),
                                           s["f1"][:, 0, kk, :].bitcast(F32).rearrange("p (m h r) -> p m h r", h=EXPERTS, r=HR),
                                           ALU.subtract)
                    pool.tensor_tensor(s["f2"][:, 1, :, :], w2raw, s["f2"][:, 0, :, :].bitcast(F32), ALU.subtract).then_inc(ffn_lo, 1)

            for kk in range(3):
                low(0, 0, kk)
            gather(2, 0)
            pool.wait_ge(bias_in, 16)
            groups(pool, body)

        @block.sync
        def _(sp):
            def mask_load(g, w):
                wait(sp, sem["ab"], g - 1)
                sp.dma_start(mask[:, w, :, :], d["masks"][:, bass.ds(g * GE, GE)].partition_broadcast(HEADS)).then_inc(mask_in[w], 16)

            mask_load(0, 0)
            for h in range(HEADS):
                sp.dma_start(gatw[h * HR:(h + 1) * HR, :, :],
                             a["L0_gnn_W2"][h * HC:(h + 1) * HC, :].rearrange("(m r) n -> r m n", r=HR)).then_inc(w2_in, 16)
            mask_load(1, 1)
            sp.dma_start(bias[:], a["L0_gnn_b2"].partition_broadcast(P)).then_inc(bias_in, 16)
            sp.dma_start(d["layer2"][EP, :], a["L0_gnn_b2"]).then_inc(dflt, 16)
            sp.wait_ge(w2_lo, 1)
            for h in range(EXPERTS):
                sp.dma_start(w1raw[:, :, h, :], a["L0_ffn_w1"][h].rearrange("(k p) u -> p k u", p=P)).then_inc(ffn_in, 16)
                sp.dma_start(w2raw[h * HR:(h + 1) * HR, :, :],
                             a["L0_ffn_w2"][h].rearrange("(m r) n -> r m n", r=HR)).then_inc(ffn_in, 16)

            def body(g, w, nxt, chain):
                if chain:
                    mask_load(g + 2, w)
                for t in range(TG):
                    sp.wait_ge(row_out, 4 * g + t + 1)
                    sp.dma_start(d["layer2"][bass.ds(g * GE + t * P, P), :], rows[:, t % 2, :]).then_inc(st[t % 2], 16)

            groups(sp, body)
            for w in range(2):
                sp.wait_ge(st[w], 16 * 2 * EG)
            sp.wait_ge(dflt, 16)

        @block.scalar
        def _(act):
            def logit_copy(G):
                act.wait_ge(lg_done, G + 1)
                wait(act, sem["ab"], G)
                act.activation(b["e"][:], LG[0:HEADS, :], ACT.Copy).then_inc(sem["e_out"], 1)

            def exps(G):
                act.wait_ge(sem["x"], G + 1)
                act.activation(b["x"][:], b["x"][:], ACT.Exp).then_inc(sem["exp"], 1)

            def ab_copy(G):
                wait(act, agg_done, 6 * G)
                act.wait_ge(ab_ex, 2 * G + 2)
                act.activation(ab[:, 0, :], EX[:], ACT.Copy)
                act.activation(ab[:, 1, :], LG[:], ACT.Copy).then_inc(ab_out, 1)

            def unit_copy(g, u):
                t, h = u // 2, u % 2
                act.wait_ge(unit_done, 8 * g + u + 1)
                if h == 0:
                    wait(act, st[t % 2], 16 * (2 * g + t // 2))
                act.activation(rows[:, t % 2, h * HALF:(h + 1) * HALF], ROW[u % 4][:, 0:HALF], ACT.Copy).then_inc(unit_out, 1)

            def high(G, W, kk):
                act.wait_ge(agg_done, 6 * G + kk + 1)
                wait(act, unit_done, 8 * G - 8)
                act.activation(xt[:, W, 0, kk, :], agg[:, kk % 2, :], ACT.Copy).then_inc(hi_out, 1)

            act.wait_ge(w2_in, 16 * HEADS)
            act.activation(w2s[:, 0, :, :], gatw[:], ACT.Copy).then_inc(w2_hi, 1)
            logit_copy(0)
            exps(0)
            ab_copy(0)
            for kk in range(KC):
                high(0, 0, kk)
                if kk == 1:
                    logit_copy(1)
                if kk == 2:
                    exps(1)
            ab_copy(1)

            def body(g, w, nxt, chain):
                for u in range(8):
                    if u >= 1:
                        unit_copy(g, u - 1)
                    if nxt and u < KC:
                        high(g + 1, 1 - w, u)
                    if chain and u == 2:
                        logit_copy(g + 2)
                    if chain and u == 3:
                        exps(g + 2)
                unit_copy(g, 7)
                if chain:
                    ab_copy(g + 2)
                if isinstance(g, int) and g == 0:
                    act.wait_ge(ffn_in, 16 * 2 * EXPERTS)
                    for kk in range(KC):
                        act.activation(s["f1"][:, 0, kk, :].rearrange("p (m h r) -> p m h r", h=EXPERTS, r=HR),
                                       w1raw[:, kk, :, :].rearrange("p h (m r) -> p m h r", r=HR), ACT.Copy)
                    act.activation(s["f2"][:, 0, :, :], w2raw, ACT.Copy).then_inc(ffn_hi, 1)

            groups(act, body)

        @block.vector
        def _(dve):
            def logit_columns(G, W):
                dve.wait_ge(raw_in[W], 64 * (G - W) + 128)
                wait(dve, lg_done, G - 1)
                dve.tensor_tensor(lcol[:, W, :, :], raw[:, W, :, D:D + 1].broadcast_to([P, TG, HEADS]),
                                  dlog[:, W, :].unsqueeze(2).broadcast_to([P, TG, HEADS]), ALU.add).then_inc(lcol_done, 1)

            def scan_chunk(G, kk):
                c = 6 * G + kk
                if kk == 0:
                    dve.wait_ge(ab_out, G + 1)
                dve.wait_ge(turned, c + 1)
                dve.tensor_tensor(msg[:, kk % 2, :], T[kk % 2][:], ab[:, 1, :], ALU.mult).then_inc(msg_done, 1)
                wait(dve, hi_out, c - 1)
                if kk in (0, 1, 5):
                    wait(dve, lo_out, 3 * G + (kk - 1 if kk < 3 else 1))
                else:
                    dve.wait_ge(lo_p, 3 * G + kk - 1)
                dve.wait_ge(msg_done, c + 1)
                dve.tensor_tensor_scan(agg[:, kk % 2, :], ab[:, 0, :], msg[:, kk % 2, :], carry[:, kk:kk + 1],
                                       ALU.mult, ALU.add).then_inc(agg_done, 1)
                dve.wait_ge(agg_done, c + 1)
                dve.tensor_copy(carry[:, kk:kk + 1], agg[:, kk % 2, GE - 1:GE]).then_inc(car, 1)

            def low(G, W, kk):
                if kk < 3:
                    return
                dve.wait_ge(hi_out, 6 * G + kk + 1)
                dve.tensor_tensor(xt[:, W, 1, kk, :], agg[:, kk % 2, :], xt[:, W, 0, kk, :].bitcast(F32),
                                  ALU.subtract).then_inc(lo_out, 1)

            def softmax(G, W):
                return softmax_steps(dve, b, sem, G, HEADS, mask[:, W, :, :], (mask_in[W], 8 * (G - W) + 16), (ab_ex, 2 * G))

            dve.wait_ge(init, 1)
            logit_columns(0, 0)
            first_, second_ = softmax(0, 0)
            first_()
            second_()
            logit_columns(1, 1)
            first_, second_ = softmax(1, 1)
            for kk in range(KC):
                scan_chunk(0, kk)
                low(0, 0, kk)
                if kk == 1:
                    first_()
                if kk == 2:
                    second_()

            def body(g, w, nxt, chain):
                for u in range(8):
                    if nxt and 1 <= u <= KC:
                        low(g + 1, 1 - w, u - 1)
                    if nxt and u < KC:
                        scan_chunk(g + 1, u)
                    if chain:
                        if u == 0:
                            logit_columns(g + 2, w)
                        if u == 2:
                            first_, second_ = softmax(g + 2, w)
                            first_()
                        if u == 4:
                            second_()

            groups(dve, body)

        @block.tensor
        def _(pe):
            def logits(G, W):
                pe.wait_ge(lcol_done, G + 1)
                wait(pe, ab_out, G)
                for t in range(TG):
                    mm = pe.transpose(LG[0:HEADS, t * P:(t + 1) * P], lcol[:, W, t, :], s["ident"][:])
                mm.then_inc(lg_done, 1)

            def spread(G):
                pe.wait_ge(sem["ab"], G + 1)
                pe.matmul(EX[:], s["headmap"][:], b["x"][:, 0, :], start=True, stop=True).then_inc(ab_ex, 1)
                pe.matmul(LG[:], s["headmap"][:], b["x"][:, 1, :], start=True, stop=True).then_inc(ab_ex, 1)

            def turn(G, W, kk):
                wait(pe, msg_done, 6 * G + kk - 1)
                for t in range(TG):
                    mm = pe.transpose(T[kk % 2][:, t * P:(t + 1) * P], raw[:, W, t, kk * P:(kk + 1) * P], s["ident"][:])
                mm.then_inc(turned, 1)

            def unit(g, w, u):
                t, h = u // 2, u % 2
                if u == 0:
                    pe.wait_ge(lo_out, 3 * g + 3)
                    pe.wait_ge(lo_p, 3 * g + 3)
                    if isinstance(g, int) and g == 0:
                        pe.wait_ge(w2_lo, 1)
                wait(pe, unit_out, 8 * g + u - 3)
                for kk in range(KC):
                    for i, (x, y) in enumerate(((0, 0), (1, 0), (0, 1))):
                        mm = pe.matmul(ROW[u % 4][:, 0:HALF], xt[:, w, x, kk, t * P:(t + 1) * P],
                                       w2s[:, y, kk, h * HALF:(h + 1) * HALF], start=kk == 0 and i == 0,
                                       stop=kk == KC - 1 and i == 2)
                mm.then_inc(unit_done, 1)

            logits(0, 0)
            spread(0)
            for kk in range(KC):
                turn(0, 0, kk)
                if kk == 0:
                    logits(1, 1)
            spread(1)

            def body(g, w, nxt, chain):
                if nxt:
                    turn(g + 1, 1 - w, 0)
                for u in range(8):
                    unit(g, w, u)
                    if nxt and u < KC - 1:
                        turn(g + 1, 1 - w, u + 1)
                    if chain and u == 1:
                        logits(g + 2, w)
                if chain:
                    spread(g + 2)

            groups(pe, body)


def moe_ffn(nc, a, d, s, out):
    with ExitStack() as ctx:
        k = Kit(nc, ctx, "f_")
        xt = k.sb("xt", [P, 2, 2, KC, GE], F32R)
        x1 = k.sb("x1", [P, 2, TG, D])
        raw = k.sb("raw", [P, TG, D])
        res = k.sb("res", [P, TG, D])
        hid = k.sb("hid", [P, FC, GE])
        hs = k.sb("hs", [P, 2, FC, GE], F32R)
        stage = k.sb("stage", [P, 2, TG], I32)
        stats = k.sb("stats", [P, 2, 2, 2, 6])
        mv = k.sb("mv", [P, 2, 2, 2])
        rstd = k.sb("rstd", [P, 2, 2])
        nmr = k.sb("nmr", [P, 2, 2])
        ln_const = k.sb("ln_const", [P, 6])
        b1 = k.sb("b1", [P, FC])
        graw = k.sb("graw", [P, KC, EXPERTS])
        gate = k.sb("gate", [P, KC, 2, EXPERTS], F32R)
        sel = k.sb("sel", [2 * EXPERTS, EXPERTS])
        b2raw = k.sb("b2raw", [96, D])
        b2s = k.sb("b2s", [96, D], F32R)
        spread_f = k.sb("spread_f", [96, P])
        spread_w = k.sb("spread_w", [96, P], F32R)
        cpad = k.sb("cpad", [P, TG, 96])
        ct = k.sb("ct", [96, GE], F32R)
        lg16 = k.sb("lg16", [2 * EXPERTS, GE])
        lg = k.sb("lg", [P, TG, EXPERTS])
        top = k.sb("top", [P, TG, 8])
        top_i = k.sb("top_i", [P, TG, 8], mybir.dt.uint32)
        top_f = k.sb("top_f", [P, TG, 2])
        iota_i = k.sb("iota_i", [P, EXPERTS], I32)
        iota_f = k.sb("iota_f", [P, EXPERTS])
        gap = k.sb("gap", [P, TG])
        wgt = k.sb("wgt", [P, 2, TG])
        onehot = k.sb("onehot", [P, 2, TG, EXPERTS])
        comb = k.sb("comb", [P, TG, EXPERTS])
        comb_hi = k.sb("comb_hi", [P, TG, EXPERTS], F32R)
        T = [k.ps("p_t0"), k.ps("p_t1")]
        H = [k.ps("p_h0"), k.ps("p_h1")]
        R = k.ps("p_r")
        ROW = [k.ps(f"p_row{i}") for i in range(3)]
        raw_in, st = k.sems("s_raw", TG), k.sems("s_st", TG)
        x_in = [k.sems(f"s_x{w}_", TG) for w in range(2)]
        (passed_p, passed_v, staged, init, added, stat, mvr, vv, pw, ln, normed, turned, hi_out, lo_out, router_done, lg16_out,
         sums_done, dv, gap_done, tanh_done, comb_done, ct_done, ct_out, ce_done, h_done, gelu_done, scaled, hhi, hlo,
         unit_done, row_out, small_in, consts) = [
            k.sem("s_" + n) for n in ("passed_p", "passed_v", "staged", "init", "added", "stat", "mvr", "vv", "pw", "ln", "normed", "turned",
                                      "hi", "lo", "router", "lg16", "sums", "dv", "gap", "tanh", "comb", "ct", "ct_out",
                                      "ce", "h", "gelu", "scaled", "hhi", "hlo", "unit", "row", "small", "consts")]
        block = k.block()

        def groups(eng, body):
            body(0, 0, True, False)
            with eng.Fori(0, (NG - 4) // 2) as i:
                body(2 * i + 1, 1, False, False)
                body(2 * i + 2, 0, False, False)
            for g in range(NG - 3, NG):
                body(g, g % 2, False, g == NG - 1)

        def rows_of(g, t):
            if isinstance(g, int) and g == NG - 1:
                return bass.ds(N - GE + t * P, P)
            return bass.ds(g * GE + t * P, P)

        @block.sync
        def _(sp):
            def load(G, W, t):
                sp.dma_start(x1[:, W, t, :], a["x"][rows_of(G, t), :]).then_inc(x_in[W][t], 16)

            for t in range(TG):
                load(0, 0, t)
            sp.wait_ge(consts, 1)
            sp.dma_start(graw[:], a["L0_ffn_gate_w"].rearrange("(k p) e -> p k e", p=P)).then_inc(small_in, 16)
            for h in range(EXPERTS):
                sp.dma_start(b1[h * HR:(h + 1) * HR, :], a["L0_ffn_b1"][h, 0, :].rearrange("(m r) -> r m", r=HR),
                             allow_slow_non_contiguous=True).then_inc(small_in, 16)
            for n in range(3):
                sp.dma_start(b2raw[32 * n:32 * n + EXPERTS, :], a["L0_ffn_b2"][:, 0, :]).then_inc(small_in, 16)
            for n in (0, 2):
                sp.dma_start(spread_f[32 * n:32 * n + EXPERTS, :], s["headmap"][:]).then_inc(small_in, 16)
            for t in range(TG):
                load(1, 1, t)

            def body(g, w, more):
                if isinstance(g, int) and g == NG - 1:
                    for t in range(TG):
                        sp.wait_ge(st[t], 16 * (NG - 1))
                for t in range(TG):
                    sp.wait_ge(row_out, 8 * g + 2 * t + 2)
                    if more:
                        load(g + 2, w, t)
                    sp.dma_start(out[rows_of(g, t), :], res[:, t, :]).then_inc(st[t], 16)

            with sp.Fori(0, (NG - 4) // 2) as i:
                body(2 * i, 0, True)
                body(2 * i + 1, 1, True)
            for g in range(NG - 4, NG):
                body(g, g % 2, g + 2 < NG)
            for t in range(TG):
                sp.wait_ge(st[t], 16 * NG)

        @block.gpsimd
        def _(pool):
            pool.memset(b2raw[:], 0.0)
            pool.memset(spread_f[:], 0.0)
            for n, v in enumerate((-0.5, EPS, -1.0)):
                pool.memset(ln_const[:, 2 * n:2 * n + 2], v)
            pool.memset(cpad[:], 0.0)
            pool.iota(iota_i[:], [[1, EXPERTS]], base=0, channel_multiplier=0)
            pool.memset(sel[:], 0.0).then_inc(consts, 1)
            pool.wait_ge(consts, 1)
            pool.affine_select(out=sel[:], in_=sel[:], compare_op=ALU.not_equal, fill=1.0, base=0,
                               pattern=[[-1, EXPERTS]], channel_multiplier=1).then_inc(init, 1)
            pool.wait_ge(init, 1)
            pool.affine_select(out=sel[:], in_=sel[:], compare_op=ALU.not_equal, fill=1.0, base=-EXPERTS,
                               pattern=[[-1, EXPERTS]], channel_multiplier=1).then_inc(init, 1)

            def group(G, W):
                wait(pool, ln, 2 * G)
                pool.tensor_copy(stage[:, W, :], s["pnode"][:, bass.ds(TG * G, TG)]).then_inc(staged, 1)
                for t in range(TG):
                    wait(pool, turned, 8 * G - 8 + 2 * t + 2)
                    carried_wait(pool, passed_p, staged, G + 1)
                    pool.indirect_dma_start(raw[:, t, :], None, d["layer2"],
                                            bass.IndirectOffsetOnAxis(ap=stage[:, W, t:t + 1], axis=0)).then_inc(raw_in[t], 16)
                for u in range(2):
                    r = 2 * G + u
                    for t in (2 * u, 2 * u + 1):
                        pool.wait_ge(raw_in[t], 16 * G + 16)
                        pool.wait_ge(x_in[W][t], 8 * (G - W) + 16)
                        pool.tensor_tensor(x1[:, W, t, :], x1[:, W, t, :], raw[:, t, :], ALU.add).then_inc(added, 1)
                    pool.wait_ge(mvr, r + 1)
                    pool.tensor_tensor(rstd[:, u, :], mv[:, u, :, 1], ln_const[:, 2:4], ALU.add)
                    pool.tensor_tensor(nmr[:, u, :], mv[:, u, :, 0], ln_const[:, 4:6], ALU.mult).then_inc(vv, 1)
                    pool.wait_ge(vv, r + 1)
                    pool.tensor_tensor(rstd[:, u, :], rstd[:, u, :], ln_const[:, 0:2], ALU.pow).then_inc(pw, 1)
                    pool.wait_ge(pw, r + 1)
                    pool.tensor_tensor(nmr[:, u, :], nmr[:, u, :], rstd[:, u, :], ALU.mult).then_inc(ln, 1)

            group(0, 0)
            group(1, 1)
            with pool.Fori(1, NG // 2) as i:
                group(2 * i, 0)
                group(2 * i + 1, 1)

        @block.scalar
        def _(act):
            def normalise(G, W, t):
                act.wait_ge(ln, 2 * G + t // 2 + 1)
                act.activation(raw[:, t, :], x1[:, W, t, :], ACT.Identity, bias=nmr[:, t // 2, t % 2:t % 2 + 1],
                               scale=rstd[:, t // 2, t % 2:t % 2 + 1]).then_inc(normed, 1)

            def high(G, W, h):
                act.wait_ge(turned, 8 * G + h + 1)
                wait(act, h_done, 3 * G - 3)
                act.activation(xt[:, W, 0, 3 * (h % 2):3 * (h % 2) + 3, (h // 2) * P:(h // 2 + 1) * P],
                               T[h % 2][:, 0:3 * P].rearrange("p (k j) -> p k j", k=3), ACT.Copy).then_inc(hi_out, 1)

            def router_copy(G):
                act.wait_ge(router_done, G + 1)
                act.activation(lg16[:], R[0:2 * EXPERTS, :], ACT.Copy).then_inc(lg16_out, 1)

            def tanh(g):
                act.wait_ge(gap_done, g + 1)
                act.activation(gap[:], gap[:], ACT.Tanh, scale=0.5).then_inc(tanh_done, 1)

            def weights_copy(g):
                act.wait_ge(ct_done, g + 1)
                wait(act, unit_done, 8 * g)
                act.activation(ct[:], R[0:96, :], ACT.Copy).then_inc(ct_out, 1)

            def gelu(g, w, m):
                c = 3 * g + m
                act.wait_ge(h_done, c + 1)
                wait(act, hlo, 3 * g)
                act.activation(hid[:, m, :], H[(w + m) % 2][:], ACT.Gelu, bias=b1[:, m:m + 1]).then_inc(gelu_done, 1)

            def hidden_high(g, m):
                act.wait_ge(scaled, 3 * g + m + 1)
                wait(act, unit_done, 8 * g)
                act.activation(hs[:, 0, m, :], hid[:, m, :], ACT.Copy).then_inc(hhi, 1)

            for t in range(TG):
                normalise(0, 0, t)
                high(0, 0, 2 * t)
                high(0, 0, 2 * t + 1)
                if t == 1:
                    act.wait_ge(small_in, 16 * 14)
                    act.activation(gate[:, :, 0, :], graw[:], ACT.Copy)
                    act.activation(b2s[:], b2raw[:], ACT.Copy)
                    act.activation(spread_w[:], spread_f[:], ACT.Copy).then_inc(consts, 1)

            def body(g, w, first, last):
                router_copy(g)
                tanh(g)
                if not last:
                    normalise(g + 1, 1 - w, 0)
                gelu(g, w, 0)
                weights_copy(g)
                if not last:
                    normalise(g + 1, 1 - w, 1)
                gelu(g, w, 1)
                hidden_high(g, 0)
                if not last:
                    high(g + 1, 1 - w, 0)
                hidden_high(g, 1)
                gelu(g, w, 2)
                if not last:
                    high(g + 1, 1 - w, 1)
                hidden_high(g, 2)
                if not last:
                    high(g + 1, 1 - w, 2)
                    for t in (2, 3):
                        normalise(g + 1, 1 - w, t)
                    for h in range(3, 8):
                        high(g + 1, 1 - w, h)

            groups(act, body)

        @block.vector
        def _(dve):
            def moments(G, W, u):
                r = 2 * G + u
                wait(dve, normed, 4 * G - 4 + 2 * u + 2)
                for n in range(2):
                    t = 2 * u + n
                    dve.wait_ge(added, 4 * G + t + 1)
                    for h in range(2):
                        ins = dve.bn_stats(stats[:, u, n, h, :], x1[:, W, t, h * HALF:(h + 1) * HALF])
                ins.then_inc(stat, 1)
                carried_wait(dve, passed_v, stat, r + 1)
                dve.bn_aggr(mv[:, u, 0, :], stats[:, u, 0, :, :])
                dve.bn_aggr(mv[:, u, 1, :], stats[:, u, 1, :, :]).then_inc(mvr, 1)

            def low(G, W, h):
                dve.wait_ge(hi_out, 8 * G + h + 1)
                v = xt[:, W, :, 3 * (h % 2):3 * (h % 2) + 3, (h // 2) * P:(h // 2 + 1) * P]
                dve.tensor_tensor(v[:, 1], T[h % 2][:, 0:3 * P].rearrange("p (k j) -> p k j", k=3), v[:, 0].bitcast(F32),
                                  ALU.subtract).then_inc(lo_out, 1)

            DV = 8

            def best_two(g):
                n = [DV * g]

                def step(ins):
                    n[0] = n[0] + 1
                    ins.then_inc(dv, 1)
                    dve.wait_ge(dv, n[0])

                dve.wait_ge(sums_done, g + 1)
                step(dve.tensor_copy(lg[:], R[:, 0:TG * EXPERTS].rearrange("p (t e) -> p t e", e=EXPERTS)))
                dve.sem_inc(passed_v, 1)
                for t in range(TG):
                    ins = dve.max(top[:, t, :], lg[:, t, :])
                step(ins)
                dve.tensor_tensor(gap[:], top[:, :, 0], top[:, :, 1], ALU.subtract).then_inc(gap_done, 1)
                for t in range(TG):
                    ins = dve.max_index(top_i[:, t, :], top[:, t, :], lg[:, t, :])
                step(ins)
                step(dve.tensor_copy(top_f[:], top_i[:, :, 0:2]))
                for j in range(2):
                    ins = dve.tensor_tensor(onehot[:, j, :, :], iota_f[:].unsqueeze(1).broadcast_to([P, TG, EXPERTS]),
                                            top_f[:, :, j:j + 1].broadcast_to([P, TG, EXPERTS]), ALU.is_equal)
                step(ins)

            def combine(g):
                n = [DV * g + 5]

                def step(ins):
                    n[0] = n[0] + 1
                    ins.then_inc(dv, 1)
                    dve.wait_ge(dv, n[0])

                dve.wait_ge(tanh_done, g + 1)
                dve.tensor_scalar(wgt[:, 0, :], gap[:], 0.5, 0.5, ALU.mult, ALU.add)
                step(dve.tensor_scalar(wgt[:, 1, :], gap[:], -0.5, 0.5, ALU.mult, ALU.add))
                step(dve.tensor_tensor(onehot[:], onehot[:], wgt[:].unsqueeze(3).broadcast_to([P, 2, TG, EXPERTS]), ALU.mult))
                step(dve.tensor_tensor(comb[:], onehot[:, 0], onehot[:, 1], ALU.add))
                dve.tensor_copy(comb_hi[:], comb[:]).then_inc(comb_done, 1)
                dve.wait_ge(comb_done, 3 * g + 1)
                dve.tensor_copy(cpad[:, :, 0:2 * 32].rearrange("p t (n e) -> p t n e", n=2)[:, :, :, 0:EXPERTS],
                                comb_hi[:].bitcast(F32).unsqueeze(2).broadcast_to([P, TG, 2, EXPERTS])).then_inc(comb_done, 1)
                dve.tensor_tensor(cpad[:, :, 64:64 + EXPERTS], comb[:], comb_hi[:].bitcast(F32), ALU.subtract).then_inc(comb_done, 1)

            def scale(g, m):
                dve.wait_ge(ce_done, g + 1)
                dve.wait_ge(gelu_done, 3 * g + m + 1)
                dve.tensor_tensor(hid[:, m, :], hid[:, m, :], R[:], ALU.mult).then_inc(scaled, 1)

            def hidden_low(g, m):
                dve.wait_ge(hhi, 3 * g + m + 1)
                dve.tensor_tensor(hs[:, 1, m, :], hid[:, m, :], hs[:, 0, m, :].bitcast(F32), ALU.subtract).then_inc(hlo, 1)

            def residual(g, w, u):
                t, h = u // 2, u % 2
                dve.wait_ge(unit_done, 8 * g + u + 1)
                if h == 0:
                    wait(dve, st[t], 16 * g)
                cols = slice(h * HALF, (h + 1) * HALF)
                dve.tensor_tensor(res[:, t, cols], ROW[u % 3][:, 0:HALF], x1[:, w, t, cols], ALU.add).then_inc(row_out, 1)

            for u in range(2):
                moments(0, 0, u)
            for h in range(8):
                low(0, 0, h)
                if h == 3:
                    dve.wait_ge(consts, 2)
                    dve.tensor_tensor(gate[:, :, 1, :], graw[:], gate[:, :, 0, :].bitcast(F32), ALU.subtract)
                    dve.tensor_copy(iota_f[:], iota_i[:])
                    dve.tensor_tensor(b2s[32:32 + EXPERTS, :], b2raw[32:32 + EXPERTS, :], b2s[32:32 + EXPERTS, :].bitcast(F32),
                                      ALU.subtract).then_inc(consts, 1)
                    dve.wait_ge(consts, 3)
            moments(1, 1, 0)

            def body(g, w, first, last):
                best_two(g)
                combine(g)
                if not last:
                    moments(g + 1, 1 - w, 1)
                scale(g, 0)
                scale(g, 1)
                hidden_low(g, 0)
                if not last:
                    low(g + 1, 1 - w, 0)
                hidden_low(g, 1)
                scale(g, 2)
                if not last:
                    low(g + 1, 1 - w, 1)
                hidden_low(g, 2)
                if not last:
                    low(g + 1, 1 - w, 2)
                for u in range(8):
                    if not last and u < 5:
                        low(g + 1, 1 - w, 3 + u)
                    residual(g, w, u)
                if not (last or isinstance(g, int) and g == NG - 2):
                    moments(g + 2, w, 0)

            groups(dve, body)

        @block.tensor
        def _(pe):
            def turn(G, h):
                t = h // 2
                pe.wait_ge(normed, 4 * G + t + 1)
                wait(pe, lo_out, 8 * G + h - 1)
                for kk in range(3):
                    mm = pe.transpose(T[h % 2][:, kk * P:(kk + 1) * P],
                                      raw[:, t, (3 * (h % 2) + kk) * P:(3 * (h % 2) + kk + 1) * P], s["ident"][:])
                mm.then_inc(turned, 1)

            def router(G, W):
                pe.wait_ge(lo_out, 8 * G + 8)
                wait(pe, scaled, 3 * G)
                for kk in range(KC):
                    pe.matmul(R[0:2 * EXPERTS, :], gate[:, kk, :, :].rearrange("p n e -> p (n e)"), xt[:, W, 0, kk, :],
                              start=kk == 0, stop=False, skip_group_check=True)
                    mm = pe.matmul(R[0:EXPERTS, :], gate[:, kk, 0, :], xt[:, W, 1, kk, :], start=False,
                                   stop=kk == KC - 1, skip_group_check=True)
                mm.then_inc(router_done, 1)

            def sums(g):
                pe.wait_ge(lg16_out, g + 1)
                for t in range(TG):
                    mm = pe.matmul(R[:, t * EXPERTS:(t + 1) * EXPERTS], lg16[:, t * P:(t + 1) * P], sel[:],
                                   start=True, stop=True, skip_group_check=True)
                mm.then_inc(sums_done, 1)

            def weights_turn(g):
                pe.wait_ge(comb_done, 3 * g + 3)
                for t in range(TG):
                    mm = pe.transpose(R[0:96, t * P:(t + 1) * P], cpad[:, t, :], s["ident"][:])
                mm.then_inc(ct_done, 1)

            def weights_spread(g):
                pe.wait_ge(ct_out, g + 1)
                pe.matmul(R[:], spread_w[:], ct[:], start=True, stop=True).then_inc(ce_done, 1)

            def hidden(g, w, m, part):
                if part == 0:
                    wait(pe, gelu_done, 3 * g + m - 1)
                for kk in (range(0, 3), range(3, KC))[part]:
                    for i, (x, y) in enumerate(((0, 0), (1, 0), (0, 1))):
                        mm = pe.matmul(H[(w + m) % 2][:], s["f1"][:, x, kk, m * P:(m + 1) * P], xt[:, w, y, kk, :],
                                       start=kk == 0 and i == 0, stop=kk == KC - 1 and i == 2, skip_group_check=True)
                if part == 1:
                    mm.then_inc(h_done, 1)

            def unit(g, u, chunks):
                t, h = u // 2, u % 2
                cols = slice(h * HALF, (h + 1) * HALF)
                if 0 in chunks:
                    wait(pe, row_out, 8 * g + (u - 2 if u >= 3 else (-1, 0, 0)[u]))
                    pe.matmul(ROW[u % 3][:, 0:HALF], ct[:, t * P:(t + 1) * P], b2s[:, cols], start=True, stop=False,
                              skip_group_check=True)
                for m in chunks:
                    if u == 0:
                        pe.wait_ge(hlo, 3 * g + m + 1)
                    for i, (x, y) in enumerate(((0, 0), (1, 0), (0, 1))):
                        mm = pe.matmul(ROW[u % 3][:, 0:HALF], hs[:, x, m, t * P:(t + 1) * P], s["f2"][:, y, m, cols],
                                       start=False, stop=m == FC - 1 and i == 2, skip_group_check=True)
                if FC - 1 in chunks:
                    mm.then_inc(unit_done, 1)

            for h in range(8):
                turn(0, h)
            pe.wait_ge(consts, 3)
            pe.wait_ge(init, 2)
            router(0, 0)

            def body(g, w, first, last):
                hidden(g, w, 0, 0)
                sums(g)
                hidden(g, w, 0, 1)
                hidden(g, w, 1, 0)
                weights_turn(g)
                hidden(g, w, 1, 1)
                weights_spread(g)
                hidden(g, w, 2, 0)
                if not last:
                    turn(g + 1, 0)
                hidden(g, w, 2, 1)
                if not last:
                    turn(g + 1, 1)
                    turn(g + 1, 2)
                for u in range(3):
                    unit(g, u, range(0, FC - 1))
                for u in range(8):
                    unit(g, u, range(FC - 1, FC) if u < 3 else range(FC))
                    if not last and u < 5:
                        turn(g + 1, 3 + u)
                if not last:
                    router(g + 1, 1 - w)

            groups(pe, body)


def build(nc, *arrays):
    names = _INS
    a = dict(zip(names, arrays))
    out = arrays[len(names)]
    d = {
        "sorted_dst": nc.dram_tensor("sorted_dst", (EP + 2, 1), F32, kind="Internal").ap(),
        "masks": nc.dram_tensor("edge_masks", (2, EP), F32, kind="Internal").ap(),
        "node_pos": nc.dram_tensor("node_pos", (10240, 1), I32, kind="Internal").ap(),
        "layer1": nc.dram_tensor("layer1", (EP + 1, RW), F32, kind="Internal").ap(),
        "dst_logit": nc.dram_tensor("dst_logit", (EP + 1, 1), F32, kind="Internal").ap(),
        "layer2": nc.dram_tensor("layer2", (EP + 1, D), F32, kind="Internal").ap(),
    }
    with ExitStack() as ctx:
        s = persistent(Kit(nc, ctx))
        order_edges(nc, a, d, s)
        gat_layer_1(nc, a, d, s)
        experts_weights(s)
        gat_layer_2(nc, a, d, s)
        moe_ffn(nc, a, d, s, out)


_INS = ["x", "src", "dst", "L0_gnn_W1", "L0_gnn_a_src1", "L0_gnn_a_dst1", "L0_gnn_b1", "L0_gnn_W2", "L0_gnn_a_src2",
        "L0_gnn_a_dst2", "L0_gnn_b2", "L0_ffn_gate_w", "L0_ffn_w1", "L0_ffn_b1", "L0_ffn_w2", "L0_ffn_b2"]
_OUTS = [((N, D), "float32")]


def kernel(**inputs):
    import numpy as _np
    import concourse.bacc as _bacc
    from concourse import mybir as _mybir
    from concourse.bass_utils import run_bass_kernel_spmd as _run

    nc = _bacc.Bacc("TRN2", target_bir_lowering=False, num_devices=1)
    arrays, args = {}, []
    for name in _INS:
        arr = _np.ascontiguousarray(inputs[name])
        arrays[f"in_{name}_dram"] = arr
        args.append(nc.dram_tensor(f"in_{name}_dram", arr.shape, _mybir.dt.from_np(arr.dtype), kind="ExternalInput").ap())
    for i, (shape, dtype) in enumerate(_OUTS):
        dt = _mybir.dt.from_np(_np.dtype(dtype))
        args.append(nc.dram_tensor(f"out_{i}_dram", shape, dt, kind="ExternalOutput").ap())
    build(nc, *args)
    r = _run(nc, [arrays], core_ids=[0])
    return r.results[0]["out_0_dram"]
```

```python
from contextlib import ExitStack

import concourse.bass as bass
from concourse import mybir

ALU = mybir.AluOpType
ACT = mybir.ActivationFunctionType
AX = mybir.AxisListType
F32 = mybir.dt.float32
F32R = mybir.dt.float32r
BF16 = mybir.dt.bfloat16
I32 = mybir.dt.int32

P = 128
N, D = 10000, 768
E = 5000
KC = D // P
HEADS, HC = 8, 96
HR = P // HEADS
GE = 512
TG = GE // P
ET = -(-E // P)
EP = ET * P
EG = EP // GE
NG = -(-N // GE)
EXPERTS, HID = 8, 48
FH = EXPERTS * HID
FC = FH // P
HB = 80
HALF = D // 2
RW = D + 1
SLOPE = 0.2
EPS = 1e-5
BIG = 3e38
assert HB * P > N and EP % GE == 0 and FH % P == 0 and EXPERTS == HEADS and KC * HR == HC and FC * HR == HID


def wait(eng, sem, value):
    if isinstance(value, int) and value <= 0:
        return
    eng.wait_ge(sem, value)


def carried_wait(eng, passed, sem, value):
    eng.wait_ge(sem, value)
    eng.sem_inc(passed, 1)


class Kit:

    def __init__(self, nc, ctx, phase=""):
        self.nc, self.ctx, self.phase, self.made = nc, ctx, phase, []

    def sb(self, name, shape, dt=F32):
        return self.ctx.enter_context(self.nc.sbuf_tensor(self.phase + name, shape, dt))

    def ps(self, name, shape=(P, 512), dt=F32):
        return self.ctx.enter_context(self.nc.psum_tensor(self.phase + name, list(shape), dt))

    def sem(self, name):
        self.made.append(self.ctx.enter_context(self.nc.semaphore(self.phase + name)))
        return self.made[-1]

    def block(self, clear=False):
        if clear:
            self.ctx.callback(self.clear)
        return self.ctx.enter_context(self.nc.Block())

    def clear(self):
        with self.nc.Block() as block:
            @block.gpsimd
            def _(pool):
                for sem in self.made:
                    pool.sem_clear(sem)

    def sems(self, name, n):
        return [self.sem(f"{name}{i}") for i in range(n)]


def persistent(k):
    s = {}
    s["ident"] = k.sb("ident", [P, P])
    s["gidx"] = k.sb("gidx", [P, EG * 8], I32)
    s["pos"] = k.sb("pos", [P, EG * 8], I32)
    s["pnode"] = k.sb("pnode", [P, NG * TG], I32)
    s["v1"] = k.sb("v1", [P, 2, 2, KC, HEADS], F32R)
    s["v2"] = k.sb("v2", [P, KC, 2])
    s["b1col"] = k.sb("b1col", [P, KC])
    s["headmap"] = k.sb("headmap", [HEADS, P])
    s["w1s"] = k.sb("w1s", [P, 2, KC, D], F32R)
    return s


def experts_weights(s):
    s["f1"] = s["w1s"][:, 0].rearrange("p k (a n) -> p a k n", a=2)
    s["f2"] = s["w1s"][:, 1].rearrange("p (a k) n -> p a k n", a=2)


def order_edges(nc, a, d, s):
    with ExitStack() as ctx:
        k = Kit(nc, ctx, "o_")
        key = k.sb("key", [P, EP])
        node_oh = k.sb("node_oh", [HB, EP])
        above = k.sb("above", [HB, EP // 4])
        oh_lo = k.sb("oh_lo", [P, ET, P], BF16)
        dst_hi = k.sb("dst_hi", [P, ET, HB], BF16)
        oh_hi = k.sb("oh_hi", [P, ET, 4, ET], BF16)
        junk = k.sb("junk", [P, 4, 2 * P])
        wraw = k.sb("wraw", [P, KC, D])
        w2raw = k.sb("w2raw", [P, KC, D])
        prod = k.sb("prod", [P, KC, D])
        avec = k.sb("avec", [P, 4, D])
        col_i = k.sb("col_i", [P, 2, ET], I32)
        dst_f = k.sb("dst_f", [P, ET])
        iota_i = k.sb("iota_i", [P, P], I32)
        iota_f = k.sb("iota_f", [P, P])
        rowp_i = k.sb("rowp_i", [P, 1], I32)
        row_start = k.sb("row_start", [P, 2])
        before = k.sb("before", [P, 2 * P])
        rows_before = k.sb("rows_before", [HB, HB])
        ones = k.sb("ones", [HB, P])
        count = k.sb("count", [HB, P])
        total = k.sb("total", [HB, P])
        offset = k.sb("offset", [HB, 1])
        first = k.sb("first", [HB, P])
        table = k.sb("table", [HB, 2, P])
        last = k.sb("last", [HB, 3, P])
        last_i = k.sb("last_i", [HB, P], I32)
        own = k.sb("own", [P, ET])
        other = k.sb("other", [P, ET])
        rank_i = k.sb("rank_i", [P, 3, ET], I32)
        part_i = k.sb("part_i", [P, 4, ET], I32)
        part_f = k.sb("part_f", [P, 4, ET])
        hl_f = k.sb("hl_f", [P, 2, ET])
        ohr = k.sb("ohr", [P, ET, ET])
        sorted4 = k.sb("sorted4", [P, 4, ET])
        col_f = k.sb("col_f", [P, 2, ET])
        clip_f = k.sb("clip_f", [P, ET])
        dst_row = k.sb("dst_row", [ET, P])
        window = k.sb("window", [ET, P + 2])
        eq = k.sb("eq", [ET, P])
        masks = k.sb("masks", [ET, 2, P])
        edge_f = k.sb("edge_f", [1, 2])
        v_f = k.sb("v_f", [P, 2, KC, HEADS])
        p_sort, p_row, p_count, p_run, p_off = [k.ps("p_" + n) for n in ("sort", "row", "count", "run", "off")]
        p_got = [k.ps("p_got0"), k.ps("p_got1")]
        (s_key, s_col, s_w1, s_av, s_w2, s_b, s_iota, s_prep, s_dve, s_oh, s_sorted, s_row, s_rowst, s_win, s_maskst,
         s_pn, s_prod, s_red, s_split, s_id, s_vec, s_hm, s_edge, s_onehot, s_count, s_node, s_total, s_off, s_first,
         s_run, s_table, s_got, s_read, s_last, s_tri, s_own) = [
            k.sem("s_" + n) for n in ("key", "col", "w1", "av", "w2", "b", "iota", "prep", "dve", "oh", "sorted", "row",
                                      "rowst", "win", "maskst", "pn", "prod", "red", "split", "id", "vec", "hm", "edge",
                                      "onehot", "count", "node", "total", "off", "first", "run", "table", "got", "read",
                                      "last", "tri", "own")]
        block = k.block(clear=True)

        full = (E // P) * P

        @block.sync
        def _(sp):
            sp.wait_ge(s_prep, 1)
            for n, v in enumerate((a["src"], a["dst"])):
                sp.dma_start(col_i[:, n, 0:E // P], v[0:full].rearrange("(t p) -> p t", p=P), allow_slow_non_contiguous=True).then_inc(s_col, 16)
                sp.dma_start(col_i[0:E - full, n, E // P:ET],
                             v[full:E].rearrange("(p o) -> p o", o=1), allow_slow_non_contiguous=True).then_inc(s_col, 16)
            sp.dma_start(key[:, 0:E].bitcast(I32), a["dst"].partition_broadcast(P)).then_inc(s_key, 16)
            sp.dma_start(wraw[:], a["L0_gnn_W1"].rearrange("(k p) n -> p k n", p=P)).then_inc(s_w1, 16)
            for n, name in enumerate(("a_src1", "a_dst1", "a_src2", "a_dst2")):
                sp.dma_start(avec[:, n, :], a["L0_gnn_" + name].rearrange("h c -> (h c)").partition_broadcast(P)).then_inc(s_av, 16)
            for h in range(HEADS):
                sp.dma_start(w2raw[h * HR:(h + 1) * HR, :, :],
                             a["L0_gnn_W2"][h * HC:(h + 1) * HC, :].rearrange("(m r) n -> r m n", r=HR)).then_inc(s_w2, 16)
                sp.dma_start(s["b1col"][h * HR:(h + 1) * HR, :],
                             a["L0_gnn_b1"][h * HC:(h + 1) * HC].rearrange("(m r) -> r m", r=HR), allow_slow_non_contiguous=True).then_inc(s_b, 16)
            sp.wait_ge(s_edge, 1)
            sp.dma_start(d["sorted_dst"][0:1, :], edge_f[0:1, 0:1]).then_inc(s_rowst, 16)
            sp.dma_start(d["sorted_dst"][EP + 1:EP + 2, :], edge_f[0:1, 1:2]).then_inc(s_rowst, 16)
            sp.wait_ge(s_last, 2)
            sp.dma_start(d["node_pos"].rearrange("(q j) o -> q (j o)", j=P), last_i[:]).then_inc(s_pn, 16)
            sp.wait_ge(s_pn, 16)
            sp.dma_start(s["pnode"][:, (NG - 1) * TG:NG * TG],
                         d["node_pos"][N - GE:N, :].rearrange("(t p) o -> p (t o)", p=P), allow_slow_non_contiguous=True).then_inc(s_pn, 16)
            sp.wait_ge(s_row, 2)
            sp.dma_start(d["sorted_dst"][1:EP + 1, :].rearrange("(t j) o -> t (j o)", j=P), dst_row[:]).then_inc(s_rowst, 16)
            sp.wait_ge(s_rowst, 48)
            sp.dma_start(window[:], bass.AP(d["sorted_dst"].tensor, 0, [[P, ET], [1, P + 2]])).then_inc(s_win, 16)
            sp.wait_ge(s_maskst, 1)
            for n in range(2):
                sp.dma_start(d["masks"][n, :].rearrange("(t j) -> t j", j=P), masks[:, n, :]).then_inc(s_maskst, 16)
            sp.wait_ge(s_pn, 32)
            sp.wait_ge(s_maskst, 33)
            sp.wait_ge(s_b, 16 * HEADS)

        @block.gpsimd
        def _(pool):
            pool.memset(col_i[:, 0, ET - 1:ET], 0)
            pool.memset(col_i[:, 1, ET - 1:ET], N).then_inc(s_prep, 1)
            pool.iota(iota_i[:], [[1, P]], base=0, channel_multiplier=0)
            pool.iota(rowp_i[:], [[1, 1]], base=0, channel_multiplier=1).then_inc(s_iota, 1)
            pool.memset(edge_f[:], -1.0).then_inc(s_edge, 1)
            pool.memset(s["ident"][:], 0.0).then_inc(s_id, 1)
            pool.wait_ge(s_id, 1)
            pool.affine_select(out=s["ident"][:], in_=s["ident"][:], compare_op=ALU.not_equal, fill=1.0, base=0,
                               pattern=[[-1, P]], channel_multiplier=1).then_inc(s_id, 1)
            pool.memset(ones[:], 1.0)
            pool.memset(before[:], 1.0)
            pool.memset(rows_before[:], 1.0)
            pool.memset(s["headmap"][:], 1.0).then_inc(s_hm, 1)
            pool.wait_ge(s_hm, 1)
            pool.affine_select(out=before[:], in_=before[:], compare_op=ALU.is_ge, fill=0.0, base=P - 1,
                               pattern=[[-1, 2 * P]], channel_multiplier=1)
            pool.affine_select(out=rows_before[:], in_=rows_before[:], compare_op=ALU.is_ge, fill=0.0, base=-1,
                               pattern=[[1, HB]], channel_multiplier=-1).then_inc(s_tri, 1)
            pool.affine_select(out=s["headmap"][:], in_=s["headmap"][:], compare_op=ALU.is_ge, fill=0.0, base=0,
                               pattern=[[1, P]], channel_multiplier=-HR).then_inc(s_hm, 1)
            pool.wait_ge(s_hm, 2)
            pool.affine_select(out=s["headmap"][:], in_=s["headmap"][:], compare_op=ALU.is_ge, fill=0.0, base=HR - 1,
                               pattern=[[-1, P]], channel_multiplier=HR).then_inc(s_hm, 1)
            pool.wait_ge(s_av, 64)
            for n in range(4):
                if n == 0:
                    pool.wait_ge(s_w1, 16)
                if n == 2:
                    pool.wait_ge(s_w2, 16 * HEADS)
                if n >= 1:
                    pool.wait_ge(s_red, n)
                w = wraw if n < 2 else w2raw
                pool.tensor_tensor(prod[:], w[:], avec[:, n, :].unsqueeze(1).broadcast_to([P, KC, D]),
                                   ALU.mult).then_inc(s_prod, 1)

        @block.vector
        def _(dve):
            n_done = [0]

            def step(ins):
                n_done[0] += 1
                ins.then_inc(s_dve, 1)
                dve.wait_ge(s_dve, n_done[0])

            def fold(n):
                dve.wait_ge(s_prod, n + 1)
                dve.tensor_reduce(v_f[:, n, :, :].rearrange("p k h -> p (k h)"),
                                  prod[:].rearrange("p k (h c) -> p (k h) c", c=HC), AX.X, ALU.add).then_inc(s_red, 1)

            dve.wait_ge(s_iota, 1)
            dve.tensor_copy(iota_f[:], iota_i[:])
            step(dve.tensor_copy(row_start[:, 0:1], rowp_i[:]))
            step(dve.tensor_scalar(row_start[:, 0:1], row_start[:, 0:1], float(P), None, ALU.mult))
            dve.tensor_scalar(row_start[:, 1:2], row_start[:, 0:1], float(P), None, ALU.add)
            dve.memset(key[:, E:EP], float(N))
            dve.wait_ge(s_col, 64)
            dve.tensor_copy(dst_f[:], col_i[:, 1, :])
            for n in range(2):
                dve.tensor_scalar(part_i[:, 2 * n, :], col_i[:, n, :], 7, None, ALU.logical_shift_right)
                ins = dve.tensor_scalar(part_i[:, 2 * n + 1, :], col_i[:, n, :], P - 1, None, ALU.bitwise_and)
            step(ins)
            step(dve.tensor_copy(part_f[:], part_i[:]))
            dve.tensor_tensor(dst_hi[:], iota_f[:, 0:HB].unsqueeze(1).broadcast_to([P, ET, HB]),
                              part_f[:, 2, :].unsqueeze(2).broadcast_to([P, ET, HB]), ALU.is_equal)
            dve.tensor_tensor(oh_lo[:], iota_f[:].unsqueeze(1).broadcast_to([P, ET, P]),
                              part_f[:, 3, :].unsqueeze(2).broadcast_to([P, ET, P]), ALU.is_equal).then_inc(s_onehot, 1)
            dve.wait_ge(s_key, 16)
            step(dve.tensor_copy(key[:, 0:E], key[:, 0:E].bitcast(I32)))
            for c in range(4):
                cols = slice(c * (EP // 4), (c + 1) * (EP // 4))
                step(dve.tensor_scalar(above[:], key[0:HB, cols], row_start[0:HB, 0:1], None, ALU.is_ge))
                step(dve.scalar_tensor_tensor(node_oh[:, cols], key[0:HB, cols], row_start[0:HB, 1:2], above[:], ALU.is_lt,
                                              ALU.mult))
            dve.sem_inc(s_node, 1)
            dve.wait_ge(s_tri, 1)
            dve.wait_ge(s_count, 1)
            step(dve.tensor_copy(count[:], p_count[0:HB, 0:P]))
            dve.tensor_tensor_scan(total[:], ones[:], count[:], 0.0, ALU.mult, ALU.add).then_inc(s_total, 1)
            dve.wait_ge(s_off, 1)
            dve.wait_ge(s_total, 1)
            step(dve.tensor_copy(offset[:], p_off[0:HB, 1:2]))
            dve.scalar_tensor_tensor(first[:], total[:], offset[:, 0:1], count[:], ALU.add, ALU.subtract).then_inc(s_first, 1)
            dve.tensor_scalar(last[:, 0, :], count[:], 0.5, None, ALU.is_ge)
            step(dve.tensor_scalar(last[:, 1, :], total[:], offset[:, 0:1], -1.0 - EP, ALU.add, ALU.add))
            step(dve.tensor_tensor(last[:, 2, :], last[:, 0, :], last[:, 1, :], ALU.mult))
            dve.tensor_scalar(last[:, 1, :], last[:, 2, :], float(EP), None, ALU.add).then_inc(s_last, 1)
            dve.wait_ge(s_last, 1)
            dve.tensor_copy(last_i[:], last[:, 1, :]).then_inc(s_last, 1)
            fold(0)
            for t in range(ET):
                if t == ET // 2:
                    fold(1)
                skip = (1 - t % 2) * P
                wait(dve, s_own, t - 1)
                dve.scalar_tensor_tensor(junk[:, t % 2, skip:2 * P], key[:, (t - t % 2) * P:(t + 1) * P], dst_f[:, t:t + 1],
                                         before[:, skip:2 * P], ALU.is_equal, ALU.mult,
                                         accum_out=own[:, t:t + 1]).then_inc(s_own, 1)
                wait(dve, s_read, t - 1)
                dve.wait_ge(s_got, t + 1)
                dve.scalar_tensor_tensor(junk[:, 2 + t % 2, 0:P], iota_f[:], part_f[:, 3, t:t + 1], p_got[t % 2][:, 0:P],
                                         ALU.is_equal, ALU.mult, accum_out=other[:, t:t + 1]).then_inc(s_read, 1)
            dve.wait_ge(s_own, ET)
            dve.wait_ge(s_read, ET)
            step(dve.tensor_tensor(rank_i[:, 0, :], own[:], other[:], ALU.add))
            dve.tensor_scalar(rank_i[:, 1, :], rank_i[:, 0, :], 7, None, ALU.logical_shift_right)
            step(dve.tensor_scalar(rank_i[:, 2, :], rank_i[:, 0, :], P - 1, None, ALU.bitwise_and))
            step(dve.tensor_copy(hl_f[:], rank_i[:, 1:3, :]))
            dve.tensor_tensor(oh_lo[:], iota_f[:].unsqueeze(1).broadcast_to([P, ET, P]),
                              hl_f[:, 1, :].unsqueeze(2).broadcast_to([P, ET, P]), ALU.is_equal)
            step(dve.tensor_tensor(ohr[:], iota_f[:, 0:ET].unsqueeze(1).broadcast_to([P, ET, ET]),
                                   hl_f[:, 0, :].unsqueeze(2).broadcast_to([P, ET, ET]), ALU.is_equal))
            for n in range(4):
                ins = dve.tensor_tensor(oh_hi[:, :, n, :], ohr[:],
                                        part_f[:, n, :].unsqueeze(2).broadcast_to([P, ET, ET]), ALU.mult)
            ins.then_inc(s_oh, 1)
            dve.wait_ge(s_sorted, 1)
            step(dve.tensor_copy(sorted4[:], p_sort[:, 0:4 * ET].rearrange("p (n t) -> p n t", t=ET)))
            for n in range(2):
                ins = dve.scalar_tensor_tensor(col_f[:, n, :], sorted4[:, 2 * n, :], float(P), sorted4[:, 2 * n + 1, :],
                                               ALU.mult, ALU.add)
            step(ins)
            dve.tensor_scalar(clip_f[:], col_f[:, 1, :], float(N - 1), None, ALU.min).then_inc(s_vec, 1)
            dve.wait_ge(s_vec, 1)
            gi = s["gidx"][:].rearrange("p (g n j) -> p g n j", n=2, j=TG)
            dve.tensor_copy(gi[:, :, 1, :], col_f[:, 0, :].rearrange("p (g j) -> p g j", j=TG))
            dve.tensor_copy(gi[:, :, 0, :], clip_f[:].rearrange("p (g j) -> p g j", j=TG))
            dve.wait_ge(s_row, 1)
            dve.tensor_copy(dst_row[:], p_row[0:ET, 0:P]).then_inc(s_row, 1)
            dve.tensor_copy(s["pnode"][:, 0:(NG - 1) * TG], p_count[:, 0:(NG - 1) * TG])
            step(dve.tensor_copy(s["v1"][:, :, 0, :, :], v_f[:]))
            dve.tensor_tensor(s["v1"][:, :, 1, :, :], v_f[:], s["v1"][:, :, 0, :, :].bitcast(F32), ALU.subtract)
            dve.wait_ge(s_split, 1)
            for kk in range(KC):
                dve.tensor_tensor(s["w1s"][:, 1, kk, :].rearrange("p (m h r) -> p m h r", h=HEADS, r=HR),
                                  wraw[:, kk, :].rearrange("p (h m r) -> p m h r", h=HEADS, r=HR),
                                  s["w1s"][:, 0, kk, :].bitcast(F32).rearrange("p (m h r) -> p m h r", h=HEADS, r=HR),
                                  ALU.subtract)
            dve.wait_ge(s_win, 16)
            step(dve.tensor_tensor(eq[:], window[:, 1:P + 1], window[:, 0:P], ALU.is_equal))
            dve.tensor_scalar(masks[:, 0, :], eq[:], 0.5, BIG, ALU.subtract, ALU.mult)
            dve.tensor_scalar(masks[:, 1, :], eq[:], 1.0, 1e30, ALU.subtract, ALU.mult).then_inc(s_maskst, 1)

        @block.tensor
        def _(pe):
            pe.wait_ge(s_onehot, 1)
            for t in range(ET):
                mm = pe.matmul(p_count[0:HB, 0:P], dst_hi[:, t, :], oh_lo[:, t, :], start=(t == 0), stop=(t == ET - 1))
            mm.then_inc(s_count, 1)
            pe.wait_ge(s_tri, 1)
            pe.wait_ge(s_total, 1)
            pe.matmul(p_off[0:HB, 0:2], rows_before[:], total[:, P - 2:P], start=True, stop=True).then_inc(s_off, 1)
            pe.wait_ge(s_id, 2)
            pe.wait_ge(s_first, 1)
            pe.matmul(p_run[0:HB, 0:P], s["ident"][0:HB, 0:HB], first[:], start=True, stop=False,
                      skip_group_check=True).then_inc(s_run, 1)
            pe.wait_ge(s_node, 1)
            for u in range(ET // 2):
                pe.wait_ge(s_table, u + 1)
                for t in (2 * u, 2 * u + 1):
                    mm = pe.matmul(p_run[0:HB, 0:P], dst_hi[:, t, :], oh_lo[:, t, :], start=False, stop=(t == ET - 1),
                                   skip_group_check=True)
                mm.then_inc(s_run, 1)
                for t in (2 * u, 2 * u + 1):
                    if t >= 2:
                        pe.wait_ge(s_read, t - 1)
                    pe.matmul(p_got[t % 2][:, 0:P], node_oh[:, t * P:(t + 1) * P], table[:, u % 2, :], start=True,
                              stop=True).then_inc(s_got, 1)
            pe.wait_ge(s_last, 2)
            pe.transpose(p_count[:, 0:HB], last[:, 1, :], s["ident"][0:HB, 0:HB])
            pe.wait_ge(s_oh, 1)
            for t in range(ET):
                mm = pe.matmul(p_sort[:, 0:4 * ET], oh_lo[:, t, :], oh_hi[:, t, :, :], start=(t == 0), stop=(t == ET - 1))
            mm.then_inc(s_sorted, 1)
            pe.wait_ge(s_vec, 1)
            pe.transpose(p_row[0:ET, 0:P], col_f[:, 1, :], s["ident"][:]).then_inc(s_row, 1)

        @block.scalar
        def _(act):
            act.wait_ge(s_w1, 16)
            for kk in range(KC):
                hi = act.activation(s["w1s"][:, 0, kk, :].rearrange("p (m h r) -> p m h r", h=HEADS, r=HR),
                                    wraw[:, kk, :].rearrange("p (h m r) -> p m h r", h=HEADS, r=HR), ACT.Copy)
            hi.then_inc(s_split, 1)
            for u in range(ET // 2):
                act.wait_ge(s_run, u + 1)
                wait(act, s_got, 2 * u - 2)
                act.activation(table[:, u % 2, :], p_run[0:HB, 0:P], ACT.Copy).then_inc(s_table, 1)
            for n in range(2):
                act.wait_ge(s_prod, n + 3)
                for kk in range(KC):
                    ins = act.activation(prod[:, kk, :], prod[:, kk, :], ACT.Copy, accum_out=s["v2"][:, kk, n:n + 1])
                ins.then_inc(s_red, 1)


def softmax_steps(dve, b, sem, g, np_, mask, mask_in, x_read):
    def first():
        dve.wait_ge(*mask_in)
        dve.wait_ge(sem["e_out"], g + 1)
        if sem["carry"](g):
            wait(dve, sem["z"], g)
            dve.tensor_copy(b["m"][:, 0:1], b["m"][:, GE:GE + 1])
        dve.scalar_tensor_tensor(b["e"][:], b["e"][:], SLOPE, b["e"][:], ALU.mult, ALU.max).then_inc(sem["lrelu"], 1)
        dve.wait_ge(sem["lrelu"], g + 1)
        dve.tensor_tensor_scan(b["m"][:, 1:GE + 1], mask[:, 0, :], b["e"][:], b["m"][:, 0:1],
                               ALU.min, ALU.max).then_inc(sem["m"], 1)
        dve.wait_ge(sem["m"], g + 1)
        wait(dve, *x_read)
        dve.tensor_tensor(b["x"][:, 1, :], b["e"][:], b["m"][:, 1:GE + 1], ALU.subtract)
        dve.tensor_tensor(b["x"][:, 0, :], b["m"][:, 0:GE], b["m"][:, 1:GE + 1], ALU.subtract).then_inc(sem["diff"], 1)
        dve.wait_ge(sem["diff"], g + 1)
        dve.scalar_tensor_tensor(b["x"][:, 0, :], b["x"][:, 0, :], 0.0, mask[:, 1, :], ALU.min,
                                 ALU.add).then_inc(sem["x"], 1)

    def second():
        dve.wait_ge(sem["exp"], g + 1)
        if sem["carry"](g):
            dve.tensor_copy(b["z"][:, 0:1], b["z"][:, GE:GE + 1]).then_inc(sem["zc"], 1)
            dve.wait_ge(sem["zc"], g)
        dve.tensor_tensor_scan(b["z"][:, 1:GE + 1], b["x"][:, 0, :], b["x"][:, 1, :], b["z"][:, 0:1],
                               ALU.mult, ALU.add).then_inc(sem["z"], 1)
        dve.wait_ge(sem["z"], g + 1)
        dve.tensor_tensor(b["x"][:, 0, :], b["x"][:, 0, :], b["z"][:, 0:GE], ALU.mult)
        dve.tensor_scalar(b["r"][:], b["z"][:, 1:GE + 1], 1e-16, None, ALU.add).then_inc(sem["zz"], 1)
        dve.wait_ge(sem["zz"], g + 1)
        dve.reciprocal(b["r"][:], b["r"][:]).then_inc(sem["rz"], 1)
        dve.wait_ge(sem["rz"], g + 1)
        dve.tensor_tensor(b["x"][:], b["x"][:], b["r"][:].unsqueeze(1).broadcast_to([np_, 2, GE]),
                          ALU.mult).then_inc(sem["ab"], 1)

    return first, second


def softmax_kit(k, np_):
    b = {"m": k.sb("run_max", [np_, GE + 1]), "z": k.sb("run_sum", [np_, GE + 1]), "e": k.sb("logit", [np_, GE]),
         "x": k.sb("expo", [np_, 2, GE]), "r": k.sb("rcp", [np_, GE])}
    sem = {n: k.sem("s_sm_" + n) for n in ("e_out", "lrelu", "m", "diff", "x", "exp", "zc", "z", "zz", "rz", "ab")}
    return b, sem


def gat_layer_1(nc, a, d, s):
    with ExitStack() as ctx:
        k = Kit(nc, ctx, "a_")
        xt = k.sb("xt", [P, 2, 2, KC, GE], F32R)
        xd = k.sb("xd", [P, 2, KC, 2 * P], F32R)
        raw = k.sb("raw", [P, 8, D])
        msg = k.sb("msg", [P, 2, GE])
        agg = k.sb("agg", [P, 2, GE])
        pos_part = k.sb("pos_part", [P, 2, GE])
        neg_part = k.sb("neg_part", [P, 2, GE])
        g1 = k.sb("g1", [P, 2, GE])
        rows = k.sb("rows", [P, 2, TG, P])
        ab = k.sb("ab", [P, 2, 2, GE])
        carry = k.sb("carry", [P, KC])
        mask = k.sb("mask", [HEADS, 2, 2, GE])
        b, sem = softmax_kit(k, HEADS)
        stage = k.sb("stage", [P, 8], I32)
        pstage = k.sb("pstage", [P, 8], I32)
        stats = k.sb("stats", [P, 2, 2, 2, 6])
        mv = k.sb("mv", [P, 2, 2, 2])
        rstd = k.sb("rstd", [P, 2, 2])
        nmr = k.sb("nmr", [P, 2, 2])
        consts = k.sb("consts", [P, 6])
        logit2 = k.sb("logit2", [P, TG, 2])
        bdef = k.sb("bdef", [P, 3, KC])
        ldef = k.sb("ldef", [1, 2])
        negb = k.sb("negb", [P, KC])
        bm1 = k.sb("bm1", [P, KC])
        T = [k.ps("p_t0"), k.ps("p_t1")]
        H = [k.ps("p_h0"), k.ps("p_h1")]
        LG, EX, AS, RO = k.ps("p_lg"), k.ps("p_ex"), k.ps("p_as"), k.ps("p_ro")
        raw_in, st, mask_in = k.sems("s_raw", 8), k.sems("s_st", 2), k.sems("s_mask", 2)
        (pos_ready, passed_p, passed_v, pos_in, staged, stat, mvr, vv, pw, ln, normed, turned, hi_out, lo_out, dlog, lg_done, ab_ex, ab_out,
         h_done, msg_done, agg_done, car, neg_done, elu_done, g_done, tail_done, rows_out, as_done, as_out, st_as,
         dflt, init) = [
            k.sem("s_" + n) for n in ("pos_ready", "passed_p", "passed_v", "pos_in", "staged", "stat", "mvr", "vv",
                                      "pw", "ln", "normed", "turned", "hi_out", "lo_out", "dlog", "lg_done",
                                      "ab_ex", "ab_out", "h_done", "msg_done", "agg_done", "car", "neg_done",
                                      "elu_done", "g_done", "tail_done", "rows_out", "as_done", "as_out", "st_as",
                                      "dflt", "init")]
        sem["carry"] = lambda g: not (isinstance(g, int) and g == 0)
        block = k.block()

        def groups(eng, body):
            body(0, 0, True, True)
            with eng.Fori(0, (EG - 4) // 2) as i:
                body(2 * i + 1, 1, True, True)
                body(2 * i + 2, 0, True, True)
            body(EG - 3, (EG - 3) % 2, True, True)
            body(EG - 2, EG % 2, True, False)
            body(EG - 1, (EG - 1) % 2, False, False)

        @block.gpsimd
        def _(pool):
            for n, v in enumerate((-0.5, EPS, -1.0)):
                pool.memset(consts[:, 2 * n:2 * n + 2], v)
            pool.memset(b["m"][:, 0:1], 0.0)
            pool.memset(b["z"][:, 0:1], 0.0)
            pool.memset(carry[:], 0.0).then_inc(init, 1)
            pool.wait_ge(init, 1)

            def gather(G, u):
                for j in (2 * u, 2 * u + 1):
                    q = 8 * G + j
                    wait(pool, turned, 2 * q - 14)
                    pool.tensor_copy(stage[:, j:j + 1], s["gidx"][:, bass.ds(q, 1)]).then_inc(staged, 1)
                    carried_wait(pool, passed_p, staged, q + 1)
                    pool.indirect_dma_start(raw[:, j, :], None, a["x"],
                                            bass.IndirectOffsetOnAxis(ap=stage[:, j:j + 1], axis=0)).then_inc(raw_in[j], 16)
                    pool.indirect_dma_start(pstage[:, j:j + 1], None, d["node_pos"],
                                            bass.IndirectOffsetOnAxis(ap=stage[:, j:j + 1], axis=0)).then_inc(pos_in, 16)

            def positions(G):
                pool.wait_ge(pos_in, 128 * G + 128)
                pool.tensor_copy(s["pos"][:, bass.ds(8 * G, 8)], pstage[:]).then_inc(init, 1)
                pool.wait_ge(init, G + 2)

            def deviations(G, u):
                r, w = 4 * G + u, u % 2
                pool.wait_ge(mvr, r + 1)
                pool.tensor_tensor(rstd[:, w, :], mv[:, w, :, 1], consts[:, 2:4], ALU.add)
                pool.tensor_tensor(nmr[:, w, :], mv[:, w, :, 0], consts[:, 4:6], ALU.mult).then_inc(vv, 1)
                pool.wait_ge(vv, r + 1)
                pool.tensor_tensor(rstd[:, w, :], rstd[:, w, :], consts[:, 0:2], ALU.pow).then_inc(pw, 1)
                pool.wait_ge(pw, r + 1)
                pool.tensor_tensor(nmr[:, w, :], nmr[:, w, :], rstd[:, w, :], ALU.mult).then_inc(ln, 1)

            def join(g, m):
                c = 6 * g + m
                wait(pool, tail_done, c - 1)
                pool.wait_ge(pos_ready, c + 1)
                pool.wait_ge(elu_done, c + 1)
                pool.tensor_tensor(g1[:, m % 2, :], neg_part[:, m % 2, :], pos_part[:, m % 2, :], ALU.add).then_inc(g_done, 1)

            gather(0, 0)
            gather(0, 1)
            deviations(0, 0)
            gather(0, 2)
            deviations(0, 1)
            gather(0, 3)
            deviations(0, 2)
            positions(0)
            deviations(0, 3)
            gather(1, 0)
            gather(1, 1)
            deviations(1, 0)
            gather(1, 2)
            deviations(1, 1)
            gather(1, 3)
            positions(1)

            def body(g, w, nxt, chain):
                for m in range(6):
                    if not (isinstance(g, int) and g == 0 and m == 0):
                        join(g if m else g - 1, (m - 1) % 6)
                    if nxt and m < 2:
                        deviations(g + 1, m + 2)
                    if chain and m == 4:
                        deviations(g + 2, 0)
                        deviations(g + 2, 1)
                    if chain and 1 <= m <= 4:
                        gather(g + 2, m - 1)
                    if chain and m == 5:
                        positions(g + 2)

            groups(pool, body)
            join(EG - 1, 5)

        @block.sync
        def _(sp):
            def mask_load(g, w):
                wait(sp, sem["ab"], g - 1)
                sp.dma_start(mask[:, w, :, :], d["masks"][:, bass.ds(g * GE, GE)].partition_broadcast(HEADS)).then_inc(mask_in[w], 16)

            def row_store(g, m):
                c = 6 * g + m
                sp.wait_ge(rows_out, c + 1)
                sp.dma_start(d["layer1"][bass.ds(g * GE, GE), m * P:(m + 1) * P].rearrange("(t p) j -> p t j", p=P),
                             rows[:, m % 2, :, :]).then_inc(st[m % 2], 16)

            def logit_store(g):
                sp.wait_ge(as_out, g + 1)
                sp.dma_start(d["layer1"][bass.ds(g * GE, GE), D:D + 1].rearrange("(t p) o -> p t o", p=P), logit2[:, :, 0:1],
                             allow_slow_non_contiguous=True).then_inc(st_as, 16)
                sp.dma_start(d["dst_logit"][bass.ds(g * GE, GE), :].rearrange("(t p) o -> p t o", p=P), logit2[:, :, 1:2],
                             allow_slow_non_contiguous=True).then_inc(st_as, 16)

            mask_load(0, 0)
            mask_load(1, 1)
            sp.wait_ge(dflt, 5)
            sp.dma_start(d["layer1"][EP:EP + 1, 0:D].rearrange("o (m p) -> p (o m)", p=P), bdef[:, 0, :], allow_slow_non_contiguous=True).then_inc(dflt, 16)
            sp.dma_start(d["layer1"][EP:EP + 1, D:D + 1], ldef[:, 0:1]).then_inc(dflt, 16)
            sp.dma_start(d["dst_logit"][EP:EP + 1, :], ldef[:, 1:2]).then_inc(dflt, 16)

            def body(g, w, nxt, chain):
                first = isinstance(g, int) and g == 0
                if not first and nxt:
                    mask_load(g + 1, 1 - w)
                for m in range(6):
                    if m >= 2:
                        row_store(g, m - 2)
                    elif not first:
                        row_store(g - 1, m + 4)
                        if m == 1:
                            logit_store(g - 1)

            groups(sp, body)
            row_store(EG - 1, 4)
            row_store(EG - 1, 5)
            logit_store(EG - 1)
            for w in range(2):
                sp.wait_ge(st[w], 16 * 3 * EG)
            sp.wait_ge(st_as, 32 * EG)
            sp.wait_ge(dflt, 53)

        @block.scalar
        def _(act):
            def normalise(G, u):
                r = 4 * G + u
                act.wait_ge(ln, r + 1)
                for n in range(2):
                    act.activation(raw[:, 2 * u + n, :], raw[:, 2 * u + n, :], ACT.Identity,
                                   bias=nmr[:, u % 2, n:n + 1], scale=rstd[:, u % 2, n:n + 1]).then_inc(normed, 1)

            def high(G, W, j):
                q = 8 * G + j
                if j in (0, 1):
                    wait(act, dlog, 2 * G)
                elif j in (2, 3):
                    act.wait_ge(dlog, 2 * G + 1)
                else:
                    wait(act, h_done, 6 * G - 6)
                for h in range(2):
                    act.wait_ge(turned, 2 * q + h + 1)
                    if j < 4:
                        out = xd[:, 0, 3 * h:3 * h + 3, (j % 2) * P:(j % 2 + 1) * P]
                    else:
                        out = xt[:, W, 0, 3 * h:3 * h + 3, (j - 4) * P:(j - 3) * P]
                    act.activation(out, T[h][:, 0:3 * P].rearrange("p (k j) -> p k j", k=3), ACT.Copy).then_inc(hi_out, 1)

            def logit_copy(G):
                act.wait_ge(lg_done, G + 1)
                wait(act, sem["ab"], G)
                act.activation(b["e"][:], LG[0:HEADS, :], ACT.Copy).then_inc(sem["e_out"], 1)

            def exps(G):
                act.wait_ge(sem["x"], G + 1)
                act.activation(b["x"][:], b["x"][:], ACT.Exp).then_inc(sem["exp"], 1)

            def ab_copy(g, w):
                wait(act, agg_done, 6 * g - 6)
                act.wait_ge(ab_ex, 2 * g + 1)
                act.activation(ab[:, w, 0, :], EX[:], ACT.Copy).then_inc(ab_out, 1)
                act.wait_ge(ab_ex, 2 * g + 2)
                act.activation(ab[:, w, 1, :], LG[:], ACT.Copy).then_inc(ab_out, 1)

            def elu(g, m):
                c = 6 * g + m
                act.wait_ge(agg_done, c + 1)
                wait(act, g_done, c - 1)
                act.activation(neg_part[:, m % 2, :], agg[:, m % 2, :], ACT.Relu, bias=negb[:, m:m + 1], scale=-1.0).then_inc(neg_done, 1)
                act.wait_ge(neg_done, c + 1)
                act.activation(neg_part[:, m % 2, :], neg_part[:, m % 2, :], ACT.Exp, scale=-1.0).then_inc(elu_done, 1)

            def rows_copy(g, m):
                c = 6 * g + m
                act.wait_ge(tail_done, c + 1)
                wait(act, st[m % 2], 16 * (3 * g + m // 2))
                act.activation(rows[:, m % 2, :, :], RO[:].rearrange("p (t j) -> p t j", t=TG), ACT.Copy).then_inc(rows_out, 1)

            def logit2_copy(g):
                act.wait_ge(as_done, g + 1)
                wait(act, st_as, 32 * g)
                act.activation(logit2[:], AS[:, 0:2 * TG].rearrange("p (t n) -> p t n", n=2), ACT.Copy).then_inc(as_out, 1)

            act.activation(negb[:], s["b1col"][:], ACT.Copy, scale=-1.0)
            act.activation(bdef[:, 0, :], s["b1col"][:], ACT.Relu)
            act.wait_ge(dflt, 1)
            act.activation(bdef[:, 1, :], bdef[:, 1, :], ACT.Exp).then_inc(dflt, 1)
            act.wait_ge(dflt, 4)
            act.activation(ldef[:], AS[0:1, 0:2], ACT.Copy).then_inc(dflt, 1)
            for u in range(4):
                normalise(0, u)
                high(0, 0, 2 * u)
                high(0, 0, 2 * u + 1)
            logit_copy(0)
            normalise(1, 0)
            exps(0)
            normalise(1, 1)

            def body(g, w, nxt, chain):
                first = isinstance(g, int) and g == 0
                for m in range(6):
                    if nxt and 1 <= m <= 4:
                        high(g + 1, 1 - w, 2 * m - 1)
                    if nxt and m == 0:
                        high(g + 1, 1 - w, 0)
                    if m == 0:
                        ab_copy(g, w)
                    if not (first and m == 0):
                        elu(g if m else g - 1, (m - 1) % 6)
                    if nxt and 1 <= m < 4:
                        high(g + 1, 1 - w, 2 * m)
                    if nxt and m < 2:
                        normalise(g + 1, m + 2)
                    if nxt and m == 4:
                        logit_copy(g + 1)
                    if chain and m == 5:
                        normalise(g + 2, 1)
                    if m >= 2:
                        rows_copy(g, m - 2)
                    elif not first:
                        rows_copy(g - 1, m + 4)
                        if m == 1:
                            logit2_copy(g - 1)
                    if nxt and m == 4:
                        exps(g + 1)
                    if chain and m == 4:
                        normalise(g + 2, 0)

            groups(act, body)
            elu(EG - 1, 5)
            rows_copy(EG - 1, 4)
            rows_copy(EG - 1, 5)
            logit2_copy(EG - 1)

        @block.vector
        def _(dve):
            def moments(G, u):
                r, w = 4 * G + u, u % 2
                wait(dve, ln, r - 1)
                wait(dve, normed, 2 * r - 2)
                for n in range(2):
                    j = 2 * u + n
                    dve.wait_ge(raw_in[j], 16 * (G + 1))
                    for h in range(2):
                        last = dve.bn_stats(stats[:, w, n, h, :], raw[:, j, h * HALF:(h + 1) * HALF])
                last.then_inc(stat, 1)
                carried_wait(dve, passed_v, stat, r + 1)
                dve.bn_aggr(mv[:, w, 0, :], stats[:, w, 0, :, :])
                dve.bn_aggr(mv[:, w, 1, :], stats[:, w, 1, :, :]).then_inc(mvr, 1)

            def low(G, W, j):
                q = 8 * G + j
                for h in range(2):
                    dve.wait_ge(hi_out, 2 * q + h + 1)
                    if j < 4:
                        v = xd[:, :, 3 * h:3 * h + 3, (j % 2) * P:(j % 2 + 1) * P]
                    else:
                        v = xt[:, W, :, 3 * h:3 * h + 3, (j - 4) * P:(j - 3) * P]
                    dve.tensor_tensor(v[:, 1], T[h][:, 0:3 * P].rearrange("p (k j) -> p k j", k=3), v[:, 0].bitcast(F32),
                                      ALU.subtract).then_inc(lo_out, 1)

            def scan_chunk(g, w, m):
                c = 6 * g + m
                if m == 0:
                    dve.wait_ge(ab_out, 2 * g + 2)
                dve.wait_ge(h_done, c + 1)
                dve.tensor_tensor(msg[:, m % 2, :], H[m % 2][:], ab[:, w, 1, :], ALU.mult).then_inc(msg_done, 1)
                wait(dve, elu_done, c - 1)
                wait(dve, pos_ready, c - 1)
                dve.wait_ge(msg_done, c + 1)
                dve.tensor_tensor_scan(agg[:, m % 2, :], ab[:, w, 0, :], msg[:, m % 2, :], carry[:, m:m + 1],
                                       ALU.mult, ALU.add).then_inc(agg_done, 1)
                dve.wait_ge(agg_done, c + 1)
                dve.tensor_copy(carry[:, m:m + 1], agg[:, m % 2, GE - 1:GE]).then_inc(car, 1)
                wait(dve, g_done, c - 1)
                dve.tensor_scalar(pos_part[:, m % 2, :], agg[:, m % 2, :], bm1[:, m:m + 1], -1.0, ALU.add,
                                  ALU.max).then_inc(pos_ready, 1)

            def softmax(G, W, loaded):
                return softmax_steps(dve, b, sem, G, HEADS, mask[:, W, :, :], (mask_in[W], loaded), (ab_ex, 2 * G))

            dve.wait_ge(init, 1)
            dve.tensor_scalar(bm1[:], s["b1col"][:], -1.0, None, ALU.add)
            dve.tensor_scalar(bdef[:, 1, :], s["b1col"][:], 0.0, None, ALU.min).then_inc(dflt, 1)
            dve.wait_ge(dflt, 2)
            dve.scalar_tensor_tensor(bdef[:, 0, :], bdef[:, 1, :], -1.0, bdef[:, 0, :], ALU.add, ALU.add).then_inc(dflt, 1)
            moments(0, 0)
            for u in range(4):
                if u < 3:
                    moments(0, u + 1)
                low(0, 0, 2 * u)
                low(0, 0, 2 * u + 1)
            first_, second_ = softmax(0, 0, 16)
            moments(1, 0)
            first_()
            moments(1, 1)
            second_()

            def body(g, w, nxt, chain):
                for m in range(6):
                    if nxt and 1 <= m <= 4:
                        low(g + 1, 1 - w, 2 * m - 1)
                    if nxt and m == 0:
                        low(g + 1, 1 - w, 0)
                    if nxt and m < 2:
                        moments(g + 1, m + 2)
                    if chain and m == 4:
                        moments(g + 2, 0)
                        moments(g + 2, 1)
                    if nxt and m == 4:
                        first_, second_ = softmax(g + 1, 1 - w, 8 * g + (24 if w else 16))
                        first_()
                    if nxt and 1 <= m < 4:
                        low(g + 1, 1 - w, 2 * m)
                    scan_chunk(g, w, m)
                    if nxt and m == 4:
                        second_()

            groups(dve, body)

        @block.tensor
        def _(pe):
            def turn(G, j):
                q = 8 * G + j
                pe.wait_ge(normed, q + 1)
                for h in range(2):
                    wait(pe, lo_out, 2 * q + h - 1)
                    for kk in range(3):
                        mm = pe.transpose(T[h][:, kk * P:(kk + 1) * P],
                                          raw[:, j, (3 * h + kk) * P:(3 * h + kk + 1) * P], s["ident"][:])
                    mm.then_inc(turned, 1)

            def passes(out, lhs, rhs, start, stop, lint=False):
                for i, (x, y) in enumerate(((0, 0), (1, 0), (0, 1))):
                    mm = pe.matmul(out, lhs(x), rhs(y), start=start and i == 0, stop=stop and i == 2, skip_group_check=lint)
                return mm

            def dst_logits(G, hh):
                pe.wait_ge(lo_out, 16 * G + 4 * hh + 4)
                if hh == 0:
                    wait(pe, ab_out, 2 * G)
                for kk in range(KC):
                    mm = passes(LG[0:HEADS, hh * 2 * P:(hh + 1) * 2 * P], lambda i: s["v1"][:, 1, i, kk, :],
                                lambda i: xd[:, i, kk, :], hh == 0 and kk == 0, False, True)
                mm.then_inc(dlog, 1)

            def src_logits(G, W):
                pe.wait_ge(lo_out, 16 * G + 16)
                for kk in range(KC):
                    mm = passes(LG[0:HEADS, :], lambda i: s["v1"][:, 0, i, kk, :], lambda i: xt[:, W, i, kk, :],
                                False, kk == KC - 1, True)
                mm.then_inc(lg_done, 1)

            def spread(g):
                pe.wait_ge(sem["ab"], g + 1)
                pe.matmul(EX[:], s["headmap"][:], b["x"][:, 0, :], start=True, stop=True).then_inc(ab_ex, 1)
                pe.matmul(LG[:], s["headmap"][:], b["x"][:, 1, :], start=True, stop=True).then_inc(ab_ex, 1)

            def products(g, w, m, part):
                c = 6 * g + m
                if part == 0:
                    wait(pe, msg_done, c - 1)
                for kk in (range(0, 3), range(3, KC))[part]:
                    mm = passes(H[m % 2][:], lambda i: s["w1s"][:, i, kk, m * P:(m + 1) * P],
                                lambda i: xt[:, w, i, kk, :], kk == 0, kk == KC - 1, True)
                if part == 1:
                    mm.then_inc(h_done, 1)

            def tail(g, m):
                c = 6 * g + m
                pe.wait_ge(g_done, c + 1)
                wait(pe, rows_out, c)
                if m == 0:
                    wait(pe, as_out, g)
                for t in range(TG):
                    mm = pe.matmul(AS[:, 2 * t:2 * t + 2], g1[:, m % 2, t * P:(t + 1) * P], s["v2"][:, m, :], start=(m == 0 and t == 0),
                                   stop=(m == 5), skip_group_check=True)
                if m == 5:
                    mm.then_inc(as_done, 1)
                for t in range(TG):
                    mm = pe.transpose(RO[:, t * P:(t + 1) * P], g1[:, m % 2, t * P:(t + 1) * P], s["ident"][:])
                mm.then_inc(tail_done, 1)

            pe.wait_ge(dflt, 3)
            for m in range(KC):
                mm = pe.matmul(AS[0:1, 0:2], bdef[:, 0, m:m + 1], s["v2"][:, m, :], start=(m == 0), stop=(m == KC - 1))
            mm.then_inc(dflt, 1)
            pe.wait_ge(dflt, 5)
            for j in range(8):
                turn(0, j)
                if j in (1, 3):
                    dst_logits(0, j // 2)
            src_logits(0, 0)

            def body(g, w, nxt, chain):
                for m in range(6):
                    products(g, w, m, 0)
                    if nxt and m in (1, 2):
                        dst_logits(g + 1, m - 1)
                    if nxt and m < 4:
                        turn(g + 1, 2 * m)
                    if nxt and m == 4:
                        src_logits(g + 1, 1 - w)
                    products(g, w, m, 1)
                    if m == 0:
                        spread(g)
                    if m >= 2:
                        tail(g, m - 2)
                    elif not (isinstance(g, int) and g == 0):
                        tail(g - 1, m + 4)
                    if nxt and m < 4:
                        turn(g + 1, 2 * m + 1)

            groups(pe, body)
            tail(EG - 1, 4)
            tail(EG - 1, 5)


def gat_layer_2(nc, a, d, s):
    with ExitStack() as ctx:
        k = Kit(nc, ctx, "b_")
        xt = k.sb("xt", [P, 2, 2, KC, GE], F32R)
        raw = k.sb("raw", [P, 2, TG, RW])
        dlog = k.sb("dlog", [P, 2, TG])
        lcol = k.sb("lcol", [P, 2, TG, HEADS])
        msg = k.sb("msg", [P, 2, GE])
        agg = k.sb("agg", [P, 2, GE])
        ab = k.sb("ab", [P, 2, GE])
        carry = k.sb("carry", [P, KC])
        mask = k.sb("mask", [HEADS, 2, 2, GE])
        b, sem = softmax_kit(k, HEADS)
        sem["carry"] = lambda g: not (isinstance(g, int) and g == 0)
        stage = k.sb("stage", [P, 2, 8], I32)
        bias = k.sb("bias", [P, D])
        rows = k.sb("rows", [P, 2, D])
        w2s = k.sb("w2s", [P, 2, KC, D], F32R)
        weights = k.sb("weights", [P, KC, D])
        w1raw = weights[:, 0:FC, :].rearrange("p m n -> p (m n)").rearrange("p (k h u) -> p k h u", h=EXPERTS, u=HID)
        w2raw = weights[:, FC:2 * FC, :]
        T = [k.ps("p_t0"), k.ps("p_t1")]
        LG, EX = k.ps("p_lg"), k.ps("p_ex")
        ROW = [k.ps(f"p_row{i}") for i in range(4)]
        raw_in, st, mask_in = k.sems("s_raw", 2), k.sems("s_st", 2), k.sems("s_mask", 2)
        (passed_p, staged, init, lcol_done, lg_done, ab_ex, ab_out, turned, msg_done, agg_done, car, hi_out, lo_out, lo_p,
         unit_done, unit_out, row_out, bias_in, dflt, ffn_in, ffn_hi, ffn_lo, w2_in, w2_hi, w2_lo) = [
            k.sem("s_" + n) for n in ("passed_p", "staged", "init", "lcol", "lg", "ab_ex", "ab_out", "turned", "msg", "agg",
                                      "car", "hi", "lo", "lo_p", "unit", "unit_out", "row", "bias", "dflt", "ffn_in", "ffn_hi", "ffn_lo", "w2_in", "w2_hi", "w2_lo")]
        block = k.block()

        def groups(eng, body):
            body(0, 0, True, True)
            with eng.Fori(0, (EG - 4) // 2) as i:
                body(2 * i + 1, 1, True, True)
                body(2 * i + 2, 0, True, True)
            body(EG - 3, (EG - 3) % 2, True, True)
            body(EG - 2, EG % 2, True, False)
            body(EG - 1, (EG - 1) % 2, False, False)

        @block.gpsimd
        def _(pool):
            pool.memset(b["m"][:, 0:1], 0.0)
            pool.memset(b["z"][:, 0:1], 0.0)
            pool.memset(carry[:], 0.0).then_inc(init, 1)

            def gather(g, w):
                wait(pool, turned, 6 * g - 6)
                pool.tensor_copy(stage[:, w, :], s["pos"][:, bass.ds(8 * g, 8)]).then_inc(staged, 1)
                carried_wait(pool, passed_p, staged, g + 1)
                for j in range(TG):
                    pool.indirect_dma_start(dlog[:, w, j:j + 1], None, d["dst_logit"],
                                            bass.IndirectOffsetOnAxis(ap=stage[:, w, j:j + 1], axis=0)).then_inc(raw_in[w], 16)
                    pool.indirect_dma_start(raw[:, w, j, :], None, d["layer1"],
                                            bass.IndirectOffsetOnAxis(ap=stage[:, w, 4 + j:5 + j], axis=0)).then_inc(raw_in[w], 16)

            def add_bias(g, tiles):
                for t in tiles:
                    pool.wait_ge(unit_out, 8 * g + 2 * t + 2)
                    pool.tensor_tensor(rows[:, t % 2, :], rows[:, t % 2, :], bias[:], ALU.add).then_inc(row_out, 1)

            gather(0, 0)
            gather(1, 1)
            pool.wait_ge(w2_hi, 1)
            pool.tensor_tensor(w2s[:, 1, :, :], weights[:], w2s[:, 0, :, :].bitcast(F32), ALU.subtract).then_inc(w2_lo, 1)
            def low(G, W, kk):
                pool.wait_ge(hi_out, 6 * G + kk + 1)
                pool.tensor_tensor(xt[:, W, 1, kk, :], agg[:, kk % 2, :], xt[:, W, 0, kk, :].bitcast(F32),
                                   ALU.subtract).then_inc(lo_p, 1)

            def body(g, w, nxt, chain):
                if nxt:
                    low(g + 1, 1 - w, 0)
                    low(g + 1, 1 - w, 1)
                add_bias(g, [0])
                if nxt:
                    low(g + 1, 1 - w, 2)
                add_bias(g, [1])
                if not isinstance(g, int) or g < EG - 3:
                    gather(g + 3, 1 - w)
                add_bias(g, [2, 3])
                if isinstance(g, int) and g == EG - 2:
                    pool.wait_ge(ffn_hi, 1)
                    for kk in range(KC):
                        pool.tensor_tensor(s["f1"][:, 1, kk, :].rearrange("p (m h r) -> p m h r", h=EXPERTS, r=HR),
                                           w1raw[:, kk, :, :].rearrange("p h (m r) -> p m h r", r=HR),
                                           s["f1"][:, 0, kk, :].bitcast(F32).rearrange("p (m h r) -> p m h r", h=EXPERTS, r=HR),
                                           ALU.subtract)
                    pool.tensor_tensor(s["f2"][:, 1, :, :], w2raw, s["f2"][:, 0, :, :].bitcast(F32), ALU.subtract).then_inc(ffn_lo, 1)

            for kk in range(3):
                low(0, 0, kk)
            gather(2, 0)
            pool.wait_ge(bias_in, 16)
            groups(pool, body)

        @block.sync
        def _(sp):
            def mask_load(g, w):
                wait(sp, sem["ab"], g - 1)
                sp.dma_start(mask[:, w, :, :], d["masks"][:, bass.ds(g * GE, GE)].partition_broadcast(HEADS)).then_inc(mask_in[w], 16)

            mask_load(0, 0)
            for h in range(HEADS):
                sp.dma_start(weights[h * HR:(h + 1) * HR, :, :],
                             a["L0_gnn_W2"][h * HC:(h + 1) * HC, :].rearrange("(m r) n -> r m n", r=HR)).then_inc(w2_in, 16)
            mask_load(1, 1)
            sp.dma_start(bias[:], a["L0_gnn_b2"].partition_broadcast(P)).then_inc(bias_in, 16)
            sp.dma_start(d["layer2"][EP, :], a["L0_gnn_b2"]).then_inc(dflt, 16)
            sp.wait_ge(w2_lo, 1)
            for h in range(EXPERTS):
                sp.dma_start(w1raw[:, :, h, :], a["L0_ffn_w1"][h].rearrange("(k p) u -> p k u", p=P)).then_inc(ffn_in, 16)
                sp.dma_start(w2raw[h * HR:(h + 1) * HR, :, :],
                             a["L0_ffn_w2"][h].rearrange("(m r) n -> r m n", r=HR)).then_inc(ffn_in, 16)

            def body(g, w, nxt, chain):
                if chain:
                    mask_load(g + 2, w)
                for t in range(TG):
                    sp.wait_ge(row_out, 4 * g + t + 1)
                    sp.dma_start(d["layer2"][bass.ds(g * GE + t * P, P), :], rows[:, t % 2, :]).then_inc(st[t % 2], 16)

            groups(sp, body)
            for w in range(2):
                sp.wait_ge(st[w], 16 * 2 * EG)
            sp.wait_ge(dflt, 16)

        @block.scalar
        def _(act):
            def logit_copy(G):
                act.wait_ge(lg_done, G + 1)
                wait(act, sem["ab"], G)
                act.activation(b["e"][:], LG[0:HEADS, :], ACT.Copy).then_inc(sem["e_out"], 1)

            def exps(G):
                act.wait_ge(sem["x"], G + 1)
                act.activation(b["x"][:], b["x"][:], ACT.Exp).then_inc(sem["exp"], 1)

            def ab_copy(G):
                wait(act, agg_done, 6 * G)
                act.wait_ge(ab_ex, 2 * G + 2)
                act.activation(ab[:, 0, :], EX[:], ACT.Copy)
                act.activation(ab[:, 1, :], LG[:], ACT.Copy).then_inc(ab_out, 1)

            def unit_copy(g, u):
                t, h = u // 2, u % 2
                act.wait_ge(unit_done, 8 * g + u + 1)
                if h == 0:
                    wait(act, st[t % 2], 16 * (2 * g + t // 2))
                act.activation(rows[:, t % 2, h * HALF:(h + 1) * HALF], ROW[u % 4][:, 0:HALF], ACT.Copy).then_inc(unit_out, 1)

            def high(G, W, kk):
                act.wait_ge(agg_done, 6 * G + kk + 1)
                wait(act, unit_done, 8 * G - 8)
                act.activation(xt[:, W, 0, kk, :], agg[:, kk % 2, :], ACT.Copy).then_inc(hi_out, 1)

            act.wait_ge(w2_in, 16 * HEADS)
            act.activation(w2s[:, 0, :, :], weights[:], ACT.Copy).then_inc(w2_hi, 1)
            logit_copy(0)
            exps(0)
            ab_copy(0)
            for kk in range(KC):
                high(0, 0, kk)
                if kk == 1:
                    logit_copy(1)
                if kk == 2:
                    exps(1)
            ab_copy(1)

            def body(g, w, nxt, chain):
                for u in range(8):
                    if u >= 1:
                        unit_copy(g, u - 1)
                    if nxt and u < KC:
                        high(g + 1, 1 - w, u)
                    if chain and u == 2:
                        logit_copy(g + 2)
                    if chain and u == 3:
                        exps(g + 2)
                unit_copy(g, 7)
                if chain:
                    ab_copy(g + 2)
                if isinstance(g, int) and g == 0:
                    act.wait_ge(ffn_in, 16 * 2 * EXPERTS)
                    for kk in range(KC):
                        act.activation(s["f1"][:, 0, kk, :].rearrange("p (m h r) -> p m h r", h=EXPERTS, r=HR),
                                       w1raw[:, kk, :, :].rearrange("p h (m r) -> p m h r", r=HR), ACT.Copy)
                    act.activation(s["f2"][:, 0, :, :], w2raw, ACT.Copy).then_inc(ffn_hi, 1)

            groups(act, body)

        @block.vector
        def _(dve):
            def logit_columns(G, W):
                dve.wait_ge(raw_in[W], 64 * (G - W) + 128)
                wait(dve, lg_done, G - 1)
                dve.tensor_tensor(lcol[:, W, :, :], raw[:, W, :, D:D + 1].broadcast_to([P, TG, HEADS]),
                                  dlog[:, W, :].unsqueeze(2).broadcast_to([P, TG, HEADS]), ALU.add).then_inc(lcol_done, 1)

            def scan_chunk(G, kk):
                c = 6 * G + kk
                if kk == 0:
                    dve.wait_ge(ab_out, G + 1)
                dve.wait_ge(turned, c + 1)
                dve.tensor_tensor(msg[:, kk % 2, :], T[kk % 2][:], ab[:, 1, :], ALU.mult).then_inc(msg_done, 1)
                wait(dve, hi_out, c - 1)
                if kk in (0, 1, 5):
                    wait(dve, lo_out, 3 * G + (kk - 1 if kk < 3 else 1))
                else:
                    dve.wait_ge(lo_p, 3 * G + kk - 1)
                dve.wait_ge(msg_done, c + 1)
                dve.tensor_tensor_scan(agg[:, kk % 2, :], ab[:, 0, :], msg[:, kk % 2, :], carry[:, kk:kk + 1],
                                       ALU.mult, ALU.add).then_inc(agg_done, 1)
                dve.wait_ge(agg_done, c + 1)
                dve.tensor_copy(carry[:, kk:kk + 1], agg[:, kk % 2, GE - 1:GE]).then_inc(car, 1)

            def low(G, W, kk):
                if kk < 3:
                    return
                dve.wait_ge(hi_out, 6 * G + kk + 1)
                dve.tensor_tensor(xt[:, W, 1, kk, :], agg[:, kk % 2, :], xt[:, W, 0, kk, :].bitcast(F32),
                                  ALU.subtract).then_inc(lo_out, 1)

            def softmax(G, W):
                return softmax_steps(dve, b, sem, G, HEADS, mask[:, W, :, :], (mask_in[W], 8 * (G - W) + 16), (ab_ex, 2 * G))

            dve.wait_ge(init, 1)
            logit_columns(0, 0)
            first_, second_ = softmax(0, 0)
            first_()
            second_()
            logit_columns(1, 1)
            first_, second_ = softmax(1, 1)
            for kk in range(KC):
                scan_chunk(0, kk)
                low(0, 0, kk)
                if kk == 1:
                    first_()
            second_()

            def body(g, w, nxt, chain):
                for u in range(8):
                    if nxt and 1 <= u <= KC:
                        low(g + 1, 1 - w, u - 1)
                    if nxt and u < KC:
                        scan_chunk(g + 1, u)
                    if chain:
                        if u == 0:
                            logit_columns(g + 2, w)
                        if u == 2:
                            first_, second_ = softmax(g + 2, w)
                            first_()
                        if u == 4:
                            second_()

            groups(dve, body)

        @block.tensor
        def _(pe):
            def logits(G, W):
                pe.wait_ge(lcol_done, G + 1)
                wait(pe, ab_out, G)
                for t in range(TG):
                    mm = pe.transpose(LG[0:HEADS, t * P:(t + 1) * P], lcol[:, W, t, :], s["ident"][:])
                mm.then_inc(lg_done, 1)

            def spread(G):
                pe.wait_ge(sem["ab"], G + 1)
                pe.matmul(EX[:], s["headmap"][:], b["x"][:, 0, :], start=True, stop=True).then_inc(ab_ex, 1)
                pe.matmul(LG[:], s["headmap"][:], b["x"][:, 1, :], start=True, stop=True).then_inc(ab_ex, 1)

            def turn(G, W, kk):
                wait(pe, msg_done, 6 * G + kk - 1)
                for t in range(TG):
                    mm = pe.transpose(T[kk % 2][:, t * P:(t + 1) * P], raw[:, W, t, kk * P:(kk + 1) * P], s["ident"][:])
                mm.then_inc(turned, 1)

            def unit(g, w, u):
                t, h = u // 2, u % 2
                if u == 0:
                    pe.wait_ge(lo_out, 3 * g + 3)
                    pe.wait_ge(lo_p, 3 * g + 3)
                    if isinstance(g, int) and g == 0:
                        pe.wait_ge(w2_lo, 1)
                wait(pe, unit_out, 8 * g + u - 3)
                for kk in range(KC):
                    for i, (x, y) in enumerate(((0, 0), (1, 0), (0, 1))):
                        mm = pe.matmul(ROW[u % 4][:, 0:HALF], xt[:, w, x, kk, t * P:(t + 1) * P],
                                       w2s[:, y, kk, h * HALF:(h + 1) * HALF], start=kk == 0 and i == 0,
                                       stop=kk == KC - 1 and i == 2)
                mm.then_inc(unit_done, 1)

            logits(0, 0)
            spread(0)
            for kk in range(KC):
                turn(0, 0, kk)
                if kk == 0:
                    logits(1, 1)

            def body(g, w, nxt, chain):
                if nxt:
                    turn(g + 1, 1 - w, 0)
                for u in range(8):
                    unit(g, w, u)
                    if isinstance(g, int) and g == 0 and u == 0:
                        spread(1)
                    if nxt and u < KC - 1:
                        turn(g + 1, 1 - w, u + 1)
                    if chain and u == 1:
                        logits(g + 2, w)
                if chain:
                    spread(g + 2)

            groups(pe, body)


def moe_ffn(nc, a, d, s, out):
    with ExitStack() as ctx:
        k = Kit(nc, ctx, "f_")
        xt = k.sb("xt", [P, 2, 2, KC, GE], F32R)
        x1 = k.sb("x1", [P, 2, TG, D])
        raw = k.sb("raw", [P, TG, D])
        res = k.sb("res", [P, TG, D])
        hid = k.sb("hid", [P, FC, GE])
        hs = k.sb("hs", [P, 2, FC, GE], F32R)
        stage = k.sb("stage", [P, 2, TG], I32)
        stats = k.sb("stats", [P, 2, 2, 2, 6])
        mv = k.sb("mv", [P, 2, 2, 2])
        rstd = k.sb("rstd", [P, 2, 2])
        nmr = k.sb("nmr", [P, 2, 2])
        ln_const = k.sb("ln_const", [P, 6])
        b1 = k.sb("b1", [P, FC])
        graw = k.sb("graw", [P, KC, EXPERTS])
        gate = k.sb("gate", [P, KC, 2, EXPERTS], F32R)
        sel = k.sb("sel", [2 * EXPERTS, EXPERTS])
        b2raw = k.sb("b2raw", [96, D])
        b2s = k.sb("b2s", [96, D], F32R)
        spread_f = k.sb("spread_f", [96, P])
        spread_w = k.sb("spread_w", [96, P], F32R)
        cpad = k.sb("cpad", [P, TG, 96])
        ct = k.sb("ct", [96, GE], F32R)
        lg16 = k.sb("lg16", [2 * EXPERTS, GE])
        lg = k.sb("lg", [P, TG, EXPERTS])
        top = k.sb("top", [P, TG, 8])
        top_i = k.sb("top_i", [P, TG, 8], mybir.dt.uint32)
        top_f = k.sb("top_f", [P, TG, 2])
        iota_i = k.sb("iota_i", [P, EXPERTS], I32)
        iota_f = k.sb("iota_f", [P, EXPERTS])
        gap = k.sb("gap", [P, TG])
        wgt = k.sb("wgt", [P, 2, TG])
        onehot = k.sb("onehot", [P, 2, TG, EXPERTS])
        comb = k.sb("comb", [P, TG, EXPERTS])
        comb_hi = k.sb("comb_hi", [P, TG, EXPERTS], F32R)
        T = [k.ps("p_t0"), k.ps("p_t1")]
        H = [k.ps("p_h0"), k.ps("p_h1")]
        R = k.ps("p_r")
        ROW = [k.ps(f"p_row{i}") for i in range(3)]
        raw_in, st = k.sems("s_raw", TG), k.sems("s_st", TG)
        x_in = [k.sems(f"s_x{w}_", TG) for w in range(2)]
        (passed_p, passed_v, staged, init, added, stat, mvr, vv, pw, ln, normed, turned, hi_out, lo_out, router_done, lg16_out,
         sums_done, dv, gap_done, tanh_done, comb_done, ct_done, ct_out, ce_done, h_done, gelu_done, scaled, hhi, hlo,
         unit_done, row_out, small_in, consts) = [
            k.sem("s_" + n) for n in ("passed_p", "passed_v", "staged", "init", "added", "stat", "mvr", "vv", "pw", "ln", "normed", "turned",
                                      "hi", "lo", "router", "lg16", "sums", "dv", "gap", "tanh", "comb", "ct", "ct_out",
                                      "ce", "h", "gelu", "scaled", "hhi", "hlo", "unit", "row", "small", "consts")]
        block = k.block()

        def groups(eng, body):
            body(0, 0, True, False)
            with eng.Fori(0, (NG - 4) // 2) as i:
                body(2 * i + 1, 1, False, False)
                body(2 * i + 2, 0, False, False)
            for g in range(NG - 3, NG):
                body(g, g % 2, False, g == NG - 1)

        def rows_of(g, t):
            if isinstance(g, int) and g == NG - 1:
                return bass.ds(N - GE + t * P, P)
            return bass.ds(g * GE + t * P, P)

        @block.sync
        def _(sp):
            def load(G, W, t):
                sp.dma_start(x1[:, W, t, :], a["x"][rows_of(G, t), :]).then_inc(x_in[W][t], 16)

            for t in range(TG):
                load(0, 0, t)
            sp.wait_ge(consts, 1)
            sp.dma_start(graw[:], a["L0_ffn_gate_w"].rearrange("(k p) e -> p k e", p=P)).then_inc(small_in, 16)
            for h in range(EXPERTS):
                sp.dma_start(b1[h * HR:(h + 1) * HR, :], a["L0_ffn_b1"][h, 0, :].rearrange("(m r) -> r m", r=HR),
                             allow_slow_non_contiguous=True).then_inc(small_in, 16)
            for n in range(3):
                sp.dma_start(b2raw[32 * n:32 * n + EXPERTS, :], a["L0_ffn_b2"][:, 0, :]).then_inc(small_in, 16)
            for n in (0, 2):
                sp.dma_start(spread_f[32 * n:32 * n + EXPERTS, :], s["headmap"][:]).then_inc(small_in, 16)
            for t in range(TG):
                load(1, 1, t)

            def body(g, w, more):
                if isinstance(g, int) and g == NG - 1:
                    for t in range(TG):
                        sp.wait_ge(st[t], 16 * (NG - 1))
                for t in range(TG):
                    sp.wait_ge(row_out, 8 * g + 2 * t + 2)
                    if more:
                        load(g + 2, w, t)
                    sp.dma_start(out[rows_of(g, t), :], res[:, t, :]).then_inc(st[t], 16)

            with sp.Fori(0, (NG - 4) // 2) as i:
                body(2 * i, 0, True)
                body(2 * i + 1, 1, True)
            for g in range(NG - 4, NG):
                body(g, g % 2, g + 2 < NG)
            for t in range(TG):
                sp.wait_ge(st[t], 16 * NG)

        @block.gpsimd
        def _(pool):
            pool.memset(b2raw[:], 0.0)
            pool.memset(spread_f[:], 0.0)
            for n, v in enumerate((-0.5, EPS, -1.0)):
                pool.memset(ln_const[:, 2 * n:2 * n + 2], v)
            pool.memset(cpad[:], 0.0)
            pool.iota(iota_i[:], [[1, EXPERTS]], base=0, channel_multiplier=0)
            pool.memset(sel[:], 0.0).then_inc(consts, 1)
            pool.wait_ge(consts, 1)
            pool.affine_select(out=sel[:], in_=sel[:], compare_op=ALU.not_equal, fill=1.0, base=0,
                               pattern=[[-1, EXPERTS]], channel_multiplier=1).then_inc(init, 1)
            pool.wait_ge(init, 1)
            pool.affine_select(out=sel[:], in_=sel[:], compare_op=ALU.not_equal, fill=1.0, base=-EXPERTS,
                               pattern=[[-1, EXPERTS]], channel_multiplier=1).then_inc(init, 1)

            def group(G, W):
                wait(pool, ln, 2 * G)
                pool.tensor_copy(stage[:, W, :], s["pnode"][:, bass.ds(TG * G, TG)]).then_inc(staged, 1)

                def gather(tiles):
                    for t in tiles:
                        wait(pool, turned, 8 * G - 8 + 2 * t + 2)
                        carried_wait(pool, passed_p, staged, G + 1)
                        pool.indirect_dma_start(raw[:, t, :], None, d["layer2"],
                                                bass.IndirectOffsetOnAxis(ap=stage[:, W, t:t + 1], axis=0)).then_inc(raw_in[t], 16)

                start = isinstance(G, int) and G == 0
                gather(range(TG))
                for u in range(2):
                    r = 2 * G + u
                    for t in (2 * u, 2 * u + 1):
                        if start:
                            continue
                        pool.wait_ge(raw_in[t], 16 * G + 16)
                        pool.wait_ge(x_in[W][t], 8 * (G - W) + 16)
                        pool.tensor_tensor(x1[:, W, t, :], x1[:, W, t, :], raw[:, t, :], ALU.add).then_inc(added, 1)
                    pool.wait_ge(mvr, r + 1)
                    pool.tensor_tensor(rstd[:, u, :], mv[:, u, :, 1], ln_const[:, 2:4], ALU.add)
                    pool.tensor_tensor(nmr[:, u, :], mv[:, u, :, 0], ln_const[:, 4:6], ALU.mult).then_inc(vv, 1)
                    pool.wait_ge(vv, r + 1)
                    pool.tensor_tensor(rstd[:, u, :], rstd[:, u, :], ln_const[:, 0:2], ALU.pow).then_inc(pw, 1)
                    pool.wait_ge(pw, r + 1)
                    pool.tensor_tensor(nmr[:, u, :], nmr[:, u, :], rstd[:, u, :], ALU.mult).then_inc(ln, 1)

            group(0, 0)
            group(1, 1)
            with pool.Fori(1, NG // 2) as i:
                group(2 * i, 0)
                group(2 * i + 1, 1)

        @block.scalar
        def _(act):
            def normalise(G, W, t):
                act.wait_ge(ln, 2 * G + t // 2 + 1)
                act.activation(raw[:, t, :], x1[:, W, t, :], ACT.Identity, bias=nmr[:, t // 2, t % 2:t % 2 + 1],
                               scale=rstd[:, t // 2, t % 2:t % 2 + 1]).then_inc(normed, 1)

            def high(G, W, h):
                act.wait_ge(turned, 8 * G + h + 1)
                wait(act, h_done, 3 * G - 3)
                act.activation(xt[:, W, 0, 3 * (h % 2):3 * (h % 2) + 3, (h // 2) * P:(h // 2 + 1) * P],
                               T[h % 2][:, 0:3 * P].rearrange("p (k j) -> p k j", k=3), ACT.Copy).then_inc(hi_out, 1)

            def router_copy(G):
                act.wait_ge(router_done, G + 1)
                act.activation(lg16[:], R[0:2 * EXPERTS, :], ACT.Copy).then_inc(lg16_out, 1)

            def tanh(g):
                act.wait_ge(gap_done, g + 1)
                act.activation(gap[:], gap[:], ACT.Tanh, scale=0.5).then_inc(tanh_done, 1)

            def weights_copy(g):
                act.wait_ge(ct_done, g + 1)
                wait(act, unit_done, 8 * g)
                act.activation(ct[:], R[0:96, :], ACT.Copy).then_inc(ct_out, 1)

            def gelu(g, w, m):
                c = 3 * g + m
                act.wait_ge(h_done, c + 1)
                wait(act, hlo, 3 * g)
                act.activation(hid[:, m, :], H[(w + m) % 2][:], ACT.Gelu, bias=b1[:, m:m + 1]).then_inc(gelu_done, 1)

            def hidden_high(g, m):
                act.wait_ge(scaled, 3 * g + m + 1)
                wait(act, unit_done, 8 * g)
                act.activation(hs[:, 0, m, :], hid[:, m, :], ACT.Copy).then_inc(hhi, 1)

            for t in range(TG):
                normalise(0, 0, t)
                high(0, 0, 2 * t)
                high(0, 0, 2 * t + 1)
                if t == 1:
                    act.wait_ge(small_in, 16 * 14)
                    act.activation(gate[:, :, 0, :], graw[:], ACT.Copy)
                    act.activation(b2s[:], b2raw[:], ACT.Copy)
                    act.activation(spread_w[:], spread_f[:], ACT.Copy).then_inc(consts, 1)

            def body(g, w, first, last):
                router_copy(g)
                tanh(g)
                if not last:
                    normalise(g + 1, 1 - w, 0)
                gelu(g, w, 0)
                weights_copy(g)
                if not last:
                    normalise(g + 1, 1 - w, 1)
                gelu(g, w, 1)
                hidden_high(g, 0)
                if not last:
                    high(g + 1, 1 - w, 0)
                hidden_high(g, 1)
                gelu(g, w, 2)
                if not last:
                    high(g + 1, 1 - w, 1)
                hidden_high(g, 2)
                if not last:
                    high(g + 1, 1 - w, 2)
                    for t in (2, 3):
                        normalise(g + 1, 1 - w, t)
                    for h in range(3, 8):
                        high(g + 1, 1 - w, h)

            groups(act, body)

        @block.vector
        def _(dve):
            def moments(G, W, u):
                r = 2 * G + u
                wait(dve, normed, 4 * G - 4 + 2 * u + 2)
                for n in range(2):
                    t = 2 * u + n
                    if isinstance(G, int) and G == 0:
                        dve.wait_ge(raw_in[t], 16)
                        dve.wait_ge(x_in[W][t], 16)
                        dve.tensor_tensor(x1[:, W, t, :], x1[:, W, t, :], raw[:, t, :], ALU.add).then_inc(added, 1)
                    dve.wait_ge(added, 4 * G + t + 1)
                    for h in range(2):
                        ins = dve.bn_stats(stats[:, u, n, h, :], x1[:, W, t, h * HALF:(h + 1) * HALF])
                ins.then_inc(stat, 1)
                carried_wait(dve, passed_v, stat, r + 1)
                dve.bn_aggr(mv[:, u, 0, :], stats[:, u, 0, :, :])
                dve.bn_aggr(mv[:, u, 1, :], stats[:, u, 1, :, :]).then_inc(mvr, 1)

            def low(G, W, h):
                dve.wait_ge(hi_out, 8 * G + h + 1)
                v = xt[:, W, :, 3 * (h % 2):3 * (h % 2) + 3, (h // 2) * P:(h // 2 + 1) * P]
                dve.tensor_tensor(v[:, 1], T[h % 2][:, 0:3 * P].rearrange("p (k j) -> p k j", k=3), v[:, 0].bitcast(F32),
                                  ALU.subtract).then_inc(lo_out, 1)

            DV = 8

            def best_two(g):
                n = [DV * g]

                def step(ins):
                    n[0] = n[0] + 1
                    ins.then_inc(dv, 1)
                    dve.wait_ge(dv, n[0])

                dve.wait_ge(sums_done, g + 1)
                step(dve.tensor_copy(lg[:], R[:, 0:TG * EXPERTS].rearrange("p (t e) -> p t e", e=EXPERTS)))
                dve.sem_inc(passed_v, 1)
                for t in range(TG):
                    ins = dve.max(top[:, t, :], lg[:, t, :])
                step(ins)
                dve.tensor_tensor(gap[:], top[:, :, 0], top[:, :, 1], ALU.subtract).then_inc(gap_done, 1)
                for t in range(TG):
                    ins = dve.max_index(top_i[:, t, :], top[:, t, :], lg[:, t, :])
                step(ins)
                step(dve.tensor_copy(top_f[:], top_i[:, :, 0:2]))
                for j in range(2):
                    ins = dve.tensor_tensor(onehot[:, j, :, :], iota_f[:].unsqueeze(1).broadcast_to([P, TG, EXPERTS]),
                                            top_f[:, :, j:j + 1].broadcast_to([P, TG, EXPERTS]), ALU.is_equal)
                step(ins)

            def combine(g):
                n = [DV * g + 5]

                def step(ins):
                    n[0] = n[0] + 1
                    ins.then_inc(dv, 1)
                    dve.wait_ge(dv, n[0])

                dve.wait_ge(tanh_done, g + 1)
                dve.tensor_scalar(wgt[:, 0, :], gap[:], 0.5, 0.5, ALU.mult, ALU.add)
                step(dve.tensor_scalar(wgt[:, 1, :], gap[:], -0.5, 0.5, ALU.mult, ALU.add))
                step(dve.tensor_tensor(onehot[:], onehot[:], wgt[:].unsqueeze(3).broadcast_to([P, 2, TG, EXPERTS]), ALU.mult))
                step(dve.tensor_tensor(comb[:], onehot[:, 0], onehot[:, 1], ALU.add))
                dve.tensor_copy(comb_hi[:], comb[:]).then_inc(comb_done, 1)
                dve.wait_ge(comb_done, 3 * g + 1)
                dve.tensor_copy(cpad[:, :, 0:2 * 32].rearrange("p t (n e) -> p t n e", n=2)[:, :, :, 0:EXPERTS],
                                comb_hi[:].bitcast(F32).unsqueeze(2).broadcast_to([P, TG, 2, EXPERTS])).then_inc(comb_done, 1)
                dve.tensor_tensor(cpad[:, :, 64:64 + EXPERTS], comb[:], comb_hi[:].bitcast(F32), ALU.subtract).then_inc(comb_done, 1)

            def scale(g, m):
                dve.wait_ge(ce_done, g + 1)
                dve.wait_ge(gelu_done, 3 * g + m + 1)
                dve.tensor_tensor(hid[:, m, :], hid[:, m, :], R[:], ALU.mult).then_inc(scaled, 1)

            def hidden_low(g, m):
                dve.wait_ge(hhi, 3 * g + m + 1)
                dve.tensor_tensor(hs[:, 1, m, :], hid[:, m, :], hs[:, 0, m, :].bitcast(F32), ALU.subtract).then_inc(hlo, 1)

            def residual(g, w, u):
                t, h = u // 2, u % 2
                dve.wait_ge(unit_done, 8 * g + u + 1)
                if h == 0:
                    wait(dve, st[t], 16 * g)
                cols = slice(h * HALF, (h + 1) * HALF)
                dve.tensor_tensor(res[:, t, cols], ROW[u % 3][:, 0:HALF], x1[:, w, t, cols], ALU.add).then_inc(row_out, 1)

            for u in range(2):
                moments(0, 0, u)
            for h in range(8):
                low(0, 0, h)
                if h == 3:
                    dve.wait_ge(consts, 2)
                    dve.tensor_tensor(gate[:, :, 1, :], graw[:], gate[:, :, 0, :].bitcast(F32), ALU.subtract)
                    dve.tensor_copy(iota_f[:], iota_i[:])
                    dve.tensor_tensor(b2s[32:32 + EXPERTS, :], b2raw[32:32 + EXPERTS, :], b2s[32:32 + EXPERTS, :].bitcast(F32),
                                      ALU.subtract).then_inc(consts, 1)
                    dve.wait_ge(consts, 3)
            moments(1, 1, 0)

            def body(g, w, first, last):
                best_two(g)
                combine(g)
                if not last:
                    moments(g + 1, 1 - w, 1)
                scale(g, 0)
                scale(g, 1)
                hidden_low(g, 0)
                if not last:
                    low(g + 1, 1 - w, 0)
                hidden_low(g, 1)
                scale(g, 2)
                if not last:
                    low(g + 1, 1 - w, 1)
                hidden_low(g, 2)
                if not last:
                    low(g + 1, 1 - w, 2)
                for u in range(8):
                    if not last and u < 5:
                        low(g + 1, 1 - w, 3 + u)
                    residual(g, w, u)
                if not (last or isinstance(g, int) and g == NG - 2):
                    moments(g + 2, w, 0)

            groups(dve, body)

        @block.tensor
        def _(pe):
            def turn(G, h):
                t = h // 2
                pe.wait_ge(normed, 4 * G + t + 1)
                wait(pe, lo_out, 8 * G + h - 1)
                for kk in range(3):
                    mm = pe.transpose(T[h % 2][:, kk * P:(kk + 1) * P],
                                      raw[:, t, (3 * (h % 2) + kk) * P:(3 * (h % 2) + kk + 1) * P], s["ident"][:])
                mm.then_inc(turned, 1)

            def router(G, W):
                pe.wait_ge(lo_out, 8 * G + 8)
                wait(pe, scaled, 3 * G)
                for kk in range(KC):
                    pe.matmul(R[0:2 * EXPERTS, :], gate[:, kk, :, :].rearrange("p n e -> p (n e)"), xt[:, W, 0, kk, :],
                              start=kk == 0, stop=False, skip_group_check=True)
                    mm = pe.matmul(R[0:EXPERTS, :], gate[:, kk, 0, :], xt[:, W, 1, kk, :], start=False,
                                   stop=kk == KC - 1, skip_group_check=True)
                mm.then_inc(router_done, 1)

            def sums(g):
                pe.wait_ge(lg16_out, g + 1)
                for t in range(TG):
                    mm = pe.matmul(R[:, t * EXPERTS:(t + 1) * EXPERTS], lg16[:, t * P:(t + 1) * P], sel[:],
                                   start=True, stop=True, skip_group_check=True)
                mm.then_inc(sums_done, 1)

            def weights_turn(g):
                pe.wait_ge(comb_done, 3 * g + 3)
                for t in range(TG):
                    mm = pe.transpose(R[0:96, t * P:(t + 1) * P], cpad[:, t, :], s["ident"][:])
                mm.then_inc(ct_done, 1)

            def weights_spread(g):
                pe.wait_ge(ct_out, g + 1)
                pe.matmul(R[:], spread_w[:], ct[:], start=True, stop=True).then_inc(ce_done, 1)

            def hidden(g, w, m, part):
                if part == 0:
                    wait(pe, gelu_done, 3 * g + m - 1)
                for kk in (range(0, 3), range(3, KC))[part]:
                    for i, (x, y) in enumerate(((0, 0), (1, 0), (0, 1))):
                        mm = pe.matmul(H[(w + m) % 2][:], s["f1"][:, x, kk, m * P:(m + 1) * P], xt[:, w, y, kk, :],
                                       start=kk == 0 and i == 0, stop=kk == KC - 1 and i == 2, skip_group_check=True)
                if part == 1:
                    mm.then_inc(h_done, 1)

            def unit(g, u, chunks):
                t, h = u // 2, u % 2
                cols = slice(h * HALF, (h + 1) * HALF)
                if 0 in chunks:
                    wait(pe, row_out, 8 * g + (u - 2 if u >= 3 else (-1, 0, 0)[u]))
                    pe.matmul(ROW[u % 3][:, 0:HALF], ct[:, t * P:(t + 1) * P], b2s[:, cols], start=True, stop=False,
                              skip_group_check=True)
                for m in chunks:
                    if u == 0:
                        pe.wait_ge(hlo, 3 * g + m + 1)
                    for i, (x, y) in enumerate(((0, 0), (1, 0), (0, 1))):
                        mm = pe.matmul(ROW[u % 3][:, 0:HALF], hs[:, x, m, t * P:(t + 1) * P], s["f2"][:, y, m, cols],
                                       start=False, stop=m == FC - 1 and i == 2, skip_group_check=True)
                if FC - 1 in chunks:
                    mm.then_inc(unit_done, 1)

            for h in range(8):
                turn(0, h)
            pe.wait_ge(consts, 3)
            pe.wait_ge(init, 2)
            router(0, 0)

            def body(g, w, first, last):
                hidden(g, w, 0, 0)
                sums(g)
                hidden(g, w, 0, 1)
                hidden(g, w, 1, 0)
                weights_turn(g)
                hidden(g, w, 1, 1)
                weights_spread(g)
                hidden(g, w, 2, 0)
                if not last:
                    turn(g + 1, 0)
                hidden(g, w, 2, 1)
                if not last:
                    turn(g + 1, 1)
                    turn(g + 1, 2)
                for u in range(3):
                    unit(g, u, range(0, FC - 1))
                for u in range(8):
                    unit(g, u, range(FC - 1, FC) if u < 3 else range(FC))
                    if not last and u < 5:
                        turn(g + 1, 3 + u)
                if not last:
                    router(g + 1, 1 - w)

            groups(pe, body)


def build(nc, *arrays):
    names = _INS
    a = dict(zip(names, arrays))
    out = arrays[len(names)]
    d = {
        "sorted_dst": nc.dram_tensor("sorted_dst", (EP + 2, 1), F32, kind="Internal").ap(),
        "masks": nc.dram_tensor("edge_masks", (2, EP), F32, kind="Internal").ap(),
        "node_pos": nc.dram_tensor("node_pos", (HB * P, 1), I32, kind="Internal").ap(),
        "layer1": nc.dram_tensor("layer1", (EP + 1, RW), F32, kind="Internal").ap(),
        "dst_logit": nc.dram_tensor("dst_logit", (EP + 1, 1), F32, kind="Internal").ap(),
        "layer2": nc.dram_tensor("layer2", (EP + 1, D), F32, kind="Internal").ap(),
    }
    with ExitStack() as ctx:
        s = persistent(Kit(nc, ctx))
        order_edges(nc, a, d, s)
        gat_layer_1(nc, a, d, s)
        experts_weights(s)
        gat_layer_2(nc, a, d, s)
        moe_ffn(nc, a, d, s, out)


_INS = ["x", "src", "dst", "L0_gnn_W1", "L0_gnn_a_src1", "L0_gnn_a_dst1", "L0_gnn_b1", "L0_gnn_W2", "L0_gnn_a_src2",
        "L0_gnn_a_dst2", "L0_gnn_b2", "L0_ffn_gate_w", "L0_ffn_w1", "L0_ffn_b1", "L0_ffn_w2", "L0_ffn_b2"]
_OUTS = [((N, D), "float32")]


def kernel(**inputs):
    import numpy as _np
    import concourse.bacc as _bacc
    from concourse import mybir as _mybir
    from concourse.bass_utils import run_bass_kernel_spmd as _run

    nc = _bacc.Bacc("TRN2", target_bir_lowering=False, num_devices=1)
    arrays, args = {}, []
    for name in _INS:
        arr = _np.ascontiguousarray(inputs[name])
        arrays[f"in_{name}_dram"] = arr
        args.append(nc.dram_tensor(f"in_{name}_dram", arr.shape, _mybir.dt.from_np(arr.dtype), kind="ExternalInput").ap())
    for i, (shape, dtype) in enumerate(_OUTS):
        dt = _mybir.dt.from_np(_np.dtype(dtype))
        args.append(nc.dram_tensor(f"out_{i}_dram", shape, dt, kind="ExternalOutput").ap())
    build(nc, *args)
    r = _run(nc, [arrays], core_ids=[0])
    return r.results[0]["out_0_dram"]
```
